# Optimizing a Trainium2 kernel written in Bass

```python
import numpy as np
import jax
import jax.numpy as jnp

def _softmax(x, axis=-1):
    return jax.nn.softmax(x, axis=axis)

def _gelu(x):
    return jax.nn.gelu(x, approximate=True)

def _silu(x):
    return jax.nn.silu(x)

def _sigmoid(x):
    return jax.nn.sigmoid(x)

def _layernorm(x, axis=-1, eps=1e-05):
    m = jnp.mean(x, axis=axis, keepdims=True)
    v = jnp.var(x, axis=axis, keepdims=True)
    return (x - m) / jnp.sqrt(v + eps)

def _scatter_add(tgt, idx, src, axis=0):
    return tgt.at[idx].add(src)

def _segment_sum(src, seg, n):
    return jax.ops.segment_sum(src, seg, n)
kernel_name = 'mk_flamingo_gated_d4_seqx_r8_a21043'

def setup_inputs(seed: int=0):
    np.random.seed(seed)
    _w = jnp.asarray

    def _rec_inputs():
        import jax
        import jax.numpy as jnp
        _rk = jax.random.key(seed)
        x = 0.000341 + 1 * jax.random.normal(jax.random.fold_in(_rk, 1), (8, 128, 256), jnp.float32)
        _lenS = 128 - jax.random.randint(jax.random.fold_in(_rk, 7), (8,), 0, max(1, 128 // 4) + 1, jnp.int32)
        _lenS2 = 128 - jax.random.randint(jax.random.fold_in(_rk, 8), (8,), 0, max(1, 128 // 4) + 1, jnp.int32)
        _ctx_2048P = jax.random.normal(jax.random.fold_in(_rk, 11), (8, 16, 256), jnp.float32)
        _ctx_2048c = jax.random.dirichlet(jax.random.fold_in(_rk, 511), 0.3 * jnp.ones((16,), jnp.float32), (8, 128))
        _ctx_2048t = jnp.einsum('bsk,bkd->bsd', _ctx_2048c, _ctx_2048P)
        _ctx_2048t = _ctx_2048t * jax.lax.rsqrt(jnp.mean(jnp.square(_ctx_2048t)) + 1e-12) * 0.953939
        ctx_2048 = -1.47943e-05 + 1.00017 * (_ctx_2048t + 0.3 * jax.random.normal(jax.random.fold_in(_rk, 611), (8, 128, 256), jnp.float32))
        _validS = jnp.arange(128)[None, :] < _lenS[:, None]
        _validS2 = jnp.arange(128)[None, :] < _lenS2[:, None]
        _causal = jnp.tril(jnp.ones((128, 128), dtype=bool))
        mask_BxS2_bk0 = jnp.logical_not(jnp.broadcast_to(_validS2[:, :], (8, 128)))
        _g = jax.random.normal(jax.random.fold_in(_rk, 9001), (2, 4), jnp.float32)
        _g = jnp.sign(_g) * jnp.maximum(jnp.abs(_g), 1.0) + (_g == 0) * 1.0
        g_xattn = _g[0]
        g_ffn = _g[1]
        return (x, ctx_2048, mask_BxS2_bk0, g_xattn, g_ffn)
    x, ctx_2048, mask_BxS2_bk0, g_xattn, g_ffn = _rec_inputs()

    def _L0_xattn_setup():
        import jax, jax.numpy as jnp
        import numpy as np

        def _wkv(time_decay, time_first, k, v):
            w = -jnp.exp(time_decay)
            u = time_first
            B, T, C = k.shape
            aa = jnp.zeros((B, C), dtype=k.dtype)
            bb = jnp.zeros((B, C), dtype=k.dtype)
            pp = jnp.full((B, C), -1e+38, dtype=k.dtype)

            def step(carry, kv_t):
                aa, bb, pp = carry
                kt, vt = kv_t
                ww = u + kt
                q = jnp.maximum(pp, ww)
                e1 = jnp.exp(pp - q)
                e2 = jnp.exp(ww - q)
                y_t = (e1 * aa + e2 * vt) / (e1 * bb + e2)
                ww2 = pp + w
                q2 = jnp.maximum(ww2, kt)
                e1b = jnp.exp(ww2 - q2)
                e2b = jnp.exp(kt - q2)
                new_carry = (e1b * aa + e2b * vt, e1b * bb + e2b, q2)
                return (new_carry, y_t)
            ks = jnp.transpose(k, (1, 0, 2))
            vs = jnp.transpose(v, (1, 0, 2))
            _, ys = jax.lax.scan(step, (aa, bb, pp), (ks, vs))
            return jnp.transpose(ys, (1, 0, 2))
        key = jax.random.key(seed)
        k1, k2, k3, k4 = jax.random.split(key, 4)
        B, T, C = (8, 128, 256)
        return {'batch_size': B, 'seq_len': T, 'embedding_dim': C, 'time_decay': jax.random.normal(k1, (C,), dtype=jnp.float32), 'time_first': jax.random.normal(k2, (C,), dtype=jnp.float32), 'k': jax.random.normal(k3, (B, T, C), dtype=jnp.float32), 'v': jax.random.normal(k4, (B, T, C), dtype=jnp.float32)}
    _L0_xattn_all = _L0_xattn_setup()
    _L0_xattn_in = {k: v for k, v in _L0_xattn_all.items() if k in ('time_decay', 'time_first')}
    del _L0_xattn_all

    def _L0_ffn_setup():
        import jax, jax.numpy as jnp
        import numpy as np
        D = 256
        F = 176
        E = 8
        K = 2
        FS = 352
        B, S = (2, 128)
        key = jax.random.key(seed)
        ks = jax.random.split(key, 9)
        sc = 0.02
        return {'x': jax.random.normal(ks[0], (B, S, D), dtype=jnp.float32), 'Wr': jax.random.normal(ks[1], (E, D), dtype=jnp.float32) * sc, 'Wg': jax.random.normal(ks[2], (E, F, D), dtype=jnp.float32) * sc, 'Wu': jax.random.normal(ks[3], (E, F, D), dtype=jnp.float32) * sc, 'Wd': jax.random.normal(ks[4], (E, D, F), dtype=jnp.float32) * sc, 'Wsg': jax.random.normal(ks[5], (FS, D), dtype=jnp.float32) * sc, 'Wsu': jax.random.normal(ks[6], (FS, D), dtype=jnp.float32) * sc, 'Wsd': jax.random.normal(ks[7], (D, FS), dtype=jnp.float32) * sc}
    _L0_ffn_all = _L0_ffn_setup()
    _L0_ffn_in = {k: v for k, v in _L0_ffn_all.items() if k in ('Wr', 'Wg', 'Wu', 'Wd', 'Wsg', 'Wsu', 'Wsd')}
    del _L0_ffn_all

    def _L1_xattn_setup():
        import jax, jax.numpy as jnp
        import numpy as np
        key = jax.random.key(seed)
        k1, k2, k3 = jax.random.split(key, 3)
        B, S, D, M = (8, 256, 256, 128)
        hidden_states = jax.random.normal(k1, (B, S, D), dtype=jnp.float32)
        memory_tokens = jax.random.normal(k2, (B, M, D), dtype=jnp.float32)
        memory_mask = jax.random.randint(k3, (B, M), 0, 2).astype(jnp.bool_)
        return {'hidden_states': hidden_states, 'memory_tokens': memory_tokens, 'memory_mask': memory_mask}
    _L1_xattn_all = _L1_xattn_setup()
    _L1_xattn_in = {k: v for k, v in _L1_xattn_all.items() if k in ()}
    del _L1_xattn_all

    def _L1_ffn_setup():
        import jax, jax.numpy as jnp
        import numpy as np
        H = 256
        I = 128
        E = 32
        K = 4
        N_SHARED = 1
        EPS = 1e-06

        def _rmsnorm(x, w, eps=EPS):
            var = jnp.mean(jnp.square(x), axis=-1, keepdims=True)
            return x * jax.lax.rsqrt(var + eps) * w

        def _moe_core(x, gate_w, w13, w2):
            T = x.shape[0]
            N = T * K
            C = 2 * N // E
            logits = jnp.einsum('th,eh->te', x.astype(jnp.float32), gate_w.astype(jnp.float32))
            scores = jax.nn.softmax(logits, axis=-1)
            topk_w, topk_ids = jax.lax.top_k(scores, K)
            topk_w = topk_w / jnp.sum(topk_w, axis=-1, keepdims=True)
            flat_ids = topk_ids.reshape(-1)
            flat_w = topk_w.reshape(-1)
            order = jnp.argsort(flat_ids)
            sorted_eid = flat_ids[order]
            tok = order // K
            counts = jnp.zeros((E,), jnp.int32).at[flat_ids].add(1)
            starts = jnp.cumsum(counts) - counts
            pos = jnp.arange(N) - starts[sorted_eid]
            buf = jnp.zeros((E, C, x.shape[1]), x.dtype).at[sorted_eid, pos].set(x[tok], mode='drop')
            gu = jnp.einsum('ech,ehf->ecf', buf, w13)
            g, u = jnp.split(gu, 2, axis=-1)
            act = jax.nn.silu(g) * u
            eo = jnp.einsum('eci,eih->ech', act, w2)
            out_slots = eo[sorted_eid, pos]
            routed = jnp.zeros_like(x).at[tok].add(out_slots * flat_w[order][:, None])
            return routed
        key = jax.random.key(seed)
        ks = jax.random.split(key, 8)
        s = 1.0 / np.sqrt(H)
        si = 1.0 / np.sqrt(I)
        return {'hidden_states': jax.random.normal(ks[0], (1, 512, H), jnp.float32), 'norm_w': jnp.ones((H,), jnp.float32), 'gate_w': jax.random.normal(ks[1], (E, H), jnp.float32) * s, 'w13': jax.random.normal(ks[2], (E, H, 2 * I), jnp.float32) * s, 'w2': jax.random.normal(ks[3], (E, I, H), jnp.float32) * si, 'shared_gate_w': jax.random.normal(ks[4], (H, I * N_SHARED), jnp.float32) * s, 'shared_up_w': jax.random.normal(ks[5], (H, I * N_SHARED), jnp.float32) * s, 'shared_down_w': jax.random.normal(ks[6], (I * N_SHARED, H), jnp.float32) * si}
    _L1_ffn_all = _L1_ffn_setup()
    _L1_ffn_in = {k: v for k, v in _L1_ffn_all.items() if k in ('norm_w', 'gate_w', 'w13', 'w2', 'shared_gate_w', 'shared_up_w', 'shared_down_w')}
    del _L1_ffn_all

    def _L2_xattn_setup():
        import jax, jax.numpy as jnp
        import numpy as np
        DIM = 256
        NHEADS = 32
        HEAD_DIM = DIM // NHEADS
        EPS = 1e-06

        def _rmsnorm(t):
            return t * jax.lax.rsqrt(jnp.mean(t * t, axis=-1, keepdims=True) + EPS)
        key = jax.random.key(seed)
        kx, kc, kq, kk, kv = jax.random.split(key, 5)
        x = jax.random.normal(kx, (2, 512, DIM), dtype=jnp.float32)
        context = jax.random.normal(kc, (2, 64, DIM), dtype=jnp.float32)
        std = 0.02
        Wq = jax.random.normal(kq, (DIM, DIM), dtype=jnp.float32) * std
        Wk = jax.random.normal(kk, (DIM, DIM), dtype=jnp.float32) * std
        Wv = jax.random.normal(kv, (DIM, DIM), dtype=jnp.float32) * std
        return {'x': x, 'context': context, 'Wq': Wq, 'Wk': Wk, 'Wv': Wv}
    _L2_xattn_all = _L2_xattn_setup()
    _L2_xattn_in = {k: v for k, v in _L2_xattn_all.items() if k in ('Wq', 'Wk', 'Wv')}
    del _L2_xattn_all

    def _L2_ffn_setup():
        import jax, jax.numpy as jnp
        import numpy as np
        import math
        GOLDEN_CENTER = 1.0 / math.e
        GOLDEN_LOWER = 0.5 - math.log(4.0 / 3.0)
        GOLDEN_UPPER = 0.5
        B, T, D = (4, 128, 256)
        E = 8
        F = 1024 // (E // 2)
        R = 64
        NL = 2

        def _router_weights(x, Wr, temperature):
            logits = jnp.einsum('btd,de->bte', x, Wr)
            inhibition = jax.nn.sigmoid(logits / temperature)
            in_zone = (inhibition >= GOLDEN_LOWER) & (inhibition <= GOLDEN_UPPER)
            distance = jnp.abs(inhibition - GOLDEN_CENTER)
            w = jnp.exp(-distance / 0.1) * in_zone.astype(x.dtype)
            wsum = w.sum(axis=-1, keepdims=True)
            no_expert = wsum < 1e-08
            fb = jnp.exp(-distance / 0.3)
            _, top2 = jax.lax.top_k(fb, 2)
            fb_mask = jax.nn.one_hot(top2, E, dtype=x.dtype).sum(axis=-2)
            fb_w = fb * fb_mask
            fb_w = fb_w / jnp.clip(fb_w.sum(axis=-1, keepdims=True), 1e-08)
            w = jnp.where(no_expert, fb_w, w)
            return w / jnp.clip(w.sum(axis=-1, keepdims=True), 1e-08)
        key = jax.random.key(seed)
        ks = jax.random.split(key, 13)
        s = 0.02
        x = jax.random.normal(ks[0], (B, T, D), dtype=jnp.float32)
        Wg = jax.random.normal(ks[1], (E, D, F), dtype=jnp.float32) * s
        Wu = jax.random.normal(ks[2], (E, D, F), dtype=jnp.float32) * s
        Wd = jax.random.normal(ks[3], (E, F, D), dtype=jnp.float32) * s
        Ga = jax.random.normal(ks[4], (NL, D, R), dtype=jnp.float32) * s
        Gb = jax.random.normal(ks[5], (NL, R, F), dtype=jnp.float32) * s
        Ua = jax.random.normal(ks[6], (NL, D, R), dtype=jnp.float32) * s
        Ub = jax.random.normal(ks[7], (NL, R, F), dtype=jnp.float32) * s
        Da = jax.random.normal(ks[8], (NL, F, R), dtype=jnp.float32) * s
        Db = jax.random.normal(ks[9], (NL, R, D), dtype=jnp.float32) * s
        Wr = jax.random.normal(ks[10], (D, E), dtype=jnp.float32) * s
        temperature = jnp.ones((1,), dtype=jnp.float32)
        return {'x': x, 'Wg': Wg, 'Wu': Wu, 'Wd': Wd, 'Ga': Ga, 'Gb': Gb, 'Ua': Ua, 'Ub': Ub, 'Da': Da, 'Db': Db, 'Wr': Wr, 'temperature': temperature}
    _L2_ffn_all = _L2_ffn_setup()
    _L2_ffn_in = {k: v for k, v in _L2_ffn_all.items() if k in ('Wg', 'Wu', 'Wd', 'Ga', 'Gb', 'Ua', 'Ub', 'Da', 'Db', 'Wr', 'temperature')}
    del _L2_ffn_all

    def _L3_xattn_setup():
        import jax, jax.numpy as jnp
        import numpy as np
        NUM_HEADS = 16

        def _qdq(x):
            s = jnp.maximum(jnp.max(jnp.abs(x), axis=-1, keepdims=True) / 127.0, 1e-08)
            return jnp.clip(jnp.round(x / s), -127.0, 127.0) * s
        key = jax.random.key(seed)
        ks = jax.random.split(key, 8)
        B, N, M, D = (2, 512, 64, 256)
        w_std = 0.02
        return {'x': jax.random.normal(ks[0], (B, N, D), jnp.float32), 'cond': jax.random.normal(ks[1], (B, M, D), jnp.float32), 'wq': jax.random.normal(ks[2], (D, D), jnp.float32) * w_std, 'bq': jax.random.normal(ks[3], (D,), jnp.float32) * w_std, 'wkv': jax.random.normal(ks[4], (2 * D, D), jnp.float32) * w_std, 'bkv': jax.random.normal(ks[5], (2 * D,), jnp.float32) * w_std, 'wp': jax.random.normal(ks[6], (D, D), jnp.float32) * w_std, 'bp': jax.random.normal(ks[7], (D,), jnp.float32) * w_std}
    _L3_xattn_all = _L3_xattn_setup()
    _L3_xattn_in = {k: v for k, v in _L3_xattn_all.items() if k in ('wq', 'bq', 'wkv', 'bkv', 'wp', 'bp')}
    del _L3_xattn_all

    def _L3_ffn_setup():
        import jax, jax.numpy as jnp
        import numpy as np
        TOP_P = 0.9
        S, B, H, I, E = (256, 4, 256, 512, 8)

        def _top_p_weights(probs, top_p):
            order = jnp.argsort(-probs, axis=-1)
            sp = jnp.take_along_axis(probs, order, axis=-1)
            cum = jnp.cumsum(sp, axis=-1)
            exceed = cum > top_p
            first_idx = jnp.argmax(exceed, axis=-1)
            first = jnp.arange(probs.shape[-1])[None, :] == first_idx[:, None]
            keep = ~exceed | first
            kept = jnp.where(keep, sp, 0.0)
            t_idx = jnp.arange(probs.shape[0])[:, None]
            return jnp.zeros_like(probs).at[t_idx, order].set(kept)
        key = jax.random.key(seed)
        ks = jax.random.split(key, 5)
        scale = 0.02
        return {'hidden_states': jax.random.normal(ks[0], (S, B, H), dtype=jnp.float32), 'router_w': jax.random.normal(ks[1], (E, H), dtype=jnp.float32) * scale, 'gate_w': jax.random.normal(ks[2], (E, I, H), dtype=jnp.float32) * scale, 'up_w': jax.random.normal(ks[3], (E, I, H), dtype=jnp.float32) * scale, 'down_w': jax.random.normal(ks[4], (E, H, I), dtype=jnp.float32) * scale}
    _L3_ffn_all = _L3_ffn_setup()
    _L3_ffn_in = {k: v for k, v in _L3_ffn_all.items() if k in ('router_w', 'gate_w', 'up_w', 'down_w')}
    del _L3_ffn_all
    return {'x': x, 'ctx_2048': ctx_2048, 'mask_BxS2_bk0': mask_BxS2_bk0, 'g_xattn': g_xattn, 'g_ffn': g_ffn, 'L0_xattn_time_decay': _L0_xattn_in['time_decay'], 'L0_xattn_time_first': _L0_xattn_in['time_first'], 'L0_ffn_Wr': _L0_ffn_in['Wr'], 'L0_ffn_Wg': _L0_ffn_in['Wg'], 'L0_ffn_Wu': _L0_ffn_in['Wu'], 'L0_ffn_Wd': _L0_ffn_in['Wd'], 'L0_ffn_Wsg': _L0_ffn_in['Wsg'], 'L0_ffn_Wsu': _L0_ffn_in['Wsu'], 'L0_ffn_Wsd': _L0_ffn_in['Wsd'], 'L1_ffn_norm_w': _L1_ffn_in['norm_w'], 'L1_ffn_gate_w': _L1_ffn_in['gate_w'], 'L1_ffn_w13': _L1_ffn_in['w13'], 'L1_ffn_w2': _L1_ffn_in['w2'], 'L1_ffn_shared_gate_w': _L1_ffn_in['shared_gate_w'], 'L1_ffn_shared_up_w': _L1_ffn_in['shared_up_w'], 'L1_ffn_shared_down_w': _L1_ffn_in['shared_down_w'], 'L2_xattn_Wq': _L2_xattn_in['Wq'], 'L2_xattn_Wk': _L2_xattn_in['Wk'], 'L2_xattn_Wv': _L2_xattn_in['Wv'], 'L2_ffn_Wg': _L2_ffn_in['Wg'], 'L2_ffn_Wu': _L2_ffn_in['Wu'], 'L2_ffn_Wd': _L2_ffn_in['Wd'], 'L2_ffn_Ga': _L2_ffn_in['Ga'], 'L2_ffn_Gb': _L2_ffn_in['Gb'], 'L2_ffn_Ua': _L2_ffn_in['Ua'], 'L2_ffn_Ub': _L2_ffn_in['Ub'], 'L2_ffn_Da': _L2_ffn_in['Da'], 'L2_ffn_Db': _L2_ffn_in['Db'], 'L2_ffn_Wr': _L2_ffn_in['Wr'], 'L2_ffn_temperature': _L2_ffn_in['temperature'], 'L3_xattn_wq': _L3_xattn_in['wq'], 'L3_xattn_bq': _L3_xattn_in['bq'], 'L3_xattn_wkv': _L3_xattn_in['wkv'], 'L3_xattn_bkv': _L3_xattn_in['bkv'], 'L3_xattn_wp': _L3_xattn_in['wp'], 'L3_xattn_bp': _L3_xattn_in['bp'], 'L3_ffn_router_w': _L3_ffn_in['router_w'], 'L3_ffn_gate_w': _L3_ffn_in['gate_w'], 'L3_ffn_up_w': _L3_ffn_in['up_w'], 'L3_ffn_down_w': _L3_ffn_in['down_w']}

def reference(x, ctx_2048, mask_BxS2_bk0, g_xattn, g_ffn, L0_xattn_time_decay, L0_xattn_time_first, L0_ffn_Wr, L0_ffn_Wg, L0_ffn_Wu, L0_ffn_Wd, L0_ffn_Wsg, L0_ffn_Wsu, L0_ffn_Wsd, L1_ffn_norm_w, L1_ffn_gate_w, L1_ffn_w13, L1_ffn_w2, L1_ffn_shared_gate_w, L1_ffn_shared_up_w, L1_ffn_shared_down_w, L2_xattn_Wq, L2_xattn_Wk, L2_xattn_Wv, L2_ffn_Wg, L2_ffn_Wu, L2_ffn_Wd, L2_ffn_Ga, L2_ffn_Gb, L2_ffn_Ua, L2_ffn_Ub, L2_ffn_Da, L2_ffn_Db, L2_ffn_Wr, L2_ffn_temperature, L3_xattn_wq, L3_xattn_bq, L3_xattn_wkv, L3_xattn_bkv, L3_xattn_wp, L3_xattn_bp, L3_ffn_router_w, L3_ffn_gate_w, L3_ffn_up_w, L3_ffn_down_w):
    import jax
    import jax.numpy as jnp

    def _L0_xattn_ref(batch_size, seq_len, embedding_dim, time_decay, time_first, k, v):
        import jax, jax.numpy as jnp
        import numpy as np

        def _wkv(time_decay, time_first, k, v):
            w = -jnp.exp(time_decay)
            u = time_first
            B, T, C = k.shape
            aa = jnp.zeros((B, C), dtype=k.dtype)
            bb = jnp.zeros((B, C), dtype=k.dtype)
            pp = jnp.full((B, C), -1e+38, dtype=k.dtype)

            def step(carry, kv_t):
                aa, bb, pp = carry
                kt, vt = kv_t
                ww = u + kt
                q = jnp.maximum(pp, ww)
                e1 = jnp.exp(pp - q)
                e2 = jnp.exp(ww - q)
                y_t = (e1 * aa + e2 * vt) / (e1 * bb + e2)
                ww2 = pp + w
                q2 = jnp.maximum(ww2, kt)
                e1b = jnp.exp(ww2 - q2)
                e2b = jnp.exp(kt - q2)
                new_carry = (e1b * aa + e2b * vt, e1b * bb + e2b, q2)
                return (new_carry, y_t)
            ks = jnp.transpose(k, (1, 0, 2))
            vs = jnp.transpose(v, (1, 0, 2))
            _, ys = jax.lax.scan(step, (aa, bb, pp), (ks, vs))
            return jnp.transpose(ys, (1, 0, 2))
        assert seq_len <= 128
        return _wkv(time_decay, time_first, k, v)

    def _L0_ffn_ref(x, Wr, Wg, Wu, Wd, Wsg, Wsu, Wsd):
        import jax, jax.numpy as jnp
        import numpy as np
        D = 256
        F = 176
        E = 8
        K = 2
        FS = 352
        B, S = (2, 128)
        silu = jax.nn.silu
        sg = silu(jnp.einsum('bsd,fd->bsf', x, Wsg))
        su = jnp.einsum('bsd,fd->bsf', x, Wsu)
        shared_out = jnp.einsum('bsf,df->bsd', sg * su, Wsd)
        logits = jnp.einsum('bsd,ed->bse', x, Wr)
        scores = jax.nn.softmax(logits, axis=-1)
        topk_scores, topk_idx = jax.lax.top_k(scores, K)
        w_full = jnp.sum(jax.nn.one_hot(topk_idx, E, dtype=x.dtype) * topk_scores[..., None], axis=-2)
        g = silu(jnp.einsum('bsd,efd->bsef', x, Wg))
        u = jnp.einsum('bsd,efd->bsef', x, Wu)
        out_e = jnp.einsum('bsef,edf->bsed', g * u, Wd)
        routed_out = jnp.einsum('bsed,bse->bsd', out_e, w_full)
        return routed_out + shared_out

    def _L1_xattn_ref(hidden_states, memory_tokens, memory_mask):
        import jax, jax.numpy as jnp
        import numpy as np
        B, S, D = hidden_states.shape
        scale = 1.0 / jnp.sqrt(jnp.asarray(D, hidden_states.dtype))
        scores = jnp.einsum('bsd,bmd->bsm', hidden_states, memory_tokens) * scale
        neg_inf = jnp.asarray(-1e+30, scores.dtype)
        scores = jnp.where(memory_mask[:, None, :], scores, neg_inf)
        attn = jax.nn.softmax(scores, axis=-1)
        readout = jnp.einsum('bsm,bmd->bsd', attn, memory_tokens)
        valid_b = jnp.any(memory_mask, axis=-1)
        out = jnp.where(valid_b[:, None, None], readout, jnp.zeros_like(readout))
        return out

    def _L1_ffn_ref(hidden_states, norm_w, gate_w, w13, w2, shared_gate_w, shared_up_w, shared_down_w):
        import jax, jax.numpy as jnp
        import numpy as np
        H = 256
        I = 128
        E = 32
        K = 4
        N_SHARED = 1
        EPS = 1e-06

        def _rmsnorm(x, w, eps=EPS):
            var = jnp.mean(jnp.square(x), axis=-1, keepdims=True)
            return x * jax.lax.rsqrt(var + eps) * w

        def _moe_core(x, gate_w, w13, w2):
            T = x.shape[0]
            N = T * K
            C = 2 * N // E
            logits = jnp.einsum('th,eh->te', x.astype(jnp.float32), gate_w.astype(jnp.float32))
            scores = jax.nn.softmax(logits, axis=-1)
            topk_w, topk_ids = jax.lax.top_k(scores, K)
            topk_w = topk_w / jnp.sum(topk_w, axis=-1, keepdims=True)
            flat_ids = topk_ids.reshape(-1)
            flat_w = topk_w.reshape(-1)
            order = jnp.argsort(flat_ids)
            sorted_eid = flat_ids[order]
            tok = order // K
            counts = jnp.zeros((E,), jnp.int32).at[flat_ids].add(1)
            starts = jnp.cumsum(counts) - counts
            pos = jnp.arange(N) - starts[sorted_eid]
            buf = jnp.zeros((E, C, x.shape[1]), x.dtype).at[sorted_eid, pos].set(x[tok], mode='drop')
            gu = jnp.einsum('ech,ehf->ecf', buf, w13)
            g, u = jnp.split(gu, 2, axis=-1)
            act = jax.nn.silu(g) * u
            eo = jnp.einsum('eci,eih->ech', act, w2)
            out_slots = eo[sorted_eid, pos]
            routed = jnp.zeros_like(x).at[tok].add(out_slots * flat_w[order][:, None])
            return routed
        B, S, Hd = hidden_states.shape
        residual = hidden_states
        h = _rmsnorm(hidden_states, norm_w)
        x = h.reshape(-1, Hd)
        routed = _moe_core(x, gate_w, w13, w2)
        shared = jax.nn.silu(x @ shared_gate_w) * (x @ shared_up_w) @ shared_down_w
        out = residual + (routed + shared).reshape(B, S, Hd)
        return out

    def _L2_xattn_ref(x, context, Wq, Wk, Wv):
        import jax, jax.numpy as jnp
        import numpy as np
        DIM = 256
        NHEADS = 32
        HEAD_DIM = DIM // NHEADS
        EPS = 1e-06

        def _rmsnorm(t):
            return t * jax.lax.rsqrt(jnp.mean(t * t, axis=-1, keepdims=True) + EPS)
        b, n, _ = x.shape
        m = context.shape[1]
        q = x @ Wq.T
        k_raw = context @ Wk.T
        v_raw = context @ Wv.T
        q = q.reshape(b, n, NHEADS, HEAD_DIM).transpose(0, 2, 1, 3)
        kv = jnp.concatenate([k_raw, v_raw], axis=-1)
        kv = kv.reshape(b, m, NHEADS, HEAD_DIM, 2)
        k = kv[..., 0].transpose(0, 2, 1, 3)
        v = kv[..., 1].transpose(0, 2, 1, 3)
        q = _rmsnorm(q)
        k = _rmsnorm(k)
        scale = HEAD_DIM ** (-0.5)
        scores = jnp.einsum('bhnd,bhmd->bhnm', q, k) * scale
        attn = jax.nn.softmax(scores, axis=-1)
        out = jnp.einsum('bhnm,bhmd->bhnd', attn, v)
        return out.transpose(0, 2, 1, 3).reshape(b, n, NHEADS * HEAD_DIM)

    def _L2_ffn_ref(x, Wg, Wu, Wd, Ga, Gb, Ua, Ub, Da, Db, Wr, temperature):
        import jax, jax.numpy as jnp
        import numpy as np
        import math
        GOLDEN_CENTER = 1.0 / math.e
        GOLDEN_LOWER = 0.5 - math.log(4.0 / 3.0)
        GOLDEN_UPPER = 0.5
        B, T, D = (4, 128, 256)
        E = 8
        F = 1024 // (E // 2)
        R = 64
        NL = 2

        def _router_weights(x, Wr, temperature):
            logits = jnp.einsum('btd,de->bte', x, Wr)
            inhibition = jax.nn.sigmoid(logits / temperature)
            in_zone = (inhibition >= GOLDEN_LOWER) & (inhibition <= GOLDEN_UPPER)
            distance = jnp.abs(inhibition - GOLDEN_CENTER)
            w = jnp.exp(-distance / 0.1) * in_zone.astype(x.dtype)
            wsum = w.sum(axis=-1, keepdims=True)
            no_expert = wsum < 1e-08
            fb = jnp.exp(-distance / 0.3)
            _, top2 = jax.lax.top_k(fb, 2)
            fb_mask = jax.nn.one_hot(top2, E, dtype=x.dtype).sum(axis=-2)
            fb_w = fb * fb_mask
            fb_w = fb_w / jnp.clip(fb_w.sum(axis=-1, keepdims=True), 1e-08)
            w = jnp.where(no_expert, fb_w, w)
            return w / jnp.clip(w.sum(axis=-1, keepdims=True), 1e-08)
        weights = _router_weights(x, Wr, temperature)
        gate = jnp.einsum('btd,edf->ebtf', x, Wg)
        up = jnp.einsum('btd,edf->ebtf', x, Wu)
        gate = gate.at[:NL].add(jnp.einsum('btd,edr,erf->ebtf', x, Ga, Gb))
        up = up.at[:NL].add(jnp.einsum('btd,edr,erf->ebtf', x, Ua, Ub))
        mid = jax.nn.silu(gate) * up
        out = jnp.einsum('ebtf,efd->ebtd', mid, Wd)
        out = out.at[:NL].add(jnp.einsum('ebtf,efr,erd->ebtd', mid[:NL], Da, Db))
        return jnp.einsum('bte,ebtd->btd', weights, out)

    def _L3_xattn_ref(x, cond, wq, bq, wkv, bkv, wp, bp):
        import jax, jax.numpy as jnp
        import numpy as np
        NUM_HEADS = 16

        def _qdq(x):
            s = jnp.maximum(jnp.max(jnp.abs(x), axis=-1, keepdims=True) / 127.0, 1e-08)
            return jnp.clip(jnp.round(x / s), -127.0, 127.0) * s
        B, N, C = x.shape
        M = cond.shape[1]
        H = NUM_HEADS
        Dh = C // H
        q = _qdq(x) @ _qdq(wq).T + bq
        kv = cond @ wkv.T + bkv
        k, v = jnp.split(kv, 2, axis=-1)
        q = q.reshape(B, N, H, Dh)
        k = k.reshape(B, M, H, Dh)
        v = v.reshape(B, M, H, Dh)
        scale = 1.0 / np.sqrt(Dh)
        attn = jax.nn.softmax(jnp.einsum('bnhd,bmhd->bhnm', q, k) * scale, axis=-1)
        o = jnp.einsum('bhnm,bmhd->bnhd', attn, v).reshape(B, N, C)
        out = _qdq(o) @ _qdq(wp).T + bp
        return out

    def _L3_ffn_ref(hidden_states, router_w, gate_w, up_w, down_w):
        import jax, jax.numpy as jnp
        import numpy as np
        TOP_P = 0.9
        S, B, H, I, E = (256, 4, 256, 512, 8)

        def _top_p_weights(probs, top_p):
            order = jnp.argsort(-probs, axis=-1)
            sp = jnp.take_along_axis(probs, order, axis=-1)
            cum = jnp.cumsum(sp, axis=-1)
            exceed = cum > top_p
            first_idx = jnp.argmax(exceed, axis=-1)
            first = jnp.arange(probs.shape[-1])[None, :] == first_idx[:, None]
            keep = ~exceed | first
            kept = jnp.where(keep, sp, 0.0)
            t_idx = jnp.arange(probs.shape[0])[:, None]
            return jnp.zeros_like(probs).at[t_idx, order].set(kept)
        s, b, h = hidden_states.shape
        x = hidden_states.reshape(-1, h)
        probs = jax.nn.softmax(x @ router_w.T, axis=-1)
        w = _top_p_weights(probs, TOP_P)
        out = jnp.zeros_like(x)
        n_exp = router_w.shape[0]
        for e in range(n_exp):
            g = jax.nn.silu(x @ gate_w[e].T)
            u = x @ up_w[e].T
            y = g * u @ down_w[e].T
            out = out + y * w[:, e:e + 1]
        return out.reshape(s, b, h)
    x = x + jnp.tanh(g_xattn[0]) * _L0_xattn_ref(8, 128, 256, L0_xattn_time_decay, L0_xattn_time_first, _layernorm(x, axis=-1), ctx_2048)
    x = x + jnp.tanh(g_ffn[0]) * _L0_ffn_ref(_layernorm(x, axis=-1), L0_ffn_Wr, L0_ffn_Wg, L0_ffn_Wu, L0_ffn_Wd, L0_ffn_Wsg, L0_ffn_Wsu, L0_ffn_Wsd)
    x = x + jnp.tanh(g_xattn[1]) * _L1_xattn_ref(_layernorm(x, axis=-1), ctx_2048, mask_BxS2_bk0)
    x = x + jnp.tanh(g_ffn[1]) * _L1_ffn_ref(_layernorm(x, axis=-1), L1_ffn_norm_w, L1_ffn_gate_w, L1_ffn_w13, L1_ffn_w2, L1_ffn_shared_gate_w, L1_ffn_shared_up_w, L1_ffn_shared_down_w)
    x = x + jnp.tanh(g_xattn[2]) * _L2_xattn_ref(_layernorm(x, axis=-1), ctx_2048, L2_xattn_Wq, L2_xattn_Wk, L2_xattn_Wv)
    x = x + jnp.tanh(g_ffn[2]) * _L2_ffn_ref(_layernorm(x, axis=-1), L2_ffn_Wg, L2_ffn_Wu, L2_ffn_Wd, L2_ffn_Ga, L2_ffn_Gb, L2_ffn_Ua, L2_ffn_Ub, L2_ffn_Da, L2_ffn_Db, L2_ffn_Wr, L2_ffn_temperature)
    x = x + jnp.tanh(g_xattn[3]) * _L3_xattn_ref(_layernorm(x, axis=-1), ctx_2048, L3_xattn_wq, L3_xattn_bq, L3_xattn_wkv, L3_xattn_bkv, L3_xattn_wp, L3_xattn_bp)
    x = x + jnp.tanh(g_ffn[3]) * _L3_ffn_ref(_layernorm(x, axis=-1), L3_ffn_router_w, L3_ffn_gate_w, L3_ffn_up_w, L3_ffn_down_w)
    return x

_drawn_inputs = setup_inputs


def setup_inputs(seed=0):
    import zlib

    import numpy as np

    out = dict(_drawn_inputs(seed))
    spreads = {'L1_ffn_norm_w': (1.0, 0.2)}
    factors = {'g_ffn': 2.678,
     'L0_ffn_Wr': 8.0,
     'L0_ffn_Wg': 8.0,
     'L0_ffn_Wu': 8.0,
     'L0_ffn_Wd': 8.0,
     'L0_ffn_Wsg': 3.106,
     'L0_ffn_Wsu': 2.92,
     'L0_ffn_Wsd': 2.879,
     'L2_xattn_Wq': 2.915,
     'L2_ffn_Wg': 8.0,
     'L2_ffn_Wu': 8.0,
     'L2_ffn_Wd': 8.0,
     'L2_ffn_Ga': 8.0,
     'L2_ffn_Gb': 8.0,
     'L2_ffn_Ua': 8.0,
     'L2_ffn_Ub': 8.0,
     'L2_ffn_Da': 8.0,
     'L2_ffn_Db': 8.0,
     'L2_ffn_Wr': 8.0,
     'L3_xattn_wq': 8.0,
     'L3_xattn_bq': 200.0,
     'L3_xattn_wkv': 3.026,
     'L3_xattn_bkv': 43.501,
     'L3_xattn_wp': 3.121,
     'L3_xattn_bp': 48.378,
     'L3_ffn_router_w': 8.0,
     'L3_ffn_gate_w': 8.0,
     'L3_ffn_up_w': 8.0,
     'L3_ffn_down_w': 8.0}
    for name, (base, spread) in spreads.items():
        noise = np.random.default_rng([zlib.crc32(name.encode()), seed]).standard_normal(out[name].shape)
        drawn = base * np.exp(spread * noise) if base else spread * noise
        out[name] = jnp.asarray(drawn.astype(out[name].dtype))
    for name, factor in factors.items():
        out[name] = (out[name] * factor).astype(out[name].dtype)
    return out
```

```python
from contextlib import ExitStack

import numpy as np

import concourse.bass as bass
from concourse import mybir
from concourse.alu_op_type import AluOpType as ALU


F32 = mybir.dt.float32
F16 = mybir.dt.float16
BF16 = mybir.dt.bfloat16
U8 = mybir.dt.uint8
ACT = mybir.ActivationFunctionType
AX = mybir.AxisListType

P = 128
B, S, D = 8, 128, 256
T = B * S
KD = D // P
HALF = T // 2
SEG = S + 1
LN_EPS = 1e-5
RMS_EPS = 1e-6
FAR = -1e38

E0, F0, FS0 = 8, 176, 352
E1, F1 = 32, 128
E2, F2 = 8, 256
E3, F3 = 8, 512
NT0 = -(-(E0 * F0 + FS0) // P)
NT1 = E1 * F1 // P + 1
NT2 = E2 * F2 // P
NT3 = E3 * F3 // P
NT = (NT0, NT1, NT2, NT3)
EXPERTS = (E0, E1, E2, E3)
ROUTER_AT = (0, E0, E0 + E1, E0 + E1 + E2)
ROUTERS = E0 + E1 + E2 + E3
TOP0, TOP1 = 2, 4
CAPACITY = 2 * T * TOP1 // E1
WROW = 3 * D
LORA_E, LORA_R = 2, 64
GOLDEN_CENTER = float(1.0 / np.e)
GOLDEN_LOWER = float(0.5 - np.log(4.0 / 3.0))
GOLDEN_UPPER = 0.5
TOP_P = 0.9
H2, DH2 = 32, 8
H3, DH3 = 16, 16
ROUND = 1.5 * 2.0 ** 23


def build(nc, a, out):
    with ExitStack() as ctx:
        def sb(name, shape, dt=F32):
            return ctx.enter_context(nc.sbuf_tensor(name, shape, dt))

        sems = {}

        def sem(name, k=None):
            key = name if k is None else f"{name}_{k}"
            if key not in sems:
                sems[key] = ctx.enter_context(nc.semaphore(key))
            return sems[key]

        ps = ctx.enter_context(nc.psum_tensor("ps", [P, 8, 512], F32))
        x = sb("x", [P, B, D])
        xn = sb("xn", [P, B, D])
        turned_buf = sb("turned_buf", [P, KD * B * SEG])
        xT = turned_buf[:, 0:KD * T].rearrange("p (c t) -> p c t", c=KD)
        wk_k = turned_buf[:, :].rearrange("p (c b s) -> p c b s", c=KD, b=B)
        ctx_sb = sb("ctx_sb", [P, B, D])
        ctxT = sb("ctxT", [P, KD, B, SEG])
        ident = sb("ident", [P, P])
        ident16 = sb("ident16", [P, P], F16)
        identb = sb("identb", [P, P], BF16)
        gates = sb("gates", [P, 8])
        tg = sb("tg", [P, 8])
        wr = sb("wr", [P, KD, ROUTERS])
        normw = sb("normw", [P, KD])
        stats = sb("stats", [P, B, 6])
        mv = sb("mv", [P, B, 2])
        veps = sb("veps", [P, B])
        rstd = sb("rstd", [P, B])
        rms = sb("rms", [P, B])
        mhalf = sb("mhalf", [P, 256])
        ones = sb("ones", [P, P])
        W = sb("W", [P, 2, WROW])
        wb = sb("wb", [P, 2, T])
        td = sb("td", [P, KD])
        tf = sb("tf", [P, KD])
        wdec = sb("wdec", [P, KD])
        tinv = sb("tinv", [P, 1])
        mask8 = sb("mask8", [P, B, S], U8)
        k2T = sb("k2T", [P, B, H2 // 4, S], F16)
        v2 = sb("v2", [P, B, H2, DH2 + 1])
        k3T = sb("k3T", [P, B, H3 // 4, S])
        v3 = sb("v3", [P, B, H3, DH3 + 1])
        wq2 = sb("wq2", [P, KD, D])
        wkv2 = sb("wkv2", [P, KD, 2 * D])
        wkv3 = sb("wkv3", [P, KD, 2 * D])
        bkv3 = sb("bkv3", [1, 2 * D])
        bq3 = sb("bq3", [P, D])
        bp3 = sb("bp3", [P, D])
        wi = sb("wi", [P, 2, KD, D], BF16)
        wscale = sb("wscale", [P, 2, D])
        k_raw = sb("k_raw", [P, 2, D])
        k_sq = sb("k_sq", [P, 2, D])
        k_norm = sb("k_norm", [P, H2])
        k_st = sb("k_st", [P, 2, H2, 4, DH2], F16)
        k3p = sb("k3p", [P, H3, 32])
        ARENA = 16600
        arena = sb("arena", [P, ARENA])

        class Arena:
            def __init__(self):
                self.at = 0

            def take(self, shape, dt=F32, rows=P):
                n = 1
                for k in shape:
                    n *= k
                words = n if dt == F32 else (n + 1) // 2
                v = arena[0:rows, self.at:self.at + words]
                self.at += words
                assert self.at <= ARENA, self.at
                if dt != F32:
                    v = v.bitcast(dt)
                if len(shape) > 1:
                    names = "abcdef"[:len(shape)]
                    v = v.rearrange(f"p ({' '.join(names)}) -> p {' '.join(names)}",
                                    **{c: k for c, k in zip(names[1:], shape[1:])})
                return v

        routed = [nc.dram_tensor(f"routed_{L}", (EXPERTS[L] + 1, T), F32, kind="Internal").ap() for L in range(4)]
        LORA_T = LORA_E * F2 // P
        folded = nc.dram_tensor("folded", (LORA_T, P, WROW), F32, kind="Internal").ap()

        ar = Arena()
        LW = B * SEG
        wk_dec = ar.take([LW])
        wk_pp = ar.take([LW + 1])
        wk_aa = ar.take([LW + 1])
        wk_bb = ar.take([LW + 1])
        wk_d = ar.take([2, LW])
        wk_e = ar.take([KD, 4, LW])
        wk_ev = ar.take([2, LW])
        lora = sb("lora", [LORA_R, 6, D])
        fold = W[:, 0, :]
        fold_add = W[:, 1, :]
        wq_s = sb("wq_s", [P, 3, 4])
        wq_f = wb[:, 0, :].rearrange("p (w o d) -> p w o d", w=2, o=KD)
        wq_i = wb[:, 1, 0:HALF].bitcast(BF16).rearrange("p (w o d) -> p w o d", w=2, o=KD)
        wq_diag = wb[:, 1, HALF:T].rearrange("p (k o) -> p k o", k=4)

        ar = Arena()
        a1_mask = ar.take([B, S])
        a1_neg = ar.take([B, S])
        a1_p = ar.take([B, S])
        a1_pT = ar.take([B, S])
        a1_s = ar.take([6, B])

        ar = Arena()
        f_s = ar.take([2, HALF])
        f_sw = ar.take([2, HALF])
        f_h = ar.take([2, T])
        f_lg = ar.take([B, E1])
        f_w = ar.take([B, E1])
        f_s8 = ar.take([6, B])
        f_wT = ar.take([T], rows=E1)
        f_cmp = ar.take([B, E0, E0])
        f_eq = ar.take([B, E0, E0])
        f_tri = ar.take([E0, E0])
        f_rk = ar.take([B, E0])
        f_a = ar.take([B, E0])
        f_b = ar.take([B, E0])
        m_x = ar.take([B, E1 + 8])
        m_rep = ar.take([B, E1 + 8])
        m_top = ar.take([B, 8])
        m_sel = ar.take([B, E1])
        m_last = ar.take([B, E1])
        m_raw = ar.take([T], rows=E1)
        m_selT = ar.take([T], rows=E1)
        m_cum = ar.take([T], rows=E1)
        m_zero = ar.take([T], rows=E1)
        m_dropT = ar.take([T], rows=E1)
        m_lastT = ar.take([T], rows=E1)
        m_xs = ar.take([KD, E1])
        m_ss = ar.take([1])
        m_hs = ar.take([2, 1])
        m_rT = ar.take([KD, E1])
        m_r = ar.take([D], rows=E1)
        x_rms = xn

        ar = Arena()
        a2_q = ar.take([B, H2, DH2])
        a2_st = ar.take([B, H2, 4, DH2], F16)
        a2_qT = ar.take([2, H2 // 4, S], F16)
        a2_p = ar.take([2, 2, 4, S])
        a2_n = ar.take([3, 256])
        a2_o = ar.take([H2, DH2])
        a2_rc = ar.take([H2])

        ar = Arena()
        a3_y = ar.take([B, D])
        a3_o = ar.take([B, D])
        a3_xi = ar.take([B, D], BF16)
        a3_xiT = ar.take([KD, T], BF16)
        a3_s = ar.take([2, 3, B])
        a3_qp = ar.take([2, H3, 32])
        a3_qT = ar.take([2, H3 // 4, S])
        a3_p = ar.take([2, H3, S])
        a3_pT = ar.take([H3, S])
        a3_mx = ar.take([H3])
        a3_rc = ar.take([H3])

        block = ctx.enter_context(nc.Block())

        def bank(k):
            return ps[:, k, :]

        def seq_heads(k):
            return ps[:, k, :].bitcast(F16)

        TURNS = [(NT[L] - 2) // 2 for L in range(4)]

        def tiles(L):
            return sum(NT[:L])

        def halves(L):
            return 2 * tiles(L)

        def slot_tiles(L, slot):
            return sum((NT[m] + 1 - slot) // 2 for m in range(L))

        def wb_loads(L, slot):
            return slot_tiles(L, slot) + (slot_tiles(1, slot) if L else 0)

        def at(n, j, per=2):
            return n if j is None else per * j + n

        def turns_before(s):
            return s if s < 7 else 6

        @block.sync
        def _(sp):
            sp.dma_start(x[:, :, :], a["x"].rearrange("b s d -> s b d")).then_inc(sem("x_in"), 16)
            sp.dma_start(td[:, :], a["time_decay"]).then_inc(sem("small_in"), 16)
            sp.dma_start(tf[:, :], a["time_first"]).then_inc(sem("small_in"), 16)
            sp.dma_start(gates[:, :], a["gates"].partition_broadcast(P)).then_inc(sem("small_in"), 16)
            sp.dma_start(tinv[:, :], a["temperature"].partition_broadcast(P)).then_inc(sem("small_in"), 16)
            sp.dma_start(normw[:, :], a["norm_w"]).then_inc(sem("small_in"), 16)
            sp.dma_start(ctx_sb[:, :, :], a["ctx"].rearrange("b s d -> s b d")).then_inc(sem("ctx_in"), 16)
            sp.dma_start(wkv2[:, :, :], a["wkv2"]).then_inc(sem("kv_in"), 16)
            sp.dma_start(wkv3[:, :, :], a["wkv3"]).then_inc(sem("kv_in"), 16)
            sp.dma_start(bkv3[:, :], a["bkv3"]).then_inc(sem("kv_in"), 16)
            sp.dma_start(wq_f, a["wqp3"]).then_inc(sem("wqp_in"), 16)
            for k in range(LORA_T):
                if k:
                    sp.wait_ge(sem("folded_out"), 16 * k)
                if k % (F2 // P) == 0:
                    if k:
                        sp.wait_ge(sem("fold_mm"), k)
                    sp.dma_start(lora[:, :, :], a["lora"][:, k * P // F2]).then_inc(sem("lora_in"), 16)
                sp.dma_start(fold, a["w2"][k]).then_inc(sem("fold_in"), 16)
                sp.wait_ge(sem("fold_sum"), k + 1)
                sp.dma_start(folded[k], fold).then_inc(sem("folded_out"), 16)
            sp.wait_ge(sem("folded_out"), 16 * LORA_T)
            sp.dma_start(wr[:, :, :], a["wr"]).then_inc(sem("late_in"), 16)
            sp.dma_start(wq2[:, :, :], a["wq2"]).then_inc(sem("late_in"), 16)
            sp.dma_start(bq3[:, :], a["bq3"].partition_broadcast(P)).then_inc(sem("late_in"), 16)
            sp.dma_start(bp3[:, :], a["bp3"].partition_broadcast(P)).then_inc(sem("late_in"), 16)
            sp.dma_start(mask8[:, :, :].rearrange("p b s -> p (b s)"),
                         a["mask"].rearrange("b s -> (b s)").partition_broadcast(P)).then_inc(sem("late_in"), 16)

            sp.wait_ge(sem("ones"), 1)
            for L in range(2):
                sp.dma_start(routed[L][EXPERTS[L]].rearrange("(p k) -> p k", p=P), ones[:, 0:T // P]).then_inc(sem("ones_out"), 16)
            sp.wait_ge(sem("ones_out"), 16 * 2)

            PARTS = ((slice(0, 2 * D), "gu_in"), (slice(2 * D, 3 * D), "down_in"))

            def source(L, i):
                return folded[i] if L == 2 and i < LORA_T else a[f"w{L}"][i]

            def head_loads(L):
                if L > 0:
                    sp.wait_ge(sem("down_done"), tiles(L))
                for i in range(2):
                    for part, name in PARTS:
                        sp.dma_start(W[:, i, part], source(L, i)[:, part]).then_inc(sem(name, i), 16)

            def routed_out(L):
                if L == 1:
                    sp.wait_ge(sem("wT_ready", 1), 1)
                else:
                    sp.wait_ge(sem("wT_half"), (2, None, 4, 6)[L])
                sp.dma_start(routed[L][0:EXPERTS[L], :], f_wT[0:EXPERTS[L], :]).then_inc(sem("routed_out"), 16)
                sp.wait_ge(sem("routed_out"), 16 * (L + 1))

            def gu_load(src, slot, before, star=None):
                sp.wait_ge(sem("gu_done"), before)
                if star is not None:
                    sp.wait_ge(sem("star_mm"), star)
                sp.dma_start(W[:, slot, 0:2 * D], src[:, 0:2 * D]).then_inc(sem("gu_in", slot), 16)

            def down_load(src, slot, before):
                sp.wait_ge(sem("down_done"), before)
                sp.dma_start(W[:, slot, 2 * D:3 * D], src[:, 2 * D:3 * D]).then_inc(sem("down_in", slot), 16)

            def wb_load(L, row, slot, before):
                sp.wait_ge(sem("sw_done"), before)
                sp.dma_start(wb[:, slot, :], routed[L][row].partition_broadcast(P))\
                    .then_inc(sem("wb_in", slot), 16)

            def tile_loads(L, i, row, e=None, per=0):
                if e is None:
                    src, n, before = source(L, i), i, tiles(L) + i - 1
                    twice = 2 * before
                else:
                    src, n, before = a[f"w{L}"][e * per + i], e * per + i, e * per + (tiles(L) + i - 1)
                    twice = e * (2 * per) + 2 * (tiles(L) + i - 1)
                old = e is not None or i >= 2
                if old:
                    gu_load(src, i % 2, twice, (i - 1 if e is None else e * per + (i - 1)) if L == 1 else None)
                wb_load(L, row, i % 2, twice)
                if old:
                    down_load(src, i % 2, before)

            def loads_0():
                sp.wait_ge(sem("wi"), 2)
                for i in range(NT0):
                    if i >= 2:
                        gu_load(a["w0"][i], i % 2, 2 * i - 2)
                        sp.wait_ge(sem("sw_done"), 2 * i - 2)
                    for lo, hi, row in PIECES[i]:
                        sp.dma_start(wb[lo:hi, i % 2, :], routed[0][row].partition_broadcast(hi - lo))\
                            .then_inc(sem("wb_in", i % 2), 16)
                    if i >= 2:
                        down_load(a["w0"][i], i % 2, i - 1)

            def loads_1():
                for i in range(2):
                    tile_loads(1, i, i)
                with sp.Fori(1, E1 // 2) as e:
                    for k in range(2):
                        tile_loads(1, k, 2 * e + k, e, 2)
                tile_loads(1, E1, E1)

            def loads_2():
                for i in range(LORA_T):
                    tile_loads(2, i, i // 2)
                with sp.Fori(LORA_T // 2, E2) as e:
                    for k in range(2):
                        tile_loads(2, k, e, e, 2)

            def loads_3():
                per = F3 // P
                for i in range(per):
                    tile_loads(3, i, 0)
                with sp.Fori(1, E3) as e:
                    for k in range(per):
                        tile_loads(3, k, e, e, per)

            for L, loads in enumerate((loads_0, loads_1, loads_2, loads_3)):
                head_loads(L)
                routed_out(L)
                loads()

            sp.wait_ge(sem("x_done"), 1)
            sp.dma_start(out.rearrange("b s d -> s b d"), x[:, :, :]).then_inc(sem("out_done"), 16)
            sp.wait_ge(sem("out_done"), 16)
            sp.wait_ge(sem("late_in"), 16 * 5)

        @block.gpsimd
        def _(pool):
            steps = [0]

            def link(ins):
                steps[0] += 1
                ins.then_inc(sem("pool_step"), 1)
                pool.wait_ge(sem("pool_step"), steps[0])

            link(nc.gpsimd.memset(ident[:, :], 0.0))
            nc.gpsimd.affine_select(out=ident[:, :], in_=ident[:, :], compare_op=ALU.not_equal, fill=1.0,
                                    base=0, pattern=[[-1, P]], channel_multiplier=1).then_inc(sem("ident"), 1)
            nc.gpsimd.memset(mhalf[:, :], -0.5).then_inc(sem("mhalf"), 1)
            nc.gpsimd.memset(ctxT[:, :, :, 0:1], 0.0).then_inc(sem("wkv_edges"), 1)
            nc.gpsimd.memset(wk_k[:, :, :, 0:1], FAR).then_inc(sem("wkv_edges"), 1)
            nc.gpsimd.memset(wk_pp[:, 0:1], 0.0).then_inc(sem("wkv_edges"), 1)
            nc.gpsimd.memset(wk_aa[:, 0:1], 0.0).then_inc(sem("wkv_edges"), 1)
            nc.gpsimd.memset(wk_bb[:, 0:1], 1.0).then_inc(sem("wkv_edges"), 1)
            pool.wait_ge(sem("ident"), 1)
            nc.gpsimd.tensor_copy(ident16[:, :], ident[:, :]).then_inc(sem("ident"), 1)
            nc.gpsimd.tensor_copy(identb[:, :], ident[:, :]).then_inc(sem("ident"), 1)
            nc.gpsimd.memset(ones[:, :], 1.0).then_inc(sem("ones"), 1)
            nc.gpsimd.memset(v2[:, :, :, DH2:DH2 + 1], 1.0).then_inc(sem("v_ones"), 1)
            nc.gpsimd.memset(v3[:, :, :, DH3:DH3 + 1], 1.0).then_inc(sem("v_ones"), 1)
            nc.gpsimd.memset(k3p[:, :, :], 0.0).then_inc(sem("k3p_zero"), 1)

            def inv_sqrt(s):
                pool.wait_ge(sem("ln_var"), s + 1)
                if s == 0:
                    pool.wait_ge(sem("mhalf"), 1)
                nc.gpsimd.tensor_tensor(rstd[:, :], veps[:, :], mhalf[:, 0:B], ALU.pow).then_inc(sem("ln_rstd"), 1)

            def wkv():
                for c in range(KD):
                    pool.wait_ge(sem("wkv_exp"), 4 * c + 3)
                    pool.wait_ge(sem("ctxT_ready"), 4)
                    if c:
                        pool.wait_ge(sem("wkv_y"), c)
                    v = ctxT[:, c, :, :].rearrange("p b s -> p (b s)")
                    for k, e in ((0, 1), (1, 2)):
                        nc.gpsimd.tensor_tensor(wk_ev[:, k, :], wk_e[:, c, e, :], v, ALU.mult)\
                            .then_inc(sem("wkv_ev"), 1)

            def fold_lora():
                for k in range(LORA_T):
                    pool.wait_ge(sem("fold_in"), 16 * (k + 1))
                    pool.wait_ge(sem("fold_add"), 2 * (k + 1))
                    nc.gpsimd.tensor_tensor(fold, fold, fold_add, ALU.add).then_inc(sem("fold_sum"), 1)

            def whole_weights():
                pool.wait_ge(sem("wq_scale"), 1)
                for k in range(4):
                    w = wq_f[:, k // 2, k % 2, :]
                    link(nc.gpsimd.tensor_scalar(w, w, wq_s[:, 2, k:k + 1], None, ALU.mult))
                link(nc.gpsimd.tensor_scalar(wq_f, wq_f, ROUND, 1.0, ALU.add, ALU.mult))
                link(nc.gpsimd.tensor_scalar(wq_f, wq_f, -ROUND, 1.0, ALU.add, ALU.mult))
                nc.gpsimd.tensor_scalar(wq_i, wq_f, 127.0, -127.0, ALU.min, ALU.max)\
                    .then_inc(sem("wq_whole"), 1)
                for k in range(4):
                    ins = nc.gpsimd.tensor_scalar(wq_diag[:, k, :], ident[:, :], wq_s[:, 1, k:k + 1], None, ALU.mult)
                ins.then_inc(sem("wq_diag"), 1)

            def keys_2():
                for b in range(B):
                    sl = b % 2
                    raw = k_raw[:, sl, :].rearrange("p (h d) -> p h d", d=DH2)
                    sq = k_sq[:, sl, :].rearrange("p (h d) -> p h d", d=DH2)
                    pool.wait_ge(sem("k2_raw"), 2 * (b + 1))
                    for n in (4, 2):
                        link(nc.gpsimd.tensor_tensor(sq[:, :, 0:n], sq[:, :, 0:n], sq[:, :, n:2 * n], ALU.add))
                    kn = k_norm[:, :]
                    link(nc.gpsimd.tensor_tensor(kn.unsqueeze(2), sq[:, :, 0:1], sq[:, :, 1:2], ALU.add))
                    link(nc.gpsimd.tensor_scalar(kn, kn, 1.0 / DH2, RMS_EPS, ALU.mult, ALU.add))
                    link(nc.gpsimd.tensor_tensor(kn, kn, mhalf[:, 0:H2], ALU.pow))
                    link(nc.gpsimd.tensor_tensor(raw, raw, kn.unsqueeze(2).to_broadcast((P, H2, DH2)), ALU.mult))
                    if b >= 2:
                        pool.wait_ge(sem("k2_turn"), b - 1)
                    nc.gpsimd.tensor_copy(k_st[:, sl, :, 0, :], raw)
                    link(nc.gpsimd.tensor_copy(k_st[:, sl, :, 2, :], raw))
                    nc.gpsimd.tensor_tensor(k_st[:, sl, :, 1, :], raw, k_st[:, sl, :, 0, :], ALU.subtract)
                    ins = nc.gpsimd.tensor_tensor(k_st[:, sl, :, 3, :], raw, k_st[:, sl, :, 2, :], ALU.subtract)
                    ins.then_inc(sem("k2_split"), 1)
                    pool.wait_ge(sem("k2_split"), b + 1)

            def sw(L, k, half, j=None):
                loads = 32 if L == 0 else 16
                arrived = 16 * wb_loads(L, k % 2) + loads * (k // 2 + 1)
                n = halves(L) + 2 * k + half + 1
                pool.wait_ge(sem("silu_done"), at(n, j, 4))
                if half == 0:
                    pool.wait_ge(sem("wb_in", k % 2), at(arrived, j, loads))
                if tiles(L) + k:
                    pool.wait_ge(sem("h_done"), at(n - 2, j, 4))
                nc.gpsimd.tensor_tensor(f_sw[:, half, :], f_s[:, half, :], wb[:, k % 2, half * HALF:(half + 1) * HALF],
                                        ALU.mult).then_inc(sem("sw_done"), 1)

            def ffn(L):
                for k in range(2):
                    for half in range(2):
                        sw(L, k, half)
                with pool.Fori(0, TURNS[L]) as j:
                    for k in (2, 3):
                        for half in range(2):
                            sw(L, k, half, j)
                if NT[L] % 2:
                    for half in range(2):
                        sw(L, NT[L] - 1, half)

            inv_sqrt(0)
            wkv()
            fold_lora()
            whole_weights()
            keys_2()
            inv_sqrt(1)
            ffn(0)
            pool.wait_ge(sem("late_in"), 16 * 5)
            inv_sqrt(2)
            link(nc.gpsimd.tensor_copy(a1_mask, mask8[:, :, :]))
            nc.gpsimd.tensor_scalar(a1_neg, a1_mask, -1.0, 1e30, ALU.add, ALU.mult).then_inc(sem("mask"), 1)
            inv_sqrt(3)
            pool.wait_ge(sem("rms_var"), 1)
            nc.gpsimd.tensor_tensor(rms[:, :], veps[:, :], mhalf[:, 0:B], ALU.pow).then_inc(sem("rms"), 1)
            ffn(1)
            inv_sqrt(4)
            pool.wait_ge(sem("q2_ss"), 1)
            nc.gpsimd.tensor_tensor(a2_n[:, 1, :], a2_n[:, 0, :], mhalf[:, :], ALU.pow).then_inc(sem("q2_rms"), 1)
            for b in range(B):
                pool.wait_ge(sem("q2_hi"), b + 1)
                nc.gpsimd.tensor_tensor(a2_st[:, b, :, 3, :], a2_q[:, b, :, :], a2_st[:, b, :, 0, :], ALU.subtract)\
                    .then_inc(sem("q2_lo_pool"), 1)
            inv_sqrt(5)
            ffn(2)
            inv_sqrt(6)
            nc.gpsimd.memset(a3_qp, 0.0).then_inc(sem("qp_zero"), 1)
            inv_sqrt(7)
            ffn(3)

        @block.scalar
        def _(act):
            act.wait_ge(sem("small_in"), 16 * 5)
            nc.scalar.activation(tg[:, :], gates[:, :], ACT.Tanh).then_inc(sem("tg"), 1)
            nc.scalar.activation(wdec[:, :], td[:, :], ACT.Exp).then_inc(sem("decay"), 1)

            def turned(s, dst, scale=None):
                for half in range(2):
                    act.wait_ge(sem("turn"), 2 * turns_before(s) + half + 1)
                    for c in range(KD):
                        src = bank(2 * c + half)
                        o = dst(c, half)
                        if len(o.shape) == 3:
                            src = src.rearrange("p (b s) -> p b s", b=B // 2)
                        nc.scalar.activation(o, src, ACT.Copy, scale=1.0 if scale is None else scale(c))\
                            .then_inc(sem("turned"), 1)

            def xT_of(c, half):
                return xT[:, c, half * HALF:(half + 1) * HALF]

            def seg_of(t):
                return lambda c, half: t[:, c, half * (B // 2):(half + 1) * (B // 2), 1:SEG]

            act.wait_ge(sem("wkv_edges"), 5)
            for half in range(2):
                act.wait_ge(sem("ctxT_turn"), half + 1)
                for c in range(KD):
                    nc.scalar.activation(seg_of(ctxT)(c, half), bank(4 + 2 * c + half).rearrange("p (b s) -> p b s", b=B // 2),
                                         ACT.Copy).then_inc(sem("ctxT_ready"), 1)
            turned(0, seg_of(wk_k))
            for c in range(KD):
                for k, scale in ((0, 1.0), (1, -1.0), (2, 1.0), (3, -1.0)):
                    act.wait_ge(sem("wkv_arg"), 4 * c + k + 1)
                    nc.scalar.activation(wk_e[:, c, k, :], wk_e[:, c, k, :], ACT.Exp, scale=scale)\
                        .then_inc(sem("wkv_exp"), 1)

            for k in range(LORA_T):
                act.wait_ge(sem("fold_mm"), k + 1)
                if k:
                    act.wait_ge(sem("fold_sum"), k)
                nc.scalar.activation(fold_add[:, 0:2 * D], bank(4), ACT.Copy).then_inc(sem("fold_add"), 1)
                nc.scalar.activation(fold_add[:, 2 * D:3 * D], ps[:, 5, 0:D], ACT.Copy).then_inc(sem("fold_add"), 1)
            act.wait_ge(sem("v_ones"), 2)
            act.wait_ge(sem("k3p_zero"), 1)

            def k2_out(b):
                act.wait_ge(sem("k2_turn"), b + 1)
                nc.scalar.activation(k2T[:, b, :, :].rearrange("p g s -> p (g s)"), seq_heads(7), ACT.Copy)\
                    .then_inc(sem("k2_ready"), 1)

            for b in range(B):
                sl = b % 2
                act.wait_ge(sem("kv2_mm"), b + 1)
                if b >= 2:
                    act.wait_ge(sem("k2_split"), b - 1)
                nc.scalar.activation(k_raw[:, sl, :], ps[:, 6, 0:D], ACT.Copy).then_inc(sem("k2_raw"), 1)
                nc.scalar.activation(k_sq[:, sl, :], ps[:, 6, 0:D], ACT.Square).then_inc(sem("k2_raw"), 1)
                nc.scalar.activation(v2[:, b, :, 0:DH2], ps[:, 6, D:2 * D].rearrange("p (h d) -> p h d", d=DH2), ACT.Copy)\
                    .then_inc(sem("v2_out"), 1)
                act.wait_ge(sem("kv3_mm"), b + 1)
                if b >= 1:
                    act.wait_ge(sem("k3_turn"), b)
                nc.scalar.activation(k3p[:, :, 0:DH3], ps[:, 5, 0:D].rearrange("p (h d) -> p h d", d=DH3), ACT.Copy)\
                    .then_inc(sem("k3_raw"), 1)
                nc.scalar.activation(v3[:, b, :, 0:DH3], ps[:, 5, D:2 * D].rearrange("p (h d) -> p h d", d=DH3), ACT.Copy)\
                    .then_inc(sem("v3_out"), 1)
                act.wait_ge(sem("k3_turn"), b + 1)
                nc.scalar.activation(k3T[:, b, :, :].rearrange("p g s -> p (g s)"), bank(4), ACT.Copy).then_inc(sem("k3_ready"), 1)
                if b >= 1:
                    k2_out(b - 1)
            k2_out(B - 1)
            act.wait_ge(sem("wi_turn"), 1)
            nc.scalar.activation(wi[:, :, :, :].rearrange("p a b c -> p (a b c)"), ps[:, 4, :].bitcast(BF16), ACT.Copy)\
                .then_inc(sem("wi"), 1)
            act.wait_ge(sem("wscale_mm"), 1)
            nc.scalar.activation(wscale[:, :, :].rearrange("p a b -> p (a b)"), bank(5), ACT.Copy).then_inc(sem("wi"), 1)

            def router_exp(L):
                n = EXPERTS[L]
                act.wait_ge(sem("router_arg"), min(L, 2) + 1)
                nc.scalar.activation(f_lg[:, :, 0:n], f_lg[:, :, 0:n], ACT.Exp).then_inc(sem("router_exp"), 1)

            def wT_copy(L):
                n = EXPERTS[L]
                act.wait_ge(sem("w_turn"), L + 1)
                dst = m_raw if L == 1 else f_wT
                for h in range(2):
                    nc.scalar.activation(dst[0:n, h * HALF:(h + 1) * HALF], ps[0:n, 5 + h, :], ACT.Copy)\
                        .then_inc(sem("wT_out" if L == 1 else "wT_half"), 1)

            def silu(L, k, half, j=None):
                n = halves(L) + 2 * k + half + 1
                act.wait_ge(sem("gu_done"), at(n, j, 4))
                if tiles(L) + k:
                    act.wait_ge(sem("sw_done"), at(n - 2, j, 4))
                nc.scalar.activation(f_s[:, half, :], bank(half), ACT.Silu).then_inc(sem("silu_done"), 1)

            def silu_star(k, j=None):
                n = k + 1
                act.wait_ge(sem("star_mm"), at(n, j))
                if k >= 1:
                    act.wait_ge(sem("star_done"), at(n - 1, j))
                nc.scalar.activation(m_ss, ps[:, 0, 0:1], ACT.Silu).then_inc(sem("star_silu"), 1)

            def ffn(L):
                for half in range(2):
                    silu(L, 0, half)
                if L != 1:
                    wT_copy(L)
                else:
                    wT_copy(1)
                    for h, bk in ((0, 7), (1, 4)):
                        nc.scalar.activation(m_selT[:, h * HALF:(h + 1) * HALF], ps[0:E1, bk, :], ACT.Copy)\
                            .then_inc(sem("wT_out"), 1)
                    act.wait_ge(sem("last_turn"), 1)
                    nc.scalar.activation(m_last, ps[:, 5, 0:B * E1].rearrange("p (t e) -> p t e", e=E1), ACT.Copy)\
                        .then_inc(sem("last_out"), 1)
                    act.wait_ge(sem("xs_mm"), 1)
                    for c in range(KD):
                        nc.scalar.activation(m_xs[:, c, :], ps[:, 6, c * E1:(c + 1) * E1], ACT.Copy, scale=normw[:, c:c + 1])\
                            .then_inc(sem("xs_out"), 1)
                    silu_star(0)
                silu(L, 1, 0)
                silu(L, 1, 1)
                if L == 1:
                    silu_star(1)
                with act.Fori(0, TURNS[L]) as j:
                    for k in (2, 3):
                        for half in range(2):
                            silu(L, k, half, j)
                        if L == 1:
                            silu_star(k, j)
                if NT[L] % 2:
                    for half in range(2):
                        silu(L, NT[L] - 1, half)

            turned(1, xT_of)
            router_exp(0)
            ffn(0)
            turned(2, xT_of)
            act.wait_ge(sem("a1_arg"), 1)
            nc.scalar.activation(a1_p, a1_p, ACT.Exp).then_inc(sem("a1_p"), 1)
            act.wait_ge(sem("a1_turn"), 1)
            for h in range(2):
                nc.scalar.activation(a1_pT[:, 4 * h:4 * h + 4, :].rearrange("p b s -> p (b s)"), bank(6 + h), ACT.Copy)\
                    .then_inc(sem("a1_pT"), 1)
            turned(3, xT_of, lambda c: normw[:, c:c + 1])
            router_exp(1)
            ffn(1)
            act.wait_ge(sem("r_turn"), 1)
            nc.scalar.activation(m_r, ps[0:E1, 0, 0:D], ACT.Copy).then_inc(sem("r_out"), 1)
            turned(4, xT_of)
            for b in range(4):
                act.wait_ge(sem("q2_mm"), b + 1)
                nc.scalar.activation(a2_q[:, 2 * b:2 * b + 2, :, :].rearrange("p b h d -> p (b h d)"), bank(4 + b), ACT.Square)\
                    .then_inc(sem("q2_sq"), 1)
            for b in range(B):
                act.wait_ge(sem("q2_norm"), b + 1)
                nc.scalar.activation(a2_st[:, b, :, 1, :], a2_q[:, b, :, :], ACT.Copy).then_inc(sem("q2_hi_act"), 1)
            for n in range(4 * B):
                act.wait_ge(sem("s2_mm"), n + 1)
                if n >= 2:
                    act.wait_ge(sem("pv2_job"), n - 1)
                pr = n % 2
                nc.scalar.activation(a2_p[:, n % 2, :, :, :].rearrange("p j g s -> p (j g s)"),
                                     ps[:, 2 * pr:2 * pr + 2, :].rearrange("p j s -> p (j s)"),
                                     ACT.Exp, scale=float(DH2) ** -0.5).then_inc(sem("p2"), 1)
            turned(5, xT_of)
            act.wait_ge(sem("router"), 3)
            act.wait_ge(sem("tinv"), 1)
            nc.scalar.activation(f_lg[:, :, 0:E2], ps[:, 4, 0:B * E2].rearrange("p (t e) -> p t e", e=E2), ACT.Tanh,
                                 scale=tinv[:, 0:1]).then_inc(sem("golden_tanh"), 1)
            act.wait_ge(sem("golden_dist"), 1)
            nc.scalar.activation(f_w[:, :, 0:E2], f_a, ACT.Exp, scale=-1.0 / 0.1).then_inc(sem("golden_exp"), 1)
            nc.scalar.activation(f_b, f_a, ACT.Exp, scale=-1.0 / 0.3).then_inc(sem("golden_exp"), 1)
            ffn(2)
            def whole_turned(k):
                act.wait_ge(sem("xi_turn", k), 1)
                for c in range(KD):
                    nc.scalar.activation(a3_xiT[:, c, :], ps[:, 4 + c, :].bitcast(BF16), ACT.Copy)\
                        .then_inc(sem("xi_turned", k), 1)

            whole_turned(0)

            def q3_copy(b):
                act.wait_ge(sem("q3_turn"), b + 1)
                nc.scalar.activation(a3_qT[:, b % 2, :, :].rearrange("p g s -> p (g s)"), bank(6), ACT.Copy)\
                    .then_inc(sem("q3_ready"), 1)

            q3_copy(0)
            for b in range(B):
                act.wait_ge(sem("p3_arg"), b + 1)
                nc.scalar.activation(a3_p[:, b % 2, :, :], a3_p[:, b % 2, :, :], ACT.Exp, scale=float(DH3) ** -0.5)\
                    .then_inc(sem("p3"), 1)
                if b + 1 < B:
                    q3_copy(b + 1)
                for h in range(2):
                    act.wait_ge(sem("p3_turn"), 2 * b + h + 1)
                    if b >= 1:
                        act.wait_ge(sem("pv3_half"), 2 * b + h - 1)
                    nc.scalar.activation(a3_pT[:, 8 * h:8 * h + 8, :].rearrange("p h s -> p (h s)"),
                                         ps[:, 4:6, :].rearrange("p h s -> p (h s)"), ACT.Copy).then_inc(sem("p3T"), 1)
            whole_turned(1)
            turned(7, xT_of)
            router_exp(3)
            ffn(3)

        @block.tensor
        def _(pe):
            def turn(s, src=xn):
                for t in range(B):
                    pe.wait_ge(sem("xn_ready"), B * s + t + 1)
                    for c in range(KD):
                        last = nc.tensor.transpose(ps[:, 2 * c + t // 4, (t % 4) * S:(t % 4 + 1) * S],
                                                   src[:, t, c * P:(c + 1) * P], ident[:, :])
                    if t % 4 == 3:
                        last.then_inc(sem("turn"), 1)

            def router(L, s):
                n = EXPERTS[L]
                for half in range(2):
                    pe.wait_ge(sem("turned"), 2 * KD * turns_before(s) + KD * (half + 1))
                    for t in range(4 * half, 4 * half + 4):
                        for c in range(KD):
                            last = nc.tensor.matmul(ps[:, 4, t * n:(t + 1) * n], xT[:, c, t * S:(t + 1) * S],
                                                    wr[:, c, ROUTER_AT[L]:ROUTER_AT[L] + n],
                                                    start=(c == 0), stop=(c == KD - 1))
                last.then_inc(sem("router"), 1)

            def turn_w(L):
                n = EXPERTS[L]
                pe.wait_ge(sem("w_ready"), L + 1)
                for t in range(B):
                    last = nc.tensor.transpose(ps[0:n, 5 + t // 4, (t % 4) * S:(t % 4 + 1) * S],
                                               f_w[:, t, 0:n], ident[:, :])
                if L == 1:
                    for t in range(B):
                        last = nc.tensor.transpose(ps[0:n, (7, 4)[t // 4], (t % 4) * S:(t % 4 + 1) * S],
                                                   m_sel[:, t, :], ident[:, :])
                last.then_inc(sem("w_turn"), 1)

            def gate_up(L, k, half, j=None):
                if half == 0:
                    pe.wait_ge(sem("gu_in", k % 2), at(16 * (slot_tiles(L, k % 2) + k // 2 + 1), j, 16))
                if k >= 1:
                    pe.wait_ge(sem("h_done"), at(halves(L) + 2 * k + half - 1, j, 4))
                    if L == 1 and half == 0:
                        pe.wait_ge(sem("star_done"), at(k, j))
                for g in range(2):
                    for c in range(KD):
                        last = nc.tensor.matmul(bank(2 * g + half), W[:, k % 2, g * D + c * P:g * D + (c + 1) * P],
                                                xT[:, c, half * HALF:(half + 1) * HALF],
                                                start=(c == 0), stop=(c == KD - 1))
                last.then_inc(sem("gu_done"), 1)

            def down(L, k, half, j=None, first=False, final=False):
                pe.wait_ge(sem("h_done"), at(halves(L) + 2 * k + half + 1, j, 4))
                if half == 0:
                    pe.wait_ge(sem("down_in", k % 2), at(16 * (slot_tiles(L, k % 2) + k // 2 + 1), j, 16))
                for t in range(4 * half, 4 * half + 4):
                    last = nc.tensor.matmul(ps[:, 4 + t // 2, (t % 2) * D:(t % 2 + 1) * D],
                                            f_h[:, k % 2, t * S:(t + 1) * S], W[:, k % 2, 2 * D:3 * D],
                                            start=(first and t % 2 == 0), stop=final, skip_group_check=True)
                if half == 1:
                    last.then_inc(sem("down_done"), 1)

            def star(k, j=None, own=True, before=True):
                pe.wait_ge(sem("h_done"), at(halves(1) + 2 * k + 1, j, 4))
                if k == 0:
                    pe.wait_ge(sem("xs_out"), KD)
                if before:
                    pe.wait_ge(sem("star_done"), at(k, j))
                e = k if j is None else 2 * j + k
                if own:
                    for g in range(2):
                        for c in range(KD):
                            last = nc.tensor.matmul(ps[:, 2 * g, 0:1], W[:, k % 2, g * D + c * P:g * D + (c + 1) * P],
                                                    m_xs[:, c, bass.ds(e, 1)],
                                                    start=(c == 0), stop=(c == KD - 1))
                if before:
                    for c in range(KD):
                        last = nc.tensor.matmul(ps[:, 2, 2 + c:3 + c], W[:, (k + 1) % 2, 2 * D + c * P:2 * D + (c + 1) * P],
                                                m_hs[:, (k + 1) % 2, :], start=True, stop=True)
                last.then_inc(sem("star_mm"), 1)

            def ffn(L):
                gate_up(L, 0, 0)
                gate_up(L, 0, 1)
                turn_w(L)
                if L == 1:
                    pe.wait_ge(sem("last_ready"), 1)
                    for t in range(B):
                        last = nc.tensor.transpose(ps[:, 5, t * E1:(t + 1) * E1], m_lastT[:, t * S:(t + 1) * S], ident[0:E1, 0:E1])
                    last.then_inc(sem("last_turn"), 1)
                    pe.wait_ge(sem("last_out"), 1)
                    for c in range(KD):
                        for t in range(B):
                            last = nc.tensor.matmul(ps[:, 6, c * E1:(c + 1) * E1], x_rms[:, t, c * P:(c + 1) * P], m_last[:, t, :],
                                                    start=(t == 0), stop=(t == B - 1))
                    last.then_inc(sem("xs_mm"), 1)
                    star(0, before=False)
                else:
                    pe.wait_ge(sem("wT_half"), (2, None, 4, 6)[L])

                def pair(k, j=None, first=False):
                    for half in range(2):
                        gate_up(L, k, half, j)
                        if L == 1 and half == 1:
                            star(k, j, own=(k < E1))
                        down(L, k - 1, half, j, first=first)

                pair(1, first=True)
                with pe.Fori(0, TURNS[L]) as j:
                    pair(2, j)
                    pair(3, j)
                if NT[L] % 2:
                    pair(NT[L] - 1)
                if L == 1:
                    pe.wait_ge(sem("star_done"), E1 + 1)
                    pe.wait_ge(sem("h_done"), halves(2))
                    for c in range(KD):
                        last = nc.tensor.transpose(ps[0:E1, 0, c * P:(c + 1) * P], m_rT[:, c, :], ident[:, :])
                    last.then_inc(sem("r_turn"), 1)
                    pe.wait_ge(sem("r_out"), 1)
                    for t in range(B):
                        nc.tensor.matmul(ps[:, 4 + t // 2, (t % 2) * D:(t % 2 + 1) * D], m_dropT[:, t * S:(t + 1) * S], m_r,
                                         start=False, stop=False, skip_group_check=True)
                for half in range(2):
                    down(L, NT[L] - 1, half, final=True)

            pe.wait_ge(sem("ident"), 3)
            pe.wait_ge(sem("ctx_in"), 16)
            for t in range(B):
                for c in range(KD):
                    last = nc.tensor.transpose(ps[:, 4 + 2 * c + t // 4, (t % 4) * S:(t % 4 + 1) * S],
                                               ctx_sb[:, t, c * P:(c + 1) * P], ident[:, :])
                if t % 4 == 3:
                    last.then_inc(sem("ctxT_turn"), 1)
            turn(0)

            pe.wait_ge(sem("ctxT_ready"), 4)
            for k in range(LORA_T):
                e, f = k // (F2 // P), k % (F2 // P)
                if k:
                    pe.wait_ge(sem("fold_add"), 2 * k)
                pe.wait_ge(sem("lora_in"), 16 * (e + 1))
                for g in range(2):
                    for c in range(KD):
                        nc.tensor.matmul(ps[:, 4, (2 * g + c) * P:(2 * g + c + 1) * P], lora[:, 2 * g, c * P:(c + 1) * P],
                                         lora[:, 2 * g + 1, f * P:(f + 1) * P], start=True, stop=True)
                nc.tensor.matmul(ps[:, 5, 0:D], lora[:, 4, f * P:(f + 1) * P], lora[:, 5, :], start=True, stop=True)\
                    .then_inc(sem("fold_mm"), 1)

            pe.wait_ge(sem("kv_in"), 16 * 3)
            pe.wait_ge(sem("ones"), 1)
            pe.wait_ge(sem("fold_add"), 2 * LORA_T)

            def turn_k2(b):
                pe.wait_ge(sem("k2_split"), b + 1)
                if b:
                    pe.wait_ge(sem("k2_ready"), b)
                for g in range(H2 // 4):
                    last = nc.tensor.transpose(seq_heads(7)[:, g * S:(g + 1) * S],
                                               k_st[:, b % 2, 4 * g:4 * g + 4, :, :].rearrange("p h i d -> p (h i d)"), ident16[:, :])
                last.then_inc(sem("k2_turn"), 1)

            for b in range(B):
                if b:
                    pe.wait_ge(sem("v2_out"), b)
                    pe.wait_ge(sem("k2_raw"), 2 * b)
                for c in range(KD):
                    last = nc.tensor.matmul(bank(6), ctxT[:, c, b, 1:SEG], wkv2[:, c, :], start=(c == 0), stop=(c == KD - 1))
                last.then_inc(sem("kv2_mm"), 1)
                if b:
                    pe.wait_ge(sem("v3_out"), b)
                for c in range(KD):
                    nc.tensor.matmul(bank(5), ctxT[:, c, b, 1:SEG], wkv3[:, c, :], start=(c == 0), stop=False)
                nc.tensor.matmul(bank(5), ones[0:1, :], bkv3[:, :], start=False, stop=True).then_inc(sem("kv3_mm"), 1)
                pe.wait_ge(sem("k3_raw"), b + 1)
                if b:
                    pe.wait_ge(sem("k3_ready"), b)
                for g in range(H3 // 4):
                    last = nc.tensor.transpose(ps[:, 4, g * S:(g + 1) * S],
                                               k3p[:, 4 * g:4 * g + 4, :].rearrange("p h d -> p (h d)"), ident[:, :])
                last.then_inc(sem("k3_turn"), 1)
                if b >= 1:
                    turn_k2(b - 1)
            turn_k2(B - 1)

            pe.wait_ge(sem("wq_whole"), 1)
            pe.wait_ge(sem("k3_ready"), B)
            for w in range(2):
                for c in range(KD):
                    for o in range(KD):
                        k = (w * KD + c) * D + o * P
                        last = nc.tensor.transpose(ps[:, 4, :].bitcast(BF16)[:, k:k + P], wq_i[:, w, o, c * P:(c + 1) * P], identb[:, :])
            last.then_inc(sem("wi_turn"), 1)
            pe.wait_ge(sem("wq_diag"), 1)
            pe.wait_ge(sem("v3_out"), B)
            for k in range(4):
                last = nc.tensor.matmul(ps[:, 5, k * P:(k + 1) * P], ones[:, :], wq_diag[:, k, :], start=True, stop=True)
            last.then_inc(sem("wscale_mm"), 1)

            for c in range(KD):
                pe.wait_ge(sem("wkv_y"), c + 1)
                if c == 0:
                    pe.wait_ge(sem("turned"), 2 * KD)
                for t in range(B):
                    last = nc.tensor.transpose(ps[:, t // 2, (t % 2) * D + c * P:(t % 2) * D + (c + 1) * P],
                                               wk_k[:, c, t, 1:SEG], ident[:, :])
            last.then_inc(sem("wkv_turn"), 1)
            pe.wait_ge(sem("wi"), 2)
            pe.wait_ge(sem("k2_ready"), B)

            pe.wait_ge(sem("late_in"), 16 * 5)
            turn(1)
            router(0, 1)
            ffn(0)
            turn(2)
            pe.wait_ge(sem("turned"), 2 * KD * 3)
            for b in range(B):
                for c in range(KD):
                    last = nc.tensor.matmul(ps[:, 4 + b // 4, (b % 4) * S:(b % 4 + 1) * S], xT[:, c, b * S:(b + 1) * S],
                                            ctxT[:, c, b, 1:SEG], start=(c == 0), stop=(c == KD - 1))
            last.then_inc(sem("a1_mm"), 1)
            pe.wait_ge(sem("a1_p"), 1)
            for b in range(B):
                last = nc.tensor.transpose(ps[:, 6 + b // 4, (b % 4) * S:(b % 4 + 1) * S], a1_p[:, b, :], ident[:, :])
            last.then_inc(sem("a1_turn"), 1)
            pe.wait_ge(sem("a1_pT"), 2)
            for b in range(B):
                last = nc.tensor.matmul(ps[:, b // 2, (b % 2) * D:(b % 2 + 1) * D], a1_pT[:, b, :], ctx_sb[:, b, :],
                                        start=True, stop=True)
            last.then_inc(sem("a1_pv"), 1)
            turn(3, x_rms)
            router(1, 3)
            ffn(1)
            turn(4)
            pe.wait_ge(sem("turned"), 2 * KD * 5)
            for t in range(B):
                for c in range(KD):
                    last = nc.tensor.matmul(ps[:, 4 + t // 2, (t % 2) * D:(t % 2 + 1) * D], xT[:, c, t * S:(t + 1) * S],
                                            wq2[:, c, :], start=(c == 0), stop=(c == KD - 1))
                if t % 2:
                    last.then_inc(sem("q2_mm"), 1)

            def turn_q2(b):
                pe.wait_ge(sem("q2_lo"), b + 1)
                pe.wait_ge(sem("q2_lo_pool"), b + 1)
                pe.wait_ge(sem("q2_hi_act"), b + 1)
                if b == 0:
                    pe.wait_ge(sem("q2_norm"), B)
                if b >= 2:
                    pe.wait_ge(sem("q2T"), b - 1)
                for g in range(H2 // 4):
                    last = nc.tensor.transpose(seq_heads(4 + b % 2)[:, g * S:(g + 1) * S],
                                               a2_st[:, b, 4 * g:4 * g + 4, :, :].rearrange("p h i d -> p (h i d)"), ident16[:, :])
                last.then_inc(sem("q2_turn"), 1)

            def pv2(n):
                b, hg, pr = n // 4, n % 4 // 2, n % 2
                pe.wait_ge(sem("p2"), n + 1)
                if n % 4 == 0 and b >= 2:
                    pe.wait_ge(sem("o2"), b - 1)
                for jj in range(2):
                    for g in range(4):
                        h = 4 * (4 * hg + g) + 2 * pr + jj
                        last = nc.tensor.matmul(ps[:, 6 + b % 2, h * (DH2 + 1):(h + 1) * (DH2 + 1)],
                                                a2_p[:, n % 2, jj, g, :], v2[:, b, h, :], start=True, stop=True)
                last.then_inc(sem("pv2_job"), 1)

            turn_q2(0)
            for n in range(4 * B):
                b, hg, pr = n // 4, n % 4 // 2, n % 2
                if n % 4 == 0:
                    pe.wait_ge(sem("q2T"), b + 1)
                if n >= 2:
                    pe.wait_ge(sem("p2"), n - 1)
                for g in range(4 * hg, 4 * hg + 4):
                    for jj in range(2):
                        i = 2 * pr + jj
                        last = nc.tensor.matmul(ps[:, i, (g % 4) * S:(g % 4 + 1) * S], k2T[32 * i:32 * i + 32, b, g, :],
                                                a2_qT[32 * i:32 * i + 32, b % 2, g, :], start=True, stop=True)
                last.then_inc(sem("s2_mm"), 1)
                if n % 4 == 1 and b + 1 < B:
                    turn_q2(b + 1)
                if n >= 1:
                    pv2(n - 1)
            pv2(4 * B - 1)
            turn(5)
            router(2, 5)
            ffn(2)
            def whole_product(k, first):
                pe.wait_ge(sem("xi", k), 1)
                for c in range(KD):
                    for t in range(B):
                        last = nc.tensor.transpose(ps[:, 4 + c, :].bitcast(BF16)[:, t * S:(t + 1) * S],
                                                   a3_xi[:, t, c * P:(c + 1) * P], identb[:, :])
                last.then_inc(sem("xi_turn", k), 1)
                pe.wait_ge(sem("xi_turned", k), KD)
                for t in range(B):
                    for c in range(KD):
                        last = nc.tensor.matmul(ps[:, t // 2, (t % 2) * D:(t % 2 + 1) * D], a3_xiT[:, c, t * S:(t + 1) * S],
                                                wi[:, k, c, :], start=(c == 0), stop=(c == KD - 1))
                last.then_inc(sem("whole_mm", k), 1)

            whole_product(0, True)

            def turn_q3(b):
                pe.wait_ge(sem("q3p"), b + 1)
                if b:
                    pe.wait_ge(sem("q3_ready"), b)
                for g in range(H3 // 4):
                    last = nc.tensor.transpose(ps[:, 6, g * S:(g + 1) * S],
                                               a3_qp[:, b % 2, 4 * g:4 * g + 4, :].rearrange("p h d -> p (h d)"), ident[:, :])
                last.then_inc(sem("q3_turn"), 1)

            def scores_3(b):
                pe.wait_ge(sem("q3_ready"), b + 1)
                if b:
                    pe.wait_ge(sem("p3_arg"), b)
                else:
                    pe.wait_ge(sem("q3"), 1)
                for g in range(H3 // 4):
                    for i in range(4):
                        last = nc.tensor.matmul(ps[:, i, g * S:(g + 1) * S], a3_qT[32 * i:32 * i + DH3, b % 2, g, :],
                                                k3T[32 * i:32 * i + DH3, b, g, :], start=True, stop=True)
                last.then_inc(sem("s3_mm"), 1)

            def pv3(b):
                pe.wait_ge(sem("p3"), b + 1)
                for h in range(2):
                    n = 2 * b + h
                    if n:
                        pe.wait_ge(sem("p3T"), n)
                    for k in range(8):
                        last = nc.tensor.transpose(ps[:, 4 + k // 4, (k % 4) * S:(k % 4 + 1) * S], a3_p[:, b % 2, 8 * h + k, :], ident[:, :])
                    last.then_inc(sem("p3_turn"), 1)
                for h in range(2):
                    pe.wait_ge(sem("p3T"), 2 * b + h + 1)
                    if b and h == 0:
                        pe.wait_ge(sem("o3"), b)
                    for k in range(8 * h, 8 * h + 8):
                        head = 4 * (k % 4) + k // 4
                        last = nc.tensor.matmul(ps[:, 7, k * (DH3 + 1):(k + 1) * (DH3 + 1)], a3_pT[:, k, :], v3[:, b, head, :],
                                                start=True, stop=True)
                    last.then_inc(sem("pv3_half"), 1)

            turn_q3(0)
            scores_3(0)
            for b in range(B):
                if b + 1 < B:
                    turn_q3(b + 1)
                    scores_3(b + 1)
                pv3(b)
            whole_product(1, False)
            turn(7)
            router(3, 7)
            ffn(3)

        @block.vector
        def _(dve):
            steps = [0]

            def link(ins):
                steps[0] += 1
                ins.then_inc(sem("dve_step"), 1)
                dve.wait_ge(sem("dve_step"), steps[0])

            def layer_norm(s, signal=True):
                for t in range(B):
                    ins = nc.vector.bn_stats(stats[:, t, :], x[:, t, :])
                link(ins)
                for t in range(B):
                    ins = nc.vector.bn_aggr(mv[:, t, :], stats[:, t, :])
                link(ins)
                nc.vector.tensor_scalar(veps[:, :], mv[:, :, 1], LN_EPS, None, ALU.add).then_inc(sem("ln_var"), 1)
                dve.wait_ge(sem("ln_rstd"), s + 1)
                for t in range(B):
                    ins = nc.vector.tensor_scalar(xn[:, t, :], x[:, t, :], mv[:, t, 0:1], rstd[:, t:t + 1],
                                                  ALU.subtract, ALU.mult)
                    if signal:
                        ins.then_inc(sem("xn_ready"), 1)
                if signal:
                    dve.wait_ge(sem("xn_ready"), B * (s + 1))
                else:
                    link(ins)

            def wkv():
                dve.wait_ge(sem("decay"), 1)
                dve.wait_ge(sem("wkv_edges"), 5)
                link(nc.vector.tensor_scalar(wdec[:, :], wdec[:, :], -1.0, None, ALU.mult))
                for c in range(KD):
                    dve.wait_ge(sem("turned"), 2 * KD)
                    k = wk_k[:, c, :, :].rearrange("p b s -> p (b s)")
                    pp = wk_pp[:, 1:LW + 1]
                    before = wk_pp[:, 0:LW]
                    link(nc.vector.tensor_scalar(wk_dec, k, 0.0, wdec[:, c:c + 1], ALU.mult, ALU.add))
                    link(nc.vector.memset(wk_dec.rearrange("p (b s) -> p b s", b=B)[:, :, 0:1], FAR))
                    link(nc.vector.tensor_tensor_scan(pp, wk_dec, k, FAR, ALU.add, ALU.max))
                    nc.vector.scalar_tensor_tensor(wk_d[:, 0, :], before, wdec[:, c:c + 1], k, ALU.add, ALU.subtract)
                    link(nc.vector.scalar_tensor_tensor(wk_d[:, 1, :], k, tf[:, c:c + 1], before, ALU.add, ALU.subtract))
                    for e, (d, op) in enumerate(((0, ALU.min), (0, ALU.max), (1, ALU.min), (1, ALU.max))):
                        nc.vector.tensor_scalar(wk_e[:, c, e, :], wk_d[:, d, :], 0.0, None, op).then_inc(sem("wkv_arg"), 1)
                    dve.wait_ge(sem("wkv_arg"), 4 * c + 4)
                for c in range(KD):
                    dve.wait_ge(sem("wkv_exp"), 4 * c + 4)
                    e1b, e2b, e2, e1 = (wk_e[:, c, k, :] for k in range(4))
                    nc.vector.tensor_tensor_scan(wk_bb[:, 1:LW + 1], e1b, e2b, 0.0, ALU.mult, ALU.add)
                    dve.wait_ge(sem("wkv_ev"), 2 * c + 2)
                    link(nc.vector.tensor_tensor_scan(wk_aa[:, 1:LW + 1], e1b, wk_ev[:, 0, :], 0.0, ALU.mult, ALU.add))
                    nc.vector.tensor_tensor(wk_d[:, 0, :], e1, wk_bb[:, 0:LW], ALU.mult)
                    link(nc.vector.tensor_tensor(wk_d[:, 1, :], e1, wk_aa[:, 0:LW], ALU.mult))
                    nc.vector.tensor_tensor(wk_d[:, 0, :], wk_d[:, 0, :], e2, ALU.add)
                    link(nc.vector.tensor_tensor(wk_d[:, 1, :], wk_d[:, 1, :], wk_ev[:, 1, :], ALU.add))
                    link(nc.vector.reciprocal(wk_d[:, 0, :], wk_d[:, 0, :]))
                    ins = nc.vector.tensor_tensor(wk_k[:, c, :, :].rearrange("p b s -> p (b s)"), wk_d[:, 0, :], wk_d[:, 1, :], ALU.mult)
                    ins.then_inc(sem("wkv_y"), 1)
                    dve.wait_ge(sem("wkv_y"), c + 1)
                dve.wait_ge(sem("tg"), 1)
                dve.wait_ge(sem("wkv_turn"), 1)
                add_banks(0, 0)

            def add_banks(first, gate):
                for b in range(4):
                    xs = x[:, 2 * b:2 * b + 2, :].rearrange("p t d -> p (t d)")
                    ins = nc.vector.scalar_tensor_tensor(xs, ps[:, first + b, :], tg[:, gate:gate + 1], xs, ALU.mult, ALU.add)
                link(ins)

            def weight_scales():
                dve.wait_ge(sem("wqp_in"), 16)
                link(nc.vector.tensor_reduce(wq_s[:, 0, :], wq_f.rearrange("p w o d -> p (w o) d"), AX.X, ALU.max,
                                             apply_absolute_value=True))
                link(nc.vector.tensor_scalar(wq_s[:, 1, :], wq_s[:, 0, :], 1.0 / 127.0, 1e-8, ALU.mult, ALU.max))
                nc.vector.reciprocal(wq_s[:, 2, :], wq_s[:, 1, :]).then_inc(sem("wq_scale"), 1)
                link(nc.vector.reciprocal(tinv[:, :], tinv[:, :]))
                nc.vector.tensor_scalar(tinv[:, :], tinv[:, :], 0.5, None, ALU.mult).then_inc(sem("tinv"), 1)

            def spread(v, n):
                return v.unsqueeze(2).to_broadcast((P, B, n))

            def softmax(L):
                n = EXPERTS[L]
                lg = f_lg[:, :, 0:n]
                mx, sm, rc = f_s8[:, 0, :], f_s8[:, 1, :], f_s8[:, 2, :]
                dve.wait_ge(sem("router"), L + 1)
                scores = ps[:, 4, 0:B * n].rearrange("p (t e) -> p t e", e=n)
                link(nc.vector.tensor_reduce(mx, scores, AX.X, ALU.max))
                nc.vector.tensor_tensor(lg, scores, spread(mx, n), ALU.subtract).then_inc(sem("router_arg"), 1)
                dve.wait_ge(sem("router_exp"), min(L, 2) + 1)
                link(nc.vector.tensor_reduce(sm, lg, AX.X, ALU.add))
                link(nc.vector.reciprocal(rc, sm))
                link(nc.vector.tensor_tensor(f_w[:, :, 0:n], lg, spread(rc, n), ALU.mult))

            def before(v):
                ve = v.unsqueeze(3).to_broadcast((P, B, E0, E0))
                vj = v.unsqueeze(2).to_broadcast((P, B, E0, E0))
                nc.vector.tensor_tensor(f_cmp, vj, ve, ALU.is_gt)
                link(nc.vector.tensor_tensor(f_eq, vj, ve, ALU.is_equal))
                link(nc.vector.tensor_tensor(f_eq, f_eq, f_tri.unsqueeze(1).to_broadcast((P, B, E0, E0)), ALU.mult))
                link(nc.vector.tensor_tensor(f_cmp, f_cmp, f_eq, ALU.add))

            def make_tri():
                link(nc.vector.memset(f_tri, 0.0))
                for e in range(1, E0):
                    ins = nc.vector.memset(f_tri[:, e, 0:e], 1.0)
                link(ins)

            def hidden(L, k, half, j=None):
                n = halves(L) + 2 * k + half + 1
                dve.wait_ge(sem("sw_done"), at(n, j, 4))
                dve.wait_ge(sem("gu_done"), at(n, j, 4))
                if k >= 2 and half == 0:
                    dve.wait_ge(sem("down_done"), at(tiles(L) + k - 1, j))
                nc.vector.tensor_tensor(f_h[:, k % 2, half * HALF:(half + 1) * HALF], bank(2 + half),
                                        f_sw[:, half, :], ALU.mult).then_inc(sem("h_done"), 1)

            def star(k, j=None, own=True, before=True):
                n = k + 1
                dve.wait_ge(sem("star_mm"), at(n, j))
                if before:
                    e = k - 1 if j is None else 2 * j + (k - 1)
                    ins = nc.vector.tensor_copy(m_rT[:, :, bass.ds(e, 1)], ps[:, 2, 2:4].unsqueeze(2))
                if own:
                    dve.wait_ge(sem("star_silu"), at(n, j))
                    ins = nc.vector.tensor_tensor(m_hs[:, k % 2, :], ps[:, 2, 0:1], m_ss, ALU.mult)
                ins.then_inc(sem("star_done"), 1)

            def ffn(L):
                if L == 1:
                    hidden(1, 0, 0)
                    star(0, before=False)
                    hidden(1, 0, 1)
                    hidden(1, 1, 0)
                    star(1)
                    hidden(1, 1, 1)
                else:
                    for k in range(2):
                        for half in range(2):
                            hidden(L, k, half)
                with dve.Fori(0, TURNS[L]) as j:
                    for k in (2, 3):
                        hidden(L, k, 0, j)
                        if L == 1:
                            star(k, j)
                        hidden(L, k, 1, j)
                if NT[L] % 2:
                    hidden(L, NT[L] - 1, 0)
                    star(NT[L] - 1, own=False)
                    hidden(L, NT[L] - 1, 1)
                dve.wait_ge(sem("down_done"), tiles(L + 1))
                add_banks(4, 4 + L)

            dve.wait_ge(sem("x_in"), 16)
            layer_norm(0)
            weight_scales()
            wkv()
            layer_norm(1)
            make_tri()
            softmax(0)
            before(f_w[:, :, 0:E0])
            link(nc.vector.tensor_reduce(f_rk, f_cmp, AX.X, ALU.add))
            nc.vector.scalar_tensor_tensor(f_w[:, :, 0:E0], f_rk, TOP0 - 0.5, f_w[:, :, 0:E0], ALU.is_lt, ALU.mult)\
                .then_inc(sem("w_ready"), 1)
            ffn(0)
            layer_norm(2)
            dve.wait_ge(sem("mask"), 1)
            link(nc.vector.tensor_reduce(a1_s[:, 0, :], a1_mask, AX.X, ALU.max))
            dve.wait_ge(sem("a1_mm"), 1)
            flat = a1_p.rearrange("p b s -> p (b s)")
            link(nc.vector.scalar_tensor_tensor(flat, ps[:, 4:6, :].rearrange("p h s -> p (h s)"), float(D) ** -0.5,
                                                a1_mask.rearrange("p b s -> p (b s)"), ALU.mult, ALU.mult))
            link(nc.vector.tensor_tensor(a1_p, a1_p, a1_neg, ALU.add))
            link(nc.vector.tensor_reduce(a1_s[:, 1, :], a1_p, AX.X, ALU.max))
            nc.vector.tensor_tensor(a1_p, a1_p, spread(a1_s[:, 1, :], S), ALU.subtract).then_inc(sem("a1_arg"), 1)
            dve.wait_ge(sem("a1_p"), 1)
            link(nc.vector.tensor_reduce(a1_s[:, 2, :], a1_p, AX.X, ALU.add))
            link(nc.vector.reciprocal(a1_s[:, 3, :], a1_s[:, 2, :]))
            link(nc.vector.scalar_tensor_tensor(a1_s[:, 4, :], a1_s[:, 3, :], tg[:, 1:2], a1_s[:, 0, :], ALU.mult, ALU.mult))
            dve.wait_ge(sem("a1_pv"), 1)
            for b in range(B):
                ins = nc.vector.scalar_tensor_tensor(x[:, b, :], ps[:, b // 2, (b % 2) * D:(b % 2 + 1) * D],
                                                     a1_s[:, 4, b:b + 1], x[:, b, :], ALU.mult, ALU.add)
            link(ins)
            layer_norm(3, signal=False)
            link(nc.vector.tensor_tensor(rms[:, :], mv[:, :, 1], rstd[:, :], ALU.mult))
            link(nc.vector.tensor_tensor(rms[:, :], rms[:, :], rstd[:, :], ALU.mult))
            nc.vector.tensor_scalar(veps[:, :], rms[:, :], RMS_EPS, None, ALU.add).then_inc(sem("rms_var"), 1)
            flat = x[:, :, :].rearrange("p t d -> p (t d)")
            link(nc.vector.scalar_tensor_tensor(flat, xn[:, :, :].rearrange("p t d -> p (t d)"), tg[:, 5:6], flat, ALU.mult, ALU.add))
            dve.wait_ge(sem("rms"), 1)
            for t in range(B):
                nc.vector.tensor_scalar(x_rms[:, t, :], xn[:, t, :], rms[:, t:t + 1], None, ALU.mult)\
                    .then_inc(sem("xn_ready"), 1)
            nc.vector.memset(m_zero, 0.0)
            nc.vector.memset(m_x[:, :, E1:E1 + 8], -1.0)
            softmax(1)
            nc.vector.tensor_copy(m_x[:, :, 0:E1], f_w)
            for t in range(B):
                ins = nc.vector.max(m_top[:, t, :], f_w[:, t, :])
            link(ins)
            link(nc.vector.memset(m_top[:, :, TOP1:8], -1.0))
            for t in range(B):
                ins = nc.vector.match_replace(m_rep[:, t, :], m_top[:, t, :], m_x[:, t, :], -2.0)
            link(ins)
            link(nc.vector.tensor_scalar(m_sel, m_rep[:, :, 0:E1], -2.0, None, ALU.is_equal))
            link(nc.vector.tensor_tensor(f_w, f_w, m_sel, ALU.mult))
            link(nc.vector.tensor_reduce(f_s8[:, 3, :], f_w, AX.X, ALU.add))
            link(nc.vector.reciprocal(f_s8[:, 4, :], f_s8[:, 3, :]))
            nc.vector.tensor_tensor(f_w, f_w, spread(f_s8[:, 4, :], E1), ALU.mult).then_inc(sem("w_ready"), 1)
            dve.wait_ge(sem("wT_out"), 4)
            link(nc.vector.tensor_tensor_scan(m_cum, m_selT, m_zero, 0.0, ALU.add, ALU.add))
            nc.vector.scalar_tensor_tensor(f_wT, m_cum, float(CAPACITY), m_raw, ALU.is_le, ALU.mult)\
                .then_inc(sem("wT_ready", 1), 1)
            nc.vector.scalar_tensor_tensor(m_dropT, m_cum, float(CAPACITY), m_raw, ALU.is_gt, ALU.mult)\
                .then_inc(sem("drop_ready"), 1)
            nc.vector.scalar_tensor_tensor(m_lastT, m_cum, float(CAPACITY), m_selT, ALU.is_equal, ALU.mult)\
                .then_inc(sem("last_ready"), 1)
            ffn(1)
            layer_norm(4)
            groups = a2_q.rearrange("p b h d -> p (b h) d")
            dve.wait_ge(sem("q2_sq"), 4)
            link(nc.vector.tensor_reduce(a2_n[:, 0, :], groups, AX.X, ALU.add))
            nc.vector.tensor_scalar(a2_n[:, 0, :], a2_n[:, 0, :], 1.0 / DH2, RMS_EPS, ALU.mult, ALU.add).then_inc(sem("q2_ss"), 1)
            dve.wait_ge(sem("q2_rms"), 1)
            for b in range(B):
                nc.vector.tensor_tensor(a2_q[:, b, :, :], ps[:, 4 + b // 2, (b % 2) * D:(b % 2 + 1) * D].rearrange("p (h d) -> p h d", d=DH2),
                                        a2_n[:, 1, b * H2:(b + 1) * H2].unsqueeze(2).to_broadcast((P, H2, DH2)), ALU.mult)\
                    .then_inc(sem("q2_norm"), 1)
                dve.wait_ge(sem("q2_norm"), b + 1)
                nc.vector.tensor_copy(a2_st[:, b, :, 0, :], a2_q[:, b, :, :]).then_inc(sem("q2_hi"), 1)
                dve.wait_ge(sem("q2_hi"), b + 1)
                nc.vector.tensor_tensor(a2_st[:, b, :, 2, :], a2_q[:, b, :, :], a2_st[:, b, :, 0, :], ALU.subtract)\
                    .then_inc(sem("q2_lo"), 1)

            def q2T(b):
                dve.wait_ge(sem("q2_turn"), b + 1)
                if b >= 2:
                    dve.wait_ge(sem("s2_mm"), 4 * (b - 1))
                nc.vector.tensor_copy(a2_qT[:, b % 2, :, :].rearrange("p g s -> p (g s)"), seq_heads(4 + b % 2)).then_inc(sem("q2T"), 1)

            q2T(0)
            for b in range(B):
                if b + 1 < B:
                    q2T(b + 1)
                dve.wait_ge(sem("pv2_job"), 4 * (b + 1))
                pv = ps[:, 6 + b % 2, 0:H2 * (DH2 + 1)].rearrange("p (h d) -> p h d", d=DH2 + 1)
                link(nc.vector.reciprocal(a2_rc.unsqueeze(2), pv[:, :, DH2:DH2 + 1]))
                ins = nc.vector.tensor_tensor(a2_o, pv[:, :, 0:DH2], a2_rc.unsqueeze(2).to_broadcast((P, H2, DH2)), ALU.mult)
                ins.then_inc(sem("o2"), 1)
                dve.wait_ge(sem("o2"), b + 1)
                link(nc.vector.scalar_tensor_tensor(x[:, b, :], a2_o.rearrange("p h d -> p (h d)"), tg[:, 2:3], x[:, b, :],
                                                    ALU.mult, ALU.add))
            layer_norm(5)
            make_tri()
            w, lg, dist, fb = f_w[:, :, 0:E2], f_lg[:, :, 0:E2], f_a, f_b
            zone = f_rk
            dve.wait_ge(sem("golden_tanh"), 1)
            link(nc.vector.tensor_scalar(lg, lg, 0.5, 0.5, ALU.mult, ALU.add))
            link(nc.vector.tensor_scalar(zone, lg, GOLDEN_LOWER, None, ALU.is_ge))
            link(nc.vector.scalar_tensor_tensor(zone, lg, GOLDEN_UPPER, zone, ALU.is_le, ALU.mult))
            link(nc.vector.tensor_scalar(dist, lg, GOLDEN_CENTER, None, ALU.subtract))
            link(nc.vector.tensor_scalar(lg, dist, -1.0, None, ALU.mult))
            nc.vector.tensor_tensor(dist, dist, lg, ALU.max).then_inc(sem("golden_dist"), 1)
            dve.wait_ge(sem("golden_exp"), 2)
            link(nc.vector.tensor_tensor(w, w, zone, ALU.mult))
            link(nc.vector.tensor_reduce(f_s8[:, 0, :], w, AX.X, ALU.add))
            link(nc.vector.tensor_scalar(f_s8[:, 1, :], f_s8[:, 0, :], 1e-8, None, ALU.is_lt))
            link(nc.vector.tensor_scalar(f_s8[:, 2, :], f_s8[:, 0, :], 1e-8, None, ALU.is_ge))
            before(fb)
            link(nc.vector.tensor_reduce(zone, f_cmp, AX.X, ALU.add))
            link(nc.vector.scalar_tensor_tensor(fb, zone, 1.5, fb, ALU.is_lt, ALU.mult))
            link(nc.vector.tensor_reduce(f_s8[:, 3, :], fb, AX.X, ALU.add))
            link(nc.vector.tensor_scalar(f_s8[:, 3, :], f_s8[:, 3, :], 1e-8, None, ALU.max))
            link(nc.vector.reciprocal(f_s8[:, 4, :], f_s8[:, 3, :]))
            link(nc.vector.tensor_tensor(f_s8[:, 4, :], f_s8[:, 4, :], f_s8[:, 1, :], ALU.mult))
            nc.vector.tensor_tensor(fb, fb, spread(f_s8[:, 4, :], E2), ALU.mult)
            link(nc.vector.tensor_tensor(w, w, spread(f_s8[:, 2, :], E2), ALU.mult))
            link(nc.vector.tensor_tensor(w, w, fb, ALU.add))
            link(nc.vector.tensor_reduce(f_s8[:, 0, :], w, AX.X, ALU.add))
            link(nc.vector.tensor_scalar(f_s8[:, 0, :], f_s8[:, 0, :], 1e-8, None, ALU.max))
            link(nc.vector.reciprocal(f_s8[:, 1, :], f_s8[:, 0, :]))
            nc.vector.tensor_tensor(w, w, spread(f_s8[:, 1, :], E2), ALU.mult).then_inc(sem("w_ready"), 1)
            ffn(2)
            def whole(src, k):
                amax, scale, inv = (a3_s[:, k, i, :] for i in range(3))
                link(nc.vector.tensor_reduce(amax, src, AX.X, ALU.max, apply_absolute_value=True))
                link(nc.vector.tensor_scalar(scale, amax, 1.0 / 127.0, 1e-8, ALU.mult, ALU.max))
                link(nc.vector.reciprocal(inv, scale))
                for t in range(B):
                    ins = nc.vector.tensor_scalar(a3_y[:, t, :], src[:, t, :], inv[:, t:t + 1], ROUND, ALU.mult, ALU.add)
                link(ins)
                link(nc.vector.tensor_scalar(a3_y, a3_y, ROUND, 127.0, ALU.subtract, ALU.min))
                nc.vector.tensor_scalar(a3_xi, a3_y, -127.0, None, ALU.max).then_inc(sem("xi", k), 1)
                dve.wait_ge(sem("xi", k), 1)

            def whole_out(k):
                dve.wait_ge(sem("whole_mm", k), 1)
                for t in range(B):
                    ins = nc.vector.scalar_tensor_tensor(a3_y[:, t, :], ps[:, t // 2, (t % 2) * D:(t % 2 + 1) * D],
                                                         a3_s[:, k, 1, t:t + 1], wscale[:, k, :], ALU.mult, ALU.mult)
                return ins

            layer_norm(6)
            whole(xn[:, :, :], 0)
            whole_out(0).then_inc(sem("q3"), 1)
            dve.wait_ge(sem("q3"), 1)
            dve.wait_ge(sem("qp_zero"), 1)

            def q3p(b):
                if b >= 2:
                    dve.wait_ge(sem("q3_turn"), b - 1)
                nc.vector.tensor_tensor(a3_qp[:, b % 2, :, 0:DH3], a3_y[:, b, :].rearrange("p (h d) -> p h d", d=DH3),
                                        bq3[:, :].rearrange("p (h d) -> p h d", d=DH3), ALU.add).then_inc(sem("q3p"), 1)

            q3p(0)
            for b in range(B):
                if b + 1 < B:
                    q3p(b + 1)
                dve.wait_ge(sem("s3_mm"), b + 1)
                scores = ps[:, 0:4, :].rearrange("p i (g s) -> p (i g) s", s=S)
                link(nc.vector.tensor_reduce(a3_mx, scores, AX.X, ALU.max))
                if b >= 2:
                    dve.wait_ge(sem("p3_turn"), 2 * (b - 1))
                nc.vector.tensor_tensor(a3_p[:, b % 2, :, :], scores, a3_mx.unsqueeze(2).to_broadcast((P, H3, S)), ALU.subtract)\
                    .then_inc(sem("p3_arg"), 1)

                def out_3(b):
                    dve.wait_ge(sem("pv3_half"), 2 * (b + 1))
                    pv = ps[:, 7, 0:H3 * (DH3 + 1)].rearrange("p (h d) -> p h d", d=DH3 + 1)
                    link(nc.vector.reciprocal(a3_rc.unsqueeze(2), pv[:, :, DH3:DH3 + 1]))
                    for i in range(4):
                        ins = nc.vector.tensor_tensor(a3_o[:, b, :].rearrange("p (g i d) -> p i g d", i=4, d=DH3)[:, i, :, :],
                                                      pv[:, 4 * i:4 * i + 4, 0:DH3],
                                                      a3_rc[:, 4 * i:4 * i + 4].unsqueeze(2).to_broadcast((P, 4, DH3)), ALU.mult)
                    ins.then_inc(sem("o3"), 1)

                if b >= 1:
                    out_3(b - 1)
            out_3(B - 1)
            dve.wait_ge(sem("o3"), B)
            whole(a3_o, 1)
            link(whole_out(1))
            link(nc.vector.tensor_tensor(a3_y, a3_y, bp3[:, :].unsqueeze(1).to_broadcast((P, B, D)), ALU.add))
            flat = x[:, :, :].rearrange("p t d -> p (t d)")
            link(nc.vector.scalar_tensor_tensor(flat, a3_y.rearrange("p t d -> p (t d)"), tg[:, 3:4], flat, ALU.mult, ALU.add))
            layer_norm(7)
            make_tri()
            softmax(3)
            before(f_w[:, :, 0:E3])
            link(nc.vector.tensor_tensor(f_eq, f_cmp, f_w[:, :, 0:E3].unsqueeze(2).to_broadcast((P, B, E3, E3)), ALU.mult))
            link(nc.vector.tensor_reduce(f_rk, f_eq, AX.X, ALU.add))
            nc.vector.scalar_tensor_tensor(f_w[:, :, 0:E3], f_rk, TOP_P, f_w[:, :, 0:E3], ALU.is_le, ALU.mult)\
                .then_inc(sem("w_ready"), 1)
            ffn(3)
            nc.vector.tensor_copy(x[:, 0, 0:1], x[:, 0, 0:1]).then_inc(sem("x_done"), 1)


PIECES = []
for _i in range(NT0):
    _cuts = [e * F0 for e in range(E0 + 1) if _i * P < e * F0 < (_i + 1) * P] or [_i * P + P // 2]
    PIECES.append([(lo - _i * P, hi - _i * P, min(lo // F0, E0))
                   for lo, hi in ((_i * P, _cuts[0]), (_cuts[0], (_i + 1) * P))])


def pack_tiles(gate, up, down):
    f, d = gate.shape
    n = -(-f // P)

    def pad(m):
        return np.concatenate([m, np.zeros((n * P - f, d), m.dtype)])

    first = [pad(m).reshape(n, P, KD, P).transpose(0, 3, 2, 1).reshape(n, P, D) for m in (gate, up)]
    return np.ascontiguousarray(np.concatenate(first + [pad(down).reshape(n, P, D)], axis=2))


def feature_rows(m):
    return np.ascontiguousarray(m.reshape(KD, P, -1).transpose(1, 0, 2))


def by_feature(m):
    return m.transpose(0, 2, 1).reshape(-1, D)


def lay_out(inputs):
    i = {k: np.asarray(v) for k, v in inputs.items()}
    g = {"x": i["x"], "ctx": i["ctx_2048"], "mask": i["mask_BxS2_bk0"]}
    g["time_decay"] = np.ascontiguousarray(i["L0_xattn_time_decay"].reshape(KD, P).T)
    g["time_first"] = np.ascontiguousarray(i["L0_xattn_time_first"].reshape(KD, P).T)
    g["norm_w"] = np.ascontiguousarray(i["L1_ffn_norm_w"].reshape(KD, P).T)
    g["gates"] = np.concatenate([i["g_xattn"], i["g_ffn"]])
    g["temperature"] = i["L2_ffn_temperature"]
    g["wr"] = feature_rows(np.concatenate([i["L0_ffn_Wr"].T, i["L1_ffn_gate_w"].T, i["L2_ffn_Wr"],
                                           i["L3_ffn_router_w"].T], axis=1))
    g["w0"] = pack_tiles(np.concatenate([i["L0_ffn_Wg"].reshape(-1, D), i["L0_ffn_Wsg"]]),
                         np.concatenate([i["L0_ffn_Wu"].reshape(-1, D), i["L0_ffn_Wsu"]]),
                         np.concatenate([by_feature(i["L0_ffn_Wd"]), i["L0_ffn_Wsd"].T]))
    w13 = i["L1_ffn_w13"]
    g["w1"] = pack_tiles(np.concatenate([by_feature(w13[:, :, :F1]), i["L1_ffn_shared_gate_w"].T]),
                         np.concatenate([by_feature(w13[:, :, F1:]), i["L1_ffn_shared_up_w"].T]),
                         np.concatenate([i["L1_ffn_w2"].reshape(-1, D), i["L1_ffn_shared_down_w"]]))
    g["w2"] = pack_tiles(by_feature(i["L2_ffn_Wg"]), by_feature(i["L2_ffn_Wu"]), i["L2_ffn_Wd"].reshape(-1, D))
    g["w3"] = pack_tiles(i["L3_ffn_gate_w"].reshape(-1, D), i["L3_ffn_up_w"].reshape(-1, D), by_feature(i["L3_ffn_down_w"]))
    g["lora"] = np.ascontiguousarray(np.stack(
        [i["L2_ffn_Ga"].transpose(0, 2, 1), i["L2_ffn_Gb"], i["L2_ffn_Ua"].transpose(0, 2, 1), i["L2_ffn_Ub"],
         i["L2_ffn_Da"].transpose(0, 2, 1), i["L2_ffn_Db"]]).transpose(2, 1, 0, 3))
    g["wq2"] = feature_rows(i["L2_xattn_Wq"].T)
    both = np.concatenate([i["L2_xattn_Wk"], i["L2_xattn_Wv"]])
    g["wkv2"] = feature_rows(np.concatenate([both[0::2], both[1::2]]).T)
    g["wkv3"] = feature_rows(i["L3_xattn_wkv"].T)
    g["bkv3"] = i["L3_xattn_bkv"].reshape(1, -1)
    g["bq3"] = i["L3_xattn_bq"]
    g["bp3"] = i["L3_xattn_bp"]
    g["wqp3"] = np.ascontiguousarray(np.stack([i["L3_xattn_wq"], i["L3_xattn_wp"]]).reshape(2, KD, P, D).transpose(2, 0, 1, 3))
    return g


def kernel(**inputs):
    import concourse.bacc as _bacc
    from concourse.bass_utils import run_bass_kernel_spmd as _run

    nc = _bacc.Bacc("TRN2", target_bir_lowering=False, num_devices=1)
    arrays, aps = {}, {}
    for name, v in lay_out(inputs).items():
        arrays[f"in_{name}"] = v
        dt = U8 if v.dtype == np.bool_ else mybir.dt.from_np(v.dtype)
        aps[name] = nc.dram_tensor(f"in_{name}", v.shape, dt, kind="ExternalInput").ap()
    result = nc.dram_tensor("out_x", (B, S, D), F32, kind="ExternalOutput").ap()
    build(nc, aps, result)
    r = _run(nc, [arrays], core_ids=[0])
    return r.results[0]["out_x"]
```

```python
from contextlib import ExitStack

import numpy as np

import concourse.bass as bass
from concourse import mybir
from concourse.alu_op_type import AluOpType as ALU


F32 = mybir.dt.float32
F16 = mybir.dt.float16
BF16 = mybir.dt.bfloat16
U8 = mybir.dt.uint8
ACT = mybir.ActivationFunctionType
AX = mybir.AxisListType

P = 128
B, S, D = 8, 128, 256
T = B * S
KD = D // P
HALF = T // 2
SEG = S + 1
LN_EPS = 1e-5
RMS_EPS = 1e-6
FAR = -1e38

E0, F0, FS0 = 8, 176, 352
E1, F1 = 32, 128
E2, F2 = 8, 256
E3, F3 = 8, 512
NT0 = -(-(E0 * F0 + FS0) // P)
NT1 = E1 * F1 // P + 1
NT2 = E2 * F2 // P
NT3 = E3 * F3 // P
NT = (NT0, NT1, NT2, NT3)
EXPERTS = (E0, E1, E2, E3)
ROUTER_AT = (0, E0, E0 + E1, E0 + E1 + E2)
ROUTERS = E0 + E1 + E2 + E3
TOP0, TOP1 = 2, 4
CAPACITY = 2 * T * TOP1 // E1
WSCALE = 64.0
WROW = 3 * D
LORA_E, LORA_R = 2, 64
GOLDEN_CENTER = float(1.0 / np.e)
GOLDEN_LOWER = float(0.5 - np.log(4.0 / 3.0))
GOLDEN_UPPER = 0.5
TOP_P = 0.9
H2, DH2 = 32, 8
H3, DH3 = 16, 16
ROUND = 1.5 * 2.0 ** 23


def build(nc, a, out):
    with ExitStack() as ctx:
        def sb(name, shape, dt=F32):
            return ctx.enter_context(nc.sbuf_tensor(name, shape, dt))

        sems = {}

        def sem(name, k=None):
            key = name if k is None else f"{name}_{k}"
            if key not in sems:
                sems[key] = ctx.enter_context(nc.semaphore(key))
            return sems[key]

        ps = ctx.enter_context(nc.psum_tensor("ps", [P, 8, 512], F32))
        x = sb("x", [P, B, D])
        xn = sb("xn", [P, B, D])
        turned_buf = sb("turned_buf", [P, KD * B * SEG])
        xT = turned_buf[:, 0:KD * T].rearrange("p (c t) -> p c t", c=KD)
        x16 = turned_buf[:, 0:KD * T].bitcast(F16).rearrange("p (i c t) -> p i c t", i=2, c=KD)
        wk_k = turned_buf[:, :].rearrange("p (c b s) -> p c b s", c=KD, b=B)
        ctx_sb = sb("ctx_sb", [P, B, D])
        ctxT = sb("ctxT", [P, KD, B, SEG])
        ident = sb("ident", [P, P])
        ident16 = sb("ident16", [P, P], F16)
        identb = sb("identb", [P, P], BF16)
        gates = sb("gates", [P, 8])
        tg = sb("tg", [P, 8])
        tg_ffn = sb("tg_ffn", [P, 8])
        wr = sb("wr", [P, KD, ROUTERS])
        wr16 = sb("wr16", [P, 2, KD, ROUTERS], F16)
        normw = sb("normw", [P, KD])
        stats = sb("stats", [P, B, 6])
        mv = sb("mv", [P, B, 2])
        veps = sb("veps", [P, B])
        rstd = sb("rstd", [P, B])
        rms = sb("rms", [P, B])
        mhalf = sb("mhalf", [P, B])
        ones = sb("ones", [P, P])
        W = sb("W", [P, 2, WROW])
        W16 = sb("W16", [P, 2, 2, WROW], F16)
        wb = sb("wb", [P, 2, T])
        td = sb("td", [P, KD])
        tf = sb("tf", [P, KD])
        wdec = sb("wdec", [P, KD])
        tinv = sb("tinv", [P, 1])
        mask8 = sb("mask8", [P, B, S], U8)
        k2T = sb("k2T", [P, B, H2 // 4, S], F16)
        v2 = sb("v2", [P, B, H2, DH2 + 1])
        k3T = sb("k3T", [P, B, H3 // 4, S])
        v3 = sb("v3", [P, B, H3, DH3 + 1])
        wq2 = sb("wq2", [P, KD, D])
        wkv2 = sb("wkv2", [P, KD, 2 * D])
        wkv3 = sb("wkv3", [P, KD, 2 * D])
        bkv3 = sb("bkv3", [1, 2 * D])
        bq3 = sb("bq3", [P, D])
        bp3 = sb("bp3", [P, D])
        wi = sb("wi", [P, 2, KD, D], BF16)
        wscale = sb("wscale", [P, 2, D])
        k_raw = sb("k_raw", [P, 2, D])
        k_sq = sb("k_sq", [P, 2, D])
        k_norm = sb("k_norm", [P, 4, H2])
        k_st = sb("k_st", [P, 2, H2, 4, DH2], F16)
        k3p = sb("k3p", [P, H3, 32])
        ARENA = 16520
        arena = sb("arena", [P, ARENA])

        class Arena:
            def __init__(self):
                self.at = 0

            def take(self, shape, dt=F32, rows=P):
                n = 1
                for k in shape:
                    n *= k
                words = n if dt == F32 else (n + 1) // 2
                v = arena[0:rows, self.at:self.at + words]
                self.at += words
                assert self.at <= ARENA, self.at
                if dt != F32:
                    v = v.bitcast(dt)
                if len(shape) > 1:
                    names = "abcdef"[:len(shape)]
                    v = v.rearrange(f"p ({' '.join(names)}) -> p {' '.join(names)}",
                                    **{c: k for c, k in zip(names[1:], shape[1:])})
                return v

        routed = [nc.dram_tensor(f"routed_{L}", (EXPERTS[L] + 1, T), F32, kind="Internal").ap() for L in range(4)]
        LORA_T = LORA_E * F2 // P
        folded = nc.dram_tensor("folded", (LORA_T, P, WROW), F32, kind="Internal").ap()

        ar = Arena()
        LW = B * SEG
        wk_dec = ar.take([LW])
        wk_pp = ar.take([LW + 1])
        wk_aa = ar.take([LW + 1])
        wk_bb = ar.take([LW + 1])
        wk_d = ar.take([2, LW])
        wk_e = ar.take([KD, 4, LW])
        wk_ev = ar.take([2, LW])
        lora = W16[0:LORA_R, :, :, :].rearrange("p a b c -> p (a b c)").bitcast(F32)\
            .rearrange("p (k d) -> p k d", d=D)
        fold = W[:, 0, :]
        fold_add = W[:, 1, :]
        wq_s = sb("wq_s", [P, 3, 4])
        wq_f = wb[:, 0, :].rearrange("p (w o d) -> p w o d", w=2, o=KD)
        wq_i = wb[:, 1, 0:HALF].bitcast(BF16).rearrange("p (w o d) -> p w o d", w=2, o=KD)
        wq_diag = wb[:, 1, HALF:T].rearrange("p (k o) -> p k o", k=4)

        ar = Arena()
        a1_mask = ar.take([B, S])
        a1_neg = ar.take([B, S])
        a1_p = ar.take([B, S])
        a1_pT = ar.take([B, S])
        a1_s = ar.take([6, B])

        ar = Arena()
        f_s = ar.take([2, HALF])
        f_sw = ar.take([2, HALF])
        f_h = ar.take([2, HALF])
        f_h16 = ar.take([2, 2, T], F16)
        f_lg = ar.take([B, E1])
        f_w = ar.take([B, E1])
        f_s8 = ar.take([6, B])
        f_wT = ar.take([T], rows=E1)
        f_cmp = ar.take([B, E0, E0])
        f_eq = ar.take([B, E0, E0])
        f_tri = ar.take([E0, E0])
        f_rk = ar.take([B, E0])
        f_a = ar.take([B, E0])
        f_b = ar.take([B, E0])
        m_x = ar.take([B, E1 + 8])
        m_rep = ar.take([B, E1 + 8])
        m_top = ar.take([B, 8])
        m_sel = ar.take([B, E1])
        m_last = ar.take([B, E1])
        m_raw = ar.take([T], rows=E1)
        m_selT = ar.take([T], rows=E1)
        m_cum = ar.take([T], rows=E1)
        m_zero = ar.take([T], rows=E1)
        m_dropT = ar.take([T], rows=E1)
        m_lastT = ar.take([T], rows=E1)
        m_xs = ar.take([2, KD, E1], F16)
        m_ss = ar.take([1])
        m_hs = ar.take([1])
        m_hs16 = ar.take([2, 2], F16)
        m_rT = ar.take([KD, E1])
        m_r = ar.take([D], rows=E1)
        x_rms = xn

        ar = Arena()
        a2_q = ar.take([B, H2, DH2])
        a2_st = ar.take([B, H2, 4, DH2], F16)
        a2_qT = ar.take([2, H2 // 4, S], F16)
        a2_p = ar.take([2, 2, 4, S])
        a2_n = ar.take([3, 256])
        a2_o = ar.take([H2, DH2])
        a2_rc = ar.take([H2])

        ar = Arena()
        a3_y = ar.take([B, D])
        a3_o = ar.take([B, D])
        a3_xi = ar.take([B, D], BF16)
        a3_xiT = ar.take([KD, T], BF16)
        a3_s = ar.take([2, 3, B])
        a3_qp = ar.take([2, H3, 32])
        a3_qT = ar.take([2, H3 // 4, S])
        a3_p = ar.take([2, H3, S])
        a3_pT = ar.take([H3, S])
        a3_mx = ar.take([H3])
        a3_rc = ar.take([H3])

        block = ctx.enter_context(nc.Block())

        def bank(k):
            return ps[:, k, :]

        def seq_heads(k):
            return ps[:, k, :].bitcast(F16)

        KEYS_BEFORE = (2, 4)
        TURNS = [(NT[L] - 2) // 2 for L in range(4)]
        MID_TURNS = TURNS[:3] + [TURNS[3] - 1]

        def tiles(L):
            return sum(NT[:L])

        def halves(L):
            return 2 * tiles(L)

        def slot_tiles(L, slot):
            return sum((NT[m] + 1 - slot) // 2 for m in range(L))

        def wb_loads(L, slot):
            return slot_tiles(L, slot) + (slot_tiles(1, slot) if L else 0)

        def at(n, j, per=2):
            return n if j is None else per * j + n

        def turns_before(s):
            return s if s < 7 else 6

        @block.sync
        def _(sp):
            sp.dma_start(x[:, :, :], a["x"].rearrange("b s d -> s b d")).then_inc(sem("x_in"), 16)
            sp.dma_start(td[:, :], a["time_decay"]).then_inc(sem("small_in"), 16)
            sp.dma_start(tf[:, :], a["time_first"]).then_inc(sem("small_in"), 16)
            sp.dma_start(gates[:, :], a["gates"].partition_broadcast(P)).then_inc(sem("small_in"), 16)
            sp.dma_start(tinv[:, :], a["temperature"].partition_broadcast(P)).then_inc(sem("small_in"), 16)
            sp.dma_start(normw[:, :], a["norm_w"]).then_inc(sem("small_in"), 16)
            sp.dma_start(ctx_sb[:, :, :], a["ctx"].rearrange("b s d -> s b d")).then_inc(sem("ctx_in"), 16)
            sp.dma_start(wkv2[:, :, :], a["wkv2"]).then_inc(sem("kv_in"), 16)
            sp.dma_start(wkv3[:, :, :], a["wkv3"]).then_inc(sem("kv_in"), 16)
            sp.dma_start(bkv3[:, :], a["bkv3"]).then_inc(sem("kv_in"), 16)
            sp.dma_start(wq_f, a["wqp3"]).then_inc(sem("wqp_in"), 16)
            for k in range(LORA_T):
                if k:
                    sp.wait_ge(sem("folded_out"), 16 * k)
                if k % (F2 // P) == 0:
                    if k:
                        sp.wait_ge(sem("fold_mm"), k)
                    sp.dma_start(lora[:, :, :], a["lora"][:, k * P // F2]).then_inc(sem("lora_in"), 16)
                sp.dma_start(fold, a["w2"][k]).then_inc(sem("fold_in"), 16)
                sp.wait_ge(sem("fold_sum"), k + 1)
                sp.dma_start(folded[k], fold).then_inc(sem("folded_out"), 16)
            sp.wait_ge(sem("folded_out"), 16 * LORA_T)
            sp.dma_start(wr[:, :, :], a["wr"]).then_inc(sem("late_in"), 16)
            sp.dma_start(wq2[:, :, :], a["wq2"]).then_inc(sem("late_in"), 16)
            sp.dma_start(bq3[:, :], a["bq3"].partition_broadcast(P)).then_inc(sem("late_in"), 16)
            sp.dma_start(bp3[:, :], a["bp3"].partition_broadcast(P)).then_inc(sem("late_in"), 16)
            sp.dma_start(mask8[:, :, :].rearrange("p b s -> p (b s)"),
                         a["mask"].rearrange("b s -> (b s)").partition_broadcast(P)).then_inc(sem("late_in"), 16)

            sp.wait_ge(sem("ones"), 1)
            for L in range(2):
                sp.dma_start(routed[L][EXPERTS[L]].rearrange("(p k) -> p k", p=P), ones[:, 0:T // P]).then_inc(sem("ones_out"), 16)
            sp.wait_ge(sem("ones_out"), 16 * 2)

            def source(L, i):
                return folded[i] if L == 2 and i < LORA_T else a[f"w{L}"][i]

            def head_loads(L):
                for i in range(2):
                    if L > 0:
                        sp.wait_ge(sem("wd_lo"), tiles(L) - (NT[L - 1] + 1 - i) % 2)
                    sp.dma_start(W[:, i, :], source(L, i)).then_inc(sem("w_in", i), 16)

            def routed_out(L):
                if L == 1:
                    sp.wait_ge(sem("wT_ready", 1), 1)
                else:
                    sp.wait_ge(sem("wT_half"), (2, None, 4, 6)[L])
                sp.dma_start(routed[L][0:EXPERTS[L], :], f_wT[0:EXPERTS[L], :]).then_inc(sem("routed_out"), 16)
                sp.wait_ge(sem("routed_out"), 16 * (L + 1))

            def w_load(src, slot, before):
                sp.wait_ge(sem("wd_lo"), before)
                sp.dma_start(W[:, slot, :], src).then_inc(sem("w_in", slot), 16)

            def wb_load(L, row, slot, before):
                sp.wait_ge(sem("sw_done"), before)
                sp.dma_start(wb[:, slot, :], routed[L][row].partition_broadcast(P))\
                    .then_inc(sem("wb_in", slot), 16)

            def tile_loads(L, i, row, e=None, per=0):
                if e is None:
                    src, before = source(L, i), tiles(L) + i - 1
                    twice = 2 * before
                else:
                    src, before = a[f"w{L}"][e * per + i], e * per + (tiles(L) + i - 1)
                    twice = e * (2 * per) + 2 * (tiles(L) + i - 1)
                if e is not None or i >= 2:
                    w_load(src, i % 2, before)
                wb_load(L, row, i % 2, twice)

            def loads_0():
                sp.wait_ge(sem("wi"), 2)
                for i in range(NT0):
                    if i >= 2:
                        w_load(a["w0"][i], i % 2, i - 1)
                        sp.wait_ge(sem("sw_done"), 2 * i - 2)
                    for lo, hi, row in PIECES[i]:
                        sp.dma_start(wb[lo:hi, i % 2, :], routed[0][row].partition_broadcast(hi - lo))\
                            .then_inc(sem("wb_in", i % 2), 16)

            def loads_1():
                for i in range(2):
                    tile_loads(1, i, i)
                with sp.Fori(1, E1 // 2) as e:
                    for k in range(2):
                        tile_loads(1, k, 2 * e + k, e, 2)
                tile_loads(1, E1, E1)

            def loads_2():
                for i in range(LORA_T):
                    tile_loads(2, i, i // 2)
                with sp.Fori(LORA_T // 2, E2) as e:
                    for k in range(2):
                        tile_loads(2, k, e, e, 2)

            def loads_3():
                per = F3 // P
                for i in range(per):
                    tile_loads(3, i, 0)
                with sp.Fori(1, E3) as e:
                    for k in range(per):
                        tile_loads(3, k, e, e, per)

            for L, loads in enumerate((loads_0, loads_1, loads_2, loads_3)):
                head_loads(L)
                routed_out(L)
                loads()

            sp.wait_ge(sem("x_done"), 1)
            sp.dma_start(out.rearrange("b s d -> s b d"), x[:, :, :]).then_inc(sem("out_done"), 16)
            sp.wait_ge(sem("out_done"), 16)
            sp.wait_ge(sem("late_in"), 16 * 5)

        @block.gpsimd
        def _(pool):
            steps = [0]

            def link(ins):
                steps[0] += 1
                ins.then_inc(sem("pool_step"), 1)
                pool.wait_ge(sem("pool_step"), steps[0])

            link(nc.gpsimd.memset(ident[:, :], 0.0))
            nc.gpsimd.affine_select(out=ident[:, :], in_=ident[:, :], compare_op=ALU.not_equal, fill=1.0,
                                    base=0, pattern=[[-1, P]], channel_multiplier=1).then_inc(sem("ident"), 1)
            nc.gpsimd.memset(mhalf[:, :], -0.5).then_inc(sem("mhalf"), 1)
            nc.gpsimd.memset(ctxT[:, :, :, 0:1], 0.0).then_inc(sem("wkv_edges"), 1)
            nc.gpsimd.memset(wk_k[:, :, :, 0:1], FAR).then_inc(sem("wkv_edges"), 1)
            nc.gpsimd.memset(wk_pp[:, 0:1], 0.0).then_inc(sem("wkv_edges"), 1)
            nc.gpsimd.memset(wk_aa[:, 0:1], 0.0).then_inc(sem("wkv_edges"), 1)
            nc.gpsimd.memset(wk_bb[:, 0:1], 1.0).then_inc(sem("wkv_edges"), 1)
            pool.wait_ge(sem("ident"), 1)
            nc.gpsimd.tensor_copy(ident16[:, :], ident[:, :]).then_inc(sem("ident"), 1)
            nc.gpsimd.tensor_copy(identb[:, :], ident[:, :]).then_inc(sem("ident"), 1)
            nc.gpsimd.memset(ones[:, :], 1.0).then_inc(sem("ones"), 1)
            nc.gpsimd.memset(v2[:, :, :, DH2:DH2 + 1], 1.0).then_inc(sem("v_ones"), 1)
            nc.gpsimd.memset(v3[:, :, :, DH3:DH3 + 1], 1.0).then_inc(sem("v_ones"), 1)
            nc.gpsimd.memset(k3p[:, :, :], 0.0).then_inc(sem("k3p_zero"), 1)

            def inv_sqrt(s):
                pool.wait_ge(sem("ln_var"), s + 1)
                if s == 0:
                    pool.wait_ge(sem("mhalf"), 1)
                nc.gpsimd.tensor_tensor(rstd[:, :], veps[:, :], mhalf[:, 0:B], ALU.pow).then_inc(sem("ln_rstd"), 1)

            def wkv(c):
                pool.wait_ge(sem("wkv_exp"), 4 * c + 3)
                pool.wait_ge(sem("ctxT_ready"), 4)
                if c:
                    pool.wait_ge(sem("wkv_y"), c)
                v = ctxT[:, c, :, :].rearrange("p b s -> p (b s)")
                for k, e in ((0, 1), (1, 2)):
                    nc.gpsimd.tensor_tensor(wk_ev[:, k, :], wk_e[:, c, e, :], v, ALU.mult)\
                        .then_inc(sem("wkv_ev"), 1)

            def fold_lora(k):
                pool.wait_ge(sem("fold_in"), 16 * (k + 1))
                pool.wait_ge(sem("fold_add"), 2 * (k + 1))
                nc.gpsimd.tensor_tensor(fold, fold, fold_add, ALU.add).then_inc(sem("fold_sum"), 1)

            def scale_diagonals():
                pool.wait_ge(sem("wq_scale"), 1)
                for k in range(4):
                    ins = nc.gpsimd.tensor_scalar(wq_diag[:, k, :], ident[:, :], wq_s[:, 1, k:k + 1], None, ALU.mult)
                ins.then_inc(sem("wq_diag"), 1)

            def keys_2(b):
                sl = b % 2
                raw = k_raw[:, sl, :].rearrange("p (h d) -> p h d", d=DH2)
                sq = k_sq[:, sl, :].rearrange("p (h d) -> p h d", d=DH2)
                ms, guess, t = (k_norm[:, i, :] for i in range(3))
                pool.wait_ge(sem("k2_raw"), 2 * (b + 1))
                for n in (4, 2):
                    link(nc.gpsimd.tensor_tensor(sq[:, :, 0:n], sq[:, :, 0:n], sq[:, :, n:2 * n], ALU.add))
                link(nc.gpsimd.tensor_tensor(ms.unsqueeze(2), sq[:, :, 0:1], sq[:, :, 1:2], ALU.add))
                nc.gpsimd.tensor_scalar(ms, ms, 1.0 / DH2, RMS_EPS, ALU.mult, ALU.add).then_inc(sem("k2_ms"), 1)
                pool.wait_ge(sem("k2_guess"), b + 1)
                link(nc.gpsimd.tensor_tensor(t, guess, guess, ALU.mult))
                link(nc.gpsimd.tensor_tensor(t, t, ms, ALU.mult))
                link(nc.gpsimd.tensor_scalar(t, t, -0.5, 1.5, ALU.mult, ALU.add))
                link(nc.gpsimd.tensor_tensor(t, t, guess, ALU.mult))
                nc.gpsimd.tensor_tensor(raw, raw, t.unsqueeze(2).to_broadcast((P, H2, DH2)), ALU.mult).then_inc(sem("k2_norm"), 1)
                pool.wait_ge(sem("k2_norm"), b + 1)
                pool.wait_ge(sem("k2_hi"), 2 * (b + 1))
                for i in (1, 3):
                    nc.gpsimd.tensor_tensor(k_st[:, sl, :, i, :], raw, k_st[:, sl, :, i - 1, :], ALU.subtract)\
                        .then_inc(sem("k2_split"), 1)

            def sw(L, k, half, j=None):
                loads = 32 if L == 0 else 16
                arrived = 16 * wb_loads(L, k % 2) + loads * (k // 2 + 1)
                n = halves(L) + 2 * k + half + 1
                pool.wait_ge(sem("silu_done"), at(n, j, 4))
                if half == 0:
                    pool.wait_ge(sem("wb_in", k % 2), at(arrived, j, loads))
                if tiles(L) + k:
                    pool.wait_ge(sem("h_full"), at(n - 2, j, 4))
                nc.gpsimd.tensor_tensor(f_sw[:, half, :], f_s[:, half, :], wb[:, k % 2, half * HALF:(half + 1) * HALF],
                                        ALU.mult).then_inc(sem("sw_done"), 1)

            def ffn(L):
                for k in range(2):
                    for half in range(2):
                        sw(L, k, half)
                with pool.Fori(0, TURNS[L]) as j:
                    for k in (2, 3):
                        for half in range(2):
                            sw(L, k, half, j)
                if NT[L] % 2:
                    for half in range(2):
                        sw(L, NT[L] - 1, half)

            inv_sqrt(0)
            for b in range(B):
                if b in KEYS_BEFORE:
                    wkv(KEYS_BEFORE.index(b))
                keys_2(b)
                if b % 2:
                    fold_lora(b // 2)
                if b == 4:
                    scale_diagonals()
            inv_sqrt(1)
            ffn(0)
            pool.wait_ge(sem("late_in"), 16 * 5)
            inv_sqrt(2)
            link(nc.gpsimd.tensor_copy(a1_mask, mask8[:, :, :]))
            nc.gpsimd.tensor_scalar(a1_neg, a1_mask, -1.0, 1e30, ALU.add, ALU.mult).then_inc(sem("mask"), 1)
            inv_sqrt(3)
            pool.wait_ge(sem("rms_var"), 1)
            nc.gpsimd.tensor_tensor(rms[:, :], veps[:, :], mhalf[:, 0:B], ALU.pow).then_inc(sem("rms"), 1)
            ffn(1)
            inv_sqrt(4)
            for b in range(B):
                pool.wait_ge(sem("q2_hi"), b + 1)
                nc.gpsimd.tensor_tensor(a2_st[:, b, :, 3, :], a2_q[:, b, :, :], a2_st[:, b, :, 0, :], ALU.subtract)\
                    .then_inc(sem("q2_lo_pool"), 1)
            inv_sqrt(5)
            ffn(2)
            inv_sqrt(6)
            nc.gpsimd.memset(a3_qp, 0.0).then_inc(sem("qp_zero"), 1)
            inv_sqrt(7)
            ffn(3)

        @block.scalar
        def _(act):
            act.wait_ge(sem("small_in"), 16 * 5)
            nc.scalar.activation(tg[:, :], gates[:, :], ACT.Tanh).then_inc(sem("tg"), 1)
            nc.scalar.activation(wdec[:, :], td[:, :], ACT.Exp).then_inc(sem("decay"), 1)

            def turned(s, dst, scale=None):
                for half in range(2):
                    act.wait_ge(sem("turn"), 2 * turns_before(s) + half + 1)
                    for c in range(KD):
                        src = bank(2 * c + half)
                        o = dst(c, half)
                        if len(o.shape) == 3:
                            src = src.rearrange("p (b s) -> p b s", b=B // 2)
                        nc.scalar.activation(o, src, ACT.Copy, scale=1.0 if scale is None else scale(c))\
                            .then_inc(sem("turned"), 1)

            def turned_16(s, scale=None):
                for half in range(2):
                    act.wait_ge(sem("turn"), 2 * turns_before(s) + half + 1)
                    for c in range(KD):
                        nc.scalar.activation(x16[:, 0, c, half * HALF:(half + 1) * HALF], bank(2 * c + half), ACT.Copy,
                                             scale=1.0 if scale is None else scale(c)).then_inc(sem("turned"), 1)

            def xT_of(c, half):
                return xT[:, c, half * HALF:(half + 1) * HALF]

            def seg_of(t):
                return lambda c, half: t[:, c, half * (B // 2):(half + 1) * (B // 2), 1:SEG]

            act.wait_ge(sem("wkv_edges"), 5)
            for half in range(2):
                act.wait_ge(sem("ctxT_turn"), half + 1)
                for c in range(KD):
                    nc.scalar.activation(seg_of(ctxT)(c, half), bank(4 + 2 * c + half).rearrange("p (b s) -> p b s", b=B // 2),
                                         ACT.Copy).then_inc(sem("ctxT_ready"), 1)
            turned(0, seg_of(wk_k))

            def wkv_exp(c):
                for k, scale in ((0, 1.0), (1, -1.0), (2, 1.0), (3, -1.0)):
                    act.wait_ge(sem("wkv_arg"), 4 * c + k + 1)
                    nc.scalar.activation(wk_e[:, c, k, :], wk_e[:, c, k, :], ACT.Exp, scale=scale)\
                        .then_inc(sem("wkv_exp"), 1)

            act.wait_ge(sem("v_ones"), 2)
            act.wait_ge(sem("k3p_zero"), 1)

            def k2_hi(b):
                ms, guess, log = (k_norm[:, i, :] for i in (0, 1, 3))
                act.wait_ge(sem("k2_ms"), b + 1)
                nc.scalar.activation(log, ms, ACT.Ln).then_inc(sem("k2_log"), 1)
                act.wait_ge(sem("k2_log"), b + 1)
                nc.scalar.activation(guess, log, ACT.Exp, scale=-0.5).then_inc(sem("k2_guess"), 1)
                act.wait_ge(sem("k2_norm"), b + 1)
                if b >= 2:
                    act.wait_ge(sem("k2_turn"), b - 1)
                for i in (0, 2):
                    nc.scalar.activation(k_st[:, b % 2, :, i, :], k_raw[:, b % 2, :].rearrange("p (h d) -> p h d", d=DH2),
                                         ACT.Copy).then_inc(sem("k2_hi"), 1)

            def fold_copy(k):
                act.wait_ge(sem("fold_mm"), k + 1)
                if k:
                    act.wait_ge(sem("fold_sum"), k)
                    act.wait_ge(sem("folded_out"), 16 * k)
                nc.scalar.activation(fold_add[:, 0:2 * D], bank(0), ACT.Copy).then_inc(sem("fold_add"), 1)
                nc.scalar.activation(fold_add[:, 2 * D:3 * D], ps[:, 1, 0:D], ACT.Copy).then_inc(sem("fold_add"), 1)

            def k2_out(b):
                act.wait_ge(sem("k2_turn"), b + 1)
                nc.scalar.activation(k2T[:, b, :, :].rearrange("p g s -> p (g s)"), seq_heads(7), ACT.Copy)\
                    .then_inc(sem("k2_ready"), 1)

            for b in range(B):
                sl = b % 2
                if b in KEYS_BEFORE:
                    wkv_exp(KEYS_BEFORE.index(b))
                act.wait_ge(sem("kv2_mm"), b + 1)
                if b >= 2:
                    act.wait_ge(sem("k2_split"), 2 * (b - 1))
                nc.scalar.activation(k_sq[:, sl, :], ps[:, 6, 0:D], ACT.Square).then_inc(sem("k2_raw"), 1)
                nc.scalar.activation(k_raw[:, sl, :], ps[:, 6, 0:D], ACT.Copy).then_inc(sem("k2_raw"), 1)
                nc.scalar.activation(v2[:, b, :, 0:DH2], ps[:, 6, D:2 * D].rearrange("p (h d) -> p h d", d=DH2), ACT.Copy)\
                    .then_inc(sem("v2_out"), 1)
                act.wait_ge(sem("kv3_mm"), b + 1)
                if b >= 1:
                    act.wait_ge(sem("k3_turn"), b)
                nc.scalar.activation(k3p[:, :, 0:DH3], ps[:, 5, 0:D].rearrange("p (h d) -> p h d", d=DH3), ACT.Copy)\
                    .then_inc(sem("k3_raw"), 1)
                nc.scalar.activation(v3[:, b, :, 0:DH3], ps[:, 5, D:2 * D].rearrange("p (h d) -> p h d", d=DH3), ACT.Copy)\
                    .then_inc(sem("v3_out"), 1)
                act.wait_ge(sem("k3_turn"), b + 1)
                nc.scalar.activation(k3T[:, b, :, :].rearrange("p g s -> p (g s)"), bank(4), ACT.Copy).then_inc(sem("k3_ready"), 1)
                k2_hi(b)
                if b >= 1:
                    k2_out(b - 1)
                if b % 2:
                    fold_copy(b // 2)
            k2_out(B - 1)
            act.wait_ge(sem("wi_turn"), 1)
            nc.scalar.activation(wi[:, :, :, :].rearrange("p a b c -> p (a b c)"), ps[:, 2, :].bitcast(BF16), ACT.Copy)\
                .then_inc(sem("wi"), 1)
            act.wait_ge(sem("wscale_mm"), 1)
            nc.scalar.activation(wscale[:, :, :].rearrange("p a b -> p (a b)"), bank(3), ACT.Copy).then_inc(sem("wi"), 1)

            def router_exp(L):
                n = EXPERTS[L]
                act.wait_ge(sem("router_arg"), min(L, 2) + 1)
                nc.scalar.activation(f_lg[:, :, 0:n], f_lg[:, :, 0:n], ACT.Exp).then_inc(sem("router_exp"), 1)

            def wT_copy(L):
                n = EXPERTS[L]
                act.wait_ge(sem("w_turn"), L + 1)
                dst = m_raw if L == 1 else f_wT
                for h in range(2):
                    nc.scalar.activation(dst[0:n, h * HALF:(h + 1) * HALF], ps[0:n, 5 + h, :], ACT.Copy)\
                        .then_inc(sem("wT_out" if L == 1 else "wT_half"), 1)

            def silu(L, k, half, j=None):
                n = halves(L) + 2 * k + half + 1
                act.wait_ge(sem("gu_done"), at(n, j, 4))
                if tiles(L) + k:
                    act.wait_ge(sem("sw_done"), at(n - 2, j, 4))
                nc.scalar.activation(f_s[:, half, :], bank(half), ACT.Silu, scale=1.0 / WSCALE).then_inc(sem("silu_done"), 1)

            def gu_hi(L, k, j=None):
                act.wait_ge(sem("w_in", k % 2), at(16 * (slot_tiles(L, k % 2) + k // 2 + 1), j, 16))
                if tiles(L) + k >= 2:
                    act.wait_ge(sem("gu_done"), at(halves(L) + 2 * k - 2, j, 4))
                    if L == 1 and k >= 2:
                        act.wait_ge(sem("star_mm"), at(k - 1, j))
                nc.scalar.activation(W16[:, k % 2, 0, 0:2 * D], W[:, k % 2, 0:2 * D], ACT.Copy, scale=WSCALE)\
                    .then_inc(sem("wgu_hi"), 1)

            def down_hi(L, k, j=None):
                if tiles(L) + k >= 2:
                    act.wait_ge(sem("down_done"), at(tiles(L) + k - 1, j))
                nc.scalar.activation(W16[:, k % 2, 0, 2 * D:3 * D], W[:, k % 2, 2 * D:3 * D], ACT.Copy, scale=WSCALE)\
                    .then_inc(sem("wd_hi"), 1)

            def h_hi(L, k, half, j=None):
                act.wait_ge(sem("h_full"), at(halves(L) + 2 * k + half + 1, j, 4))
                if tiles(L) + k >= 2 and half == 0:
                    act.wait_ge(sem("down_done"), at(tiles(L) + k - 1, j))
                nc.scalar.activation(f_h16[:, k % 2, 0, half * HALF:(half + 1) * HALF], f_h[:, half, :], ACT.Copy)\
                    .then_inc(sem("h_hi"), 1)

            def tile(L, k, j=None, last=False, meanwhile=None):
                down_hi(L, k, j)
                silu(L, k, 0, j)
                if meanwhile:
                    meanwhile()
                if not last:
                    gu_hi(L, k + 1, j)
                h_hi(L, k, 0, j)
                silu(L, k, 1, j)
                if L == 1 and k < E1:
                    silu_star(k, j)
                h_hi(L, k, 1, j)

            def silu_star(k, j=None):
                n = k + 1
                act.wait_ge(sem("star_mm"), at(n, j))
                if k >= 1:
                    act.wait_ge(sem("star_done"), at(n - 1, j))
                nc.scalar.activation(m_ss, ps[:, 0, 0:1], ACT.Silu, scale=1.0 / WSCALE).then_inc(sem("star_silu"), 1)

            def ffn(L):
                def meanwhile():
                    wT_copy(L)
                    if L == 1:
                        for h, bk in ((0, 7), (1, 4)):
                            nc.scalar.activation(m_selT[:, h * HALF:(h + 1) * HALF], ps[0:E1, bk, :], ACT.Copy)\
                                .then_inc(sem("wT_out"), 1)
                        act.wait_ge(sem("last_turn"), 1)
                        nc.scalar.activation(m_last, ps[:, 5, 0:B * E1].rearrange("p (t e) -> p t e", e=E1), ACT.Copy)\
                            .then_inc(sem("last_out"), 1)
                        act.wait_ge(sem("xs_mm"), 1)
                        for c in range(KD):
                            nc.scalar.activation(m_xs[:, 0, c, :], ps[:, 6, c * E1:(c + 1) * E1], ACT.Copy, scale=normw[:, c:c + 1])\
                                .then_inc(sem("xs_hi"), 1)

                tile(L, 0, meanwhile=meanwhile)
                tile(L, 1)
                with act.Fori(0, MID_TURNS[L]) as j:
                    tile(L, 2, j)
                    tile(L, 3, j)
                for k in range(2 + 2 * MID_TURNS[L], NT[L]):
                    tile(L, k, last=(k == NT[L] - 1))

            act.wait_ge(sem("late_in"), 16 * 5)
            nc.scalar.activation(wr16[:, 0, :, :], wr[:, :, :], ACT.Copy).then_inc(sem("wr_hi"), 1)
            gu_hi(0, 0)
            turned_16(1)
            router_exp(0)
            ffn(0)
            turned(2, xT_of)
            act.wait_ge(sem("a1_arg"), 1)
            nc.scalar.activation(a1_p, a1_p, ACT.Exp).then_inc(sem("a1_p"), 1)
            act.wait_ge(sem("a1_turn"), 1)
            for h in range(2):
                nc.scalar.activation(a1_pT[:, 4 * h:4 * h + 4, :].rearrange("p b s -> p (b s)"), bank(6 + h), ACT.Copy)\
                    .then_inc(sem("a1_pT"), 1)
            turned_16(3, lambda c: normw[:, c:c + 1])
            router_exp(1)
            ffn(1)
            act.wait_ge(sem("r_turn"), 1)
            nc.scalar.activation(m_r, ps[0:E1, 0, 0:D], ACT.Copy).then_inc(sem("r_out"), 1)
            turned(4, xT_of)
            for b in range(4):
                act.wait_ge(sem("q2_mm"), b + 1)
                nc.scalar.activation(a2_q[:, 2 * b:2 * b + 2, :, :].rearrange("p b h d -> p (b h d)"), bank(4 + b), ACT.Square)\
                    .then_inc(sem("q2_sq"), 1)
            act.wait_ge(sem("q2_ss"), 1)
            nc.scalar.activation(a2_n[:, 2, :], a2_n[:, 0, :], ACT.Ln).then_inc(sem("q2_log"), 1)
            act.wait_ge(sem("q2_log"), 1)
            nc.scalar.activation(a2_n[:, 1, :], a2_n[:, 2, :], ACT.Exp, scale=-0.5).then_inc(sem("q2_rms"), 1)
            for b in range(B):
                act.wait_ge(sem("q2_norm"), b + 1)
                nc.scalar.activation(a2_st[:, b, :, 1, :], a2_q[:, b, :, :], ACT.Copy).then_inc(sem("q2_hi_act"), 1)
            for n in range(4 * B):
                act.wait_ge(sem("s2_mm"), n + 1)
                if n >= 2:
                    act.wait_ge(sem("pv2_job"), n - 1)
                pr = n % 2
                nc.scalar.activation(a2_p[:, n % 2, :, :, :].rearrange("p j g s -> p (j g s)"),
                                     ps[:, 2 * pr:2 * pr + 2, :].rearrange("p j s -> p (j s)"),
                                     ACT.Exp, scale=float(DH2) ** -0.5).then_inc(sem("p2"), 1)
            gu_hi(2, 0)
            turned_16(5)
            act.wait_ge(sem("router"), 3)
            act.wait_ge(sem("tinv"), 1)
            nc.scalar.activation(f_lg[:, :, 0:E2], ps[:, 4, 0:B * E2].rearrange("p (t e) -> p t e", e=E2), ACT.Tanh,
                                 scale=tinv[:, 0:1]).then_inc(sem("golden_tanh"), 1)
            act.wait_ge(sem("golden_dist"), 1)
            nc.scalar.activation(f_w[:, :, 0:E2], f_a, ACT.Exp, scale=-1.0 / 0.1).then_inc(sem("golden_exp"), 1)
            nc.scalar.activation(f_b, f_a, ACT.Exp, scale=-1.0 / 0.3).then_inc(sem("golden_exp"), 1)
            ffn(2)
            def whole_turned(k):
                act.wait_ge(sem("xi_turn", k), 1)
                for c in range(KD):
                    nc.scalar.activation(a3_xiT[:, c, :], ps[:, 4 + c, :].bitcast(BF16), ACT.Copy)\
                        .then_inc(sem("xi_turned", k), 1)

            whole_turned(0)

            def q3_copy(b):
                act.wait_ge(sem("q3_turn"), b + 1)
                nc.scalar.activation(a3_qT[:, b % 2, :, :].rearrange("p g s -> p (g s)"), bank(6), ACT.Copy)\
                    .then_inc(sem("q3_ready"), 1)

            q3_copy(0)
            for b in range(B):
                act.wait_ge(sem("p3_arg"), b + 1)
                nc.scalar.activation(a3_p[:, b % 2, :, :], a3_p[:, b % 2, :, :], ACT.Exp, scale=float(DH3) ** -0.5)\
                    .then_inc(sem("p3"), 1)
                if b + 1 < B:
                    q3_copy(b + 1)
                for h in range(2):
                    act.wait_ge(sem("p3_turn"), 2 * b + h + 1)
                    if b >= 1:
                        act.wait_ge(sem("pv3_half"), 2 * b + h - 1)
                    nc.scalar.activation(a3_pT[:, 8 * h:8 * h + 8, :].rearrange("p h s -> p (h s)"),
                                         ps[:, 4:6, :].rearrange("p h s -> p (h s)"), ACT.Copy).then_inc(sem("p3T"), 1)
            whole_turned(1)
            turned_16(7)
            router_exp(3)
            ffn(3)

        @block.tensor
        def _(pe):
            def turn(s, src=xn):
                for t in range(B):
                    pe.wait_ge(sem("xn_ready"), B * s + t + 1)
                    for c in range(KD):
                        last = nc.tensor.transpose(ps[:, 2 * c + t // 4, (t % 4) * S:(t % 4 + 1) * S],
                                                   src[:, t, c * P:(c + 1) * P], ident[:, :])
                    if t % 4 == 3:
                        last.then_inc(sem("turn"), 1)

            THREE = ((0, 0), (1, 0), (0, 1))

            def router(L, s):
                n = EXPERTS[L]
                for half in range(2):
                    pe.wait_ge(sem("x_lo"), 2 * KD * L + KD * (half + 1))
                    for t in range(4 * half, 4 * half + 4):
                        for c in range(KD):
                            for i, w in THREE:
                                last = nc.tensor.matmul(ps[:, 4, t * n:(t + 1) * n], x16[:, i, c, t * S:(t + 1) * S],
                                                        wr16[:, w, c, ROUTER_AT[L]:ROUTER_AT[L] + n],
                                                        start=(c == 0 and i + w == 0), stop=(c == KD - 1 and w == 1))
                last.then_inc(sem("router"), 1)

            def turn_w(L):
                n = EXPERTS[L]
                pe.wait_ge(sem("w_ready"), L + 1)
                for t in range(B):
                    last = nc.tensor.transpose(ps[0:n, 5 + t // 4, (t % 4) * S:(t % 4 + 1) * S],
                                               f_w[:, t, 0:n], ident[:, :])
                if L == 1:
                    for t in range(B):
                        last = nc.tensor.transpose(ps[0:n, (7, 4)[t // 4], (t % 4) * S:(t % 4 + 1) * S],
                                                   m_sel[:, t, :], ident[:, :])
                last.then_inc(sem("w_turn"), 1)

            def gate_up(L, k, half, j=None):
                if half == 0:
                    pe.wait_ge(sem("wgu_lo"), at(tiles(L) + k + 1, j))
                if k >= 1:
                    pe.wait_ge(sem("h_full"), at(halves(L) + 2 * k + half - 1, j, 4))
                    if L == 1 and half == 0:
                        pe.wait_ge(sem("star_done"), at(k, j))
                for g in range(2):
                    for c in range(KD):
                        for i, w in THREE:
                            last = nc.tensor.matmul(bank(2 * g + half), W16[:, k % 2, w, g * D + c * P:g * D + (c + 1) * P],
                                                    x16[:, i, c, half * HALF:(half + 1) * HALF],
                                                    start=(c == 0 and i + w == 0), stop=(c == KD - 1 and w == 1))
                last.then_inc(sem("gu_done"), 1)

            def down(L, k, half, j=None, first=False, final=False):
                if half == 0:
                    pe.wait_ge(sem("wd_lo"), at(tiles(L) + k + 1, j))
                pe.wait_ge(sem("h_lo"), at(halves(L) + 2 * k + half + 1, j, 4))
                for t in range(4 * half, 4 * half + 4):
                    for w, i in THREE:
                        last = nc.tensor.matmul(ps[:, 4 + t // 2, (t % 2) * D:(t % 2 + 1) * D],
                                                f_h16[:, k % 2, i, t * S:(t + 1) * S], W16[:, k % 2, w, 2 * D:3 * D],
                                                start=(first and t % 2 == 0 and i + w == 0), stop=final,
                                                skip_group_check=True)
                if half == 1:
                    last.then_inc(sem("down_done"), 1)

            def star(k, j=None, own=True, before=True):
                pe.wait_ge(sem("h_full"), at(halves(1) + 2 * k + 1, j, 4))
                if k == 0:
                    pe.wait_ge(sem("xs_lo"), KD)
                if before:
                    pe.wait_ge(sem("star_done"), at(k, j))
                e = at(k, j)
                if own:
                    for g in range(2):
                        for c in range(KD):
                            for w, i in THREE:
                                last = nc.tensor.matmul(ps[:, 2 * g, 0:1], W16[:, k % 2, w, g * D + c * P:g * D + (c + 1) * P],
                                                        m_xs[:, i, c, bass.ds(e, 1)],
                                                        start=(c == 0 and i + w == 0), stop=(c == KD - 1 and i == 1))
                if before:
                    for c in range(KD):
                        for w, i in THREE:
                            last = nc.tensor.matmul(ps[:, 2, 2 + c:3 + c],
                                                    W16[:, (k + 1) % 2, w, 2 * D + c * P:2 * D + (c + 1) * P],
                                                    m_hs16[:, (k + 1) % 2, i:i + 1], start=(i + w == 0), stop=(i == 1))
                last.then_inc(sem("star_mm"), 1)

            def ffn(L):
                gate_up(L, 0, 0)
                gate_up(L, 0, 1)
                turn_w(L)
                if L == 1:
                    pe.wait_ge(sem("last_ready"), 1)
                    for t in range(B):
                        last = nc.tensor.transpose(ps[:, 5, t * E1:(t + 1) * E1], m_lastT[:, t * S:(t + 1) * S], ident[0:E1, 0:E1])
                    last.then_inc(sem("last_turn"), 1)
                    pe.wait_ge(sem("last_out"), 1)
                    for c in range(KD):
                        for t in range(B):
                            last = nc.tensor.matmul(ps[:, 6, c * E1:(c + 1) * E1], x_rms[:, t, c * P:(c + 1) * P], m_last[:, t, :],
                                                    start=(t == 0), stop=(t == B - 1))
                    last.then_inc(sem("xs_mm"), 1)
                    star(0, before=False)
                else:
                    pe.wait_ge(sem("wT_half"), (2, None, 4, 6)[L])

                def pair(k, j=None, first=False):
                    for half in range(2):
                        gate_up(L, k, half, j)
                        if L == 1 and half == 1:
                            star(k, j, own=(k < E1))
                        down(L, k - 1, half, j, first=first)

                pair(1, first=True)
                with pe.Fori(0, TURNS[L]) as j:
                    pair(2, j)
                    pair(3, j)
                if NT[L] % 2:
                    pair(NT[L] - 1)
                if L == 1:
                    pe.wait_ge(sem("star_done"), E1 + 1)
                    pe.wait_ge(sem("h_full"), halves(2))
                    for c in range(KD):
                        last = nc.tensor.transpose(ps[0:E1, 0, c * P:(c + 1) * P], m_rT[:, c, :], ident[:, :])
                    last.then_inc(sem("r_turn"), 1)
                    pe.wait_ge(sem("r_out"), 1)
                    for t in range(B):
                        nc.tensor.matmul(ps[:, 4 + t // 2, (t % 2) * D:(t % 2 + 1) * D], m_dropT[:, t * S:(t + 1) * S], m_r,
                                         start=False, stop=False, skip_group_check=True)
                for half in range(2):
                    down(L, NT[L] - 1, half, final=True)

            pe.wait_ge(sem("ident"), 3)
            pe.wait_ge(sem("ctx_in"), 16)
            for t in range(B):
                for c in range(KD):
                    last = nc.tensor.transpose(ps[:, 4 + 2 * c + t // 4, (t % 4) * S:(t % 4 + 1) * S],
                                               ctx_sb[:, t, c * P:(c + 1) * P], ident[:, :])
                if t % 4 == 3:
                    last.then_inc(sem("ctxT_turn"), 1)
            turn(0)

            pe.wait_ge(sem("ctxT_ready"), 4)
            pe.wait_ge(sem("kv_in"), 16 * 3)
            pe.wait_ge(sem("ones"), 1)

            def fold_products(k):
                e, f = k // (F2 // P), k % (F2 // P)
                if k:
                    pe.wait_ge(sem("fold_add"), 2 * k)
                else:
                    pe.wait_ge(sem("turned"), 2 * KD)
                pe.wait_ge(sem("lora_in"), 16 * (e + 1))
                for g in range(2):
                    for c in range(KD):
                        nc.tensor.matmul(ps[:, 0, (2 * g + c) * P:(2 * g + c + 1) * P], lora[:, 2 * g, c * P:(c + 1) * P],
                                         lora[:, 2 * g + 1, f * P:(f + 1) * P], start=True, stop=True)
                nc.tensor.matmul(ps[:, 1, 0:D], lora[:, 4, f * P:(f + 1) * P], lora[:, 5, :], start=True, stop=True)\
                    .then_inc(sem("fold_mm"), 1)

            def turn_k2(b):
                pe.wait_ge(sem("k2_split"), 2 * (b + 1))
                if b:
                    pe.wait_ge(sem("k2_ready"), b)
                for g in range(H2 // 4):
                    last = nc.tensor.transpose(seq_heads(7)[:, g * S:(g + 1) * S],
                                               k_st[:, b % 2, 4 * g:4 * g + 4, :, :].rearrange("p h i d -> p (h i d)"), ident16[:, :])
                last.then_inc(sem("k2_turn"), 1)

            for b in range(B):
                if b:
                    pe.wait_ge(sem("v2_out"), b)
                    pe.wait_ge(sem("k2_raw"), 2 * b)
                for c in range(KD):
                    last = nc.tensor.matmul(bank(6), ctxT[:, c, b, 1:SEG], wkv2[:, c, :], start=(c == 0), stop=(c == KD - 1))
                last.then_inc(sem("kv2_mm"), 1)
                if b:
                    pe.wait_ge(sem("v3_out"), b)
                for c in range(KD):
                    nc.tensor.matmul(bank(5), ctxT[:, c, b, 1:SEG], wkv3[:, c, :], start=(c == 0), stop=False)
                nc.tensor.matmul(bank(5), ones[0:1, :], bkv3[:, :], start=False, stop=True).then_inc(sem("kv3_mm"), 1)
                pe.wait_ge(sem("k3_raw"), b + 1)
                if b:
                    pe.wait_ge(sem("k3_ready"), b)
                for g in range(H3 // 4):
                    last = nc.tensor.transpose(ps[:, 4, g * S:(g + 1) * S],
                                               k3p[:, 4 * g:4 * g + 4, :].rearrange("p h d -> p (h d)"), ident[:, :])
                last.then_inc(sem("k3_turn"), 1)
                if b >= 1:
                    turn_k2(b - 1)
                if b % 2:
                    fold_products(b // 2)
            turn_k2(B - 1)

            pe.wait_ge(sem("wq_whole"), 1)
            for w in range(2):
                for c in range(KD):
                    for o in range(KD):
                        k = (w * KD + c) * D + o * P
                        last = nc.tensor.transpose(ps[:, 2, :].bitcast(BF16)[:, k:k + P], wq_i[:, w, o, c * P:(c + 1) * P], identb[:, :])
            last.then_inc(sem("wi_turn"), 1)
            pe.wait_ge(sem("wq_diag"), 1)
            for k in range(4):
                last = nc.tensor.matmul(ps[:, 3, k * P:(k + 1) * P], ones[:, :], wq_diag[:, k, :], start=True, stop=True)
            last.then_inc(sem("wscale_mm"), 1)

            for c in range(KD):
                pe.wait_ge(sem("wkv_y"), c + 1)
                if c == 0:
                    pe.wait_ge(sem("fold_add"), 2 * LORA_T)
                    pe.wait_ge(sem("wi"), 2)
                for t in range(B):
                    last = nc.tensor.transpose(ps[:, t // 2, (t % 2) * D + c * P:(t % 2) * D + (c + 1) * P],
                                               wk_k[:, c, t, 1:SEG], ident[:, :])
            last.then_inc(sem("wkv_turn"), 1)
            pe.wait_ge(sem("k2_ready"), B)
            pe.wait_ge(sem("k3_ready"), B)
            pe.wait_ge(sem("v3_out"), B)

            pe.wait_ge(sem("late_in"), 16 * 5)
            turn(1)
            pe.wait_ge(sem("wr_lo"), 1)
            router(0, 1)
            ffn(0)
            turn(2)
            pe.wait_ge(sem("turned"), 2 * KD * 3)
            for b in range(B):
                for c in range(KD):
                    last = nc.tensor.matmul(ps[:, 4 + b // 4, (b % 4) * S:(b % 4 + 1) * S], xT[:, c, b * S:(b + 1) * S],
                                            ctxT[:, c, b, 1:SEG], start=(c == 0), stop=(c == KD - 1))
            last.then_inc(sem("a1_mm"), 1)
            pe.wait_ge(sem("a1_p"), 1)
            for b in range(B):
                last = nc.tensor.transpose(ps[:, 6 + b // 4, (b % 4) * S:(b % 4 + 1) * S], a1_p[:, b, :], ident[:, :])
            last.then_inc(sem("a1_turn"), 1)
            pe.wait_ge(sem("a1_pT"), 2)
            for b in range(B):
                last = nc.tensor.matmul(ps[:, b // 2, (b % 2) * D:(b % 2 + 1) * D], a1_pT[:, b, :], ctx_sb[:, b, :],
                                        start=True, stop=True)
            last.then_inc(sem("a1_pv"), 1)
            turn(3, x_rms)
            router(1, 3)
            ffn(1)
            turn(4)
            pe.wait_ge(sem("turned"), 2 * KD * 5)
            for t in range(B):
                for c in range(KD):
                    last = nc.tensor.matmul(ps[:, 4 + t // 2, (t % 2) * D:(t % 2 + 1) * D], xT[:, c, t * S:(t + 1) * S],
                                            wq2[:, c, :], start=(c == 0), stop=(c == KD - 1))
                if t % 2:
                    last.then_inc(sem("q2_mm"), 1)

            def turn_q2(b):
                pe.wait_ge(sem("q2_lo"), b + 1)
                pe.wait_ge(sem("q2_lo_pool"), b + 1)
                pe.wait_ge(sem("q2_hi_act"), b + 1)
                if b == 0:
                    pe.wait_ge(sem("q2_norm"), B)
                if b >= 2:
                    pe.wait_ge(sem("q2T"), b - 1)
                for g in range(H2 // 4):
                    last = nc.tensor.transpose(seq_heads(4 + b % 2)[:, g * S:(g + 1) * S],
                                               a2_st[:, b, 4 * g:4 * g + 4, :, :].rearrange("p h i d -> p (h i d)"), ident16[:, :])
                last.then_inc(sem("q2_turn"), 1)

            def pv2(n):
                b, hg, pr = n // 4, n % 4 // 2, n % 2
                pe.wait_ge(sem("p2"), n + 1)
                if n % 4 == 0 and b >= 2:
                    pe.wait_ge(sem("o2"), b - 1)
                for jj in range(2):
                    for g in range(4):
                        h = 4 * (4 * hg + g) + 2 * pr + jj
                        last = nc.tensor.matmul(ps[:, 6 + b % 2, h * (DH2 + 1):(h + 1) * (DH2 + 1)],
                                                a2_p[:, n % 2, jj, g, :], v2[:, b, h, :], start=True, stop=True)
                last.then_inc(sem("pv2_job"), 1)

            turn_q2(0)
            for n in range(4 * B):
                b, hg, pr = n // 4, n % 4 // 2, n % 2
                if n % 4 == 0:
                    pe.wait_ge(sem("q2T"), b + 1)
                if n >= 2:
                    pe.wait_ge(sem("p2"), n - 1)
                for g in range(4 * hg, 4 * hg + 4):
                    for jj in range(2):
                        i = 2 * pr + jj
                        last = nc.tensor.matmul(ps[:, i, (g % 4) * S:(g % 4 + 1) * S], k2T[32 * i:32 * i + 32, b, g, :],
                                                a2_qT[32 * i:32 * i + 32, b % 2, g, :], start=True, stop=True)
                last.then_inc(sem("s2_mm"), 1)
                if n % 4 == 1 and b + 1 < B:
                    turn_q2(b + 1)
                if n >= 1:
                    pv2(n - 1)
            pv2(4 * B - 1)
            turn(5)
            router(2, 5)
            ffn(2)
            def whole_product(k, first):
                pe.wait_ge(sem("xi", k), 1)
                for c in range(KD):
                    for t in range(B):
                        last = nc.tensor.transpose(ps[:, 4 + c, :].bitcast(BF16)[:, t * S:(t + 1) * S],
                                                   a3_xi[:, t, c * P:(c + 1) * P], identb[:, :])
                last.then_inc(sem("xi_turn", k), 1)
                pe.wait_ge(sem("xi_turned", k), KD)
                for t in range(B):
                    for c in range(KD):
                        last = nc.tensor.matmul(ps[:, t // 2, (t % 2) * D:(t % 2 + 1) * D], a3_xiT[:, c, t * S:(t + 1) * S],
                                                wi[:, k, c, :], start=(c == 0), stop=(c == KD - 1))
                last.then_inc(sem("whole_mm", k), 1)

            whole_product(0, True)

            def turn_q3(b):
                pe.wait_ge(sem("q3p"), b + 1)
                if b:
                    pe.wait_ge(sem("q3_ready"), b)
                for g in range(H3 // 4):
                    last = nc.tensor.transpose(ps[:, 6, g * S:(g + 1) * S],
                                               a3_qp[:, b % 2, 4 * g:4 * g + 4, :].rearrange("p h d -> p (h d)"), ident[:, :])
                last.then_inc(sem("q3_turn"), 1)

            def scores_3(b):
                pe.wait_ge(sem("q3_ready"), b + 1)
                if b:
                    pe.wait_ge(sem("p3_arg"), b)
                else:
                    pe.wait_ge(sem("q3"), 1)
                for g in range(H3 // 4):
                    for i in range(4):
                        last = nc.tensor.matmul(ps[:, i, g * S:(g + 1) * S], a3_qT[32 * i:32 * i + DH3, b % 2, g, :],
                                                k3T[32 * i:32 * i + DH3, b, g, :], start=True, stop=True)
                last.then_inc(sem("s3_mm"), 1)

            def pv3(b):
                pe.wait_ge(sem("p3"), b + 1)
                for h in range(2):
                    n = 2 * b + h
                    if n:
                        pe.wait_ge(sem("p3T"), n)
                    for k in range(8):
                        last = nc.tensor.transpose(ps[:, 4 + k // 4, (k % 4) * S:(k % 4 + 1) * S], a3_p[:, b % 2, 8 * h + k, :], ident[:, :])
                    last.then_inc(sem("p3_turn"), 1)
                for h in range(2):
                    pe.wait_ge(sem("p3T"), 2 * b + h + 1)
                    if b and h == 0:
                        pe.wait_ge(sem("o3"), b)
                    for k in range(8 * h, 8 * h + 8):
                        head = 4 * (k % 4) + k // 4
                        last = nc.tensor.matmul(ps[:, 7, k * (DH3 + 1):(k + 1) * (DH3 + 1)], a3_pT[:, k, :], v3[:, b, head, :],
                                                start=True, stop=True)
                    last.then_inc(sem("pv3_half"), 1)

            turn_q3(0)
            scores_3(0)
            for b in range(B):
                if b + 1 < B:
                    turn_q3(b + 1)
                    scores_3(b + 1)
                pv3(b)
            whole_product(1, False)
            turn(7)
            router(3, 7)
            ffn(3)

        @block.vector
        def _(dve):
            steps = [0]

            def link(ins):
                steps[0] += 1
                ins.then_inc(sem("dve_step"), 1)
                dve.wait_ge(sem("dve_step"), steps[0])

            def layer_norm(s, signal=True):
                for t in range(B):
                    ins = nc.vector.bn_stats(stats[:, t, :], x[:, t, :])
                link(ins)
                for t in range(B):
                    ins = nc.vector.bn_aggr(mv[:, t, :], stats[:, t, :])
                link(ins)
                nc.vector.tensor_scalar(veps[:, :], mv[:, :, 1], LN_EPS, None, ALU.add).then_inc(sem("ln_var"), 1)
                dve.wait_ge(sem("ln_rstd"), s + 1)
                for t in range(B):
                    ins = nc.vector.tensor_scalar(xn[:, t, :], x[:, t, :], mv[:, t, 0:1], rstd[:, t:t + 1],
                                                  ALU.subtract, ALU.mult)
                    if signal:
                        ins.then_inc(sem("xn_ready"), 1)
                if signal:
                    dve.wait_ge(sem("xn_ready"), B * (s + 1))
                else:
                    link(ins)

            def wkv():
                dve.wait_ge(sem("decay"), 1)
                dve.wait_ge(sem("wkv_edges"), 5)
                link(nc.vector.tensor_scalar(wdec[:, :], wdec[:, :], -1.0, None, ALU.mult))
                for c in range(KD):
                    dve.wait_ge(sem("turned"), 2 * KD)
                    k = wk_k[:, c, :, :].rearrange("p b s -> p (b s)")
                    pp = wk_pp[:, 1:LW + 1]
                    before = wk_pp[:, 0:LW]
                    link(nc.vector.tensor_scalar(wk_dec, k, 0.0, wdec[:, c:c + 1], ALU.mult, ALU.add))
                    link(nc.vector.memset(wk_dec.rearrange("p (b s) -> p b s", b=B)[:, :, 0:1], FAR))
                    link(nc.vector.tensor_tensor_scan(pp, wk_dec, k, FAR, ALU.add, ALU.max))
                    nc.vector.scalar_tensor_tensor(wk_d[:, 0, :], before, wdec[:, c:c + 1], k, ALU.add, ALU.subtract)
                    link(nc.vector.scalar_tensor_tensor(wk_d[:, 1, :], k, tf[:, c:c + 1], before, ALU.add, ALU.subtract))
                    for e, (d, op) in enumerate(((0, ALU.min), (0, ALU.max), (1, ALU.min), (1, ALU.max))):
                        nc.vector.tensor_scalar(wk_e[:, c, e, :], wk_d[:, d, :], 0.0, None, op).then_inc(sem("wkv_arg"), 1)
                    dve.wait_ge(sem("wkv_arg"), 4 * c + 4)
                weight_scales()
                for c in range(KD):
                    dve.wait_ge(sem("wkv_exp"), 4 * c + 4)
                    e1b, e2b, e2, e1 = (wk_e[:, c, k, :] for k in range(4))
                    nc.vector.tensor_tensor_scan(wk_bb[:, 1:LW + 1], e1b, e2b, 0.0, ALU.mult, ALU.add)
                    dve.wait_ge(sem("wkv_ev"), 2 * c + 2)
                    link(nc.vector.tensor_tensor_scan(wk_aa[:, 1:LW + 1], e1b, wk_ev[:, 0, :], 0.0, ALU.mult, ALU.add))
                    nc.vector.tensor_tensor(wk_d[:, 0, :], e1, wk_bb[:, 0:LW], ALU.mult)
                    link(nc.vector.tensor_tensor(wk_d[:, 1, :], e1, wk_aa[:, 0:LW], ALU.mult))
                    nc.vector.tensor_tensor(wk_d[:, 0, :], wk_d[:, 0, :], e2, ALU.add)
                    link(nc.vector.tensor_tensor(wk_d[:, 1, :], wk_d[:, 1, :], wk_ev[:, 1, :], ALU.add))
                    link(nc.vector.reciprocal(wk_d[:, 0, :], wk_d[:, 0, :]))
                    ins = nc.vector.tensor_tensor(wk_k[:, c, :, :].rearrange("p b s -> p (b s)"), wk_d[:, 0, :], wk_d[:, 1, :], ALU.mult)
                    ins.then_inc(sem("wkv_y"), 1)
                    dve.wait_ge(sem("wkv_y"), c + 1)
                dve.wait_ge(sem("tg"), 1)
                link(nc.vector.tensor_scalar(tg_ffn[:, :], tg[:, :], 1.0 / WSCALE, None, ALU.mult))
                dve.wait_ge(sem("wkv_turn"), 1)
                add_banks(0, 0, tg)

            def add_banks(first, gate, tg):
                for b in range(4):
                    xs = x[:, 2 * b:2 * b + 2, :].rearrange("p t d -> p (t d)")
                    ins = nc.vector.scalar_tensor_tensor(xs, ps[:, first + b, :], tg[:, gate:gate + 1], xs, ALU.mult, ALU.add)
                link(ins)

            def weight_scales():
                dve.wait_ge(sem("wqp_in"), 16)
                link(nc.vector.tensor_reduce(wq_s[:, 0, :], wq_f.rearrange("p w o d -> p (w o) d"), AX.X, ALU.max,
                                             apply_absolute_value=True))
                link(nc.vector.tensor_scalar(wq_s[:, 1, :], wq_s[:, 0, :], 1.0 / 127.0, 1e-8, ALU.mult, ALU.max))
                nc.vector.reciprocal(wq_s[:, 2, :], wq_s[:, 1, :]).then_inc(sem("wq_scale"), 1)
                dve.wait_ge(sem("wq_scale"), 1)
                for k in range(4):
                    w = wq_f[:, k // 2, k % 2, :]
                    ins = nc.vector.tensor_scalar(w, w, wq_s[:, 2, k:k + 1], ROUND, ALU.mult, ALU.add)
                link(ins)
                link(nc.vector.tensor_scalar(wq_f, wq_f, ROUND, 127.0, ALU.subtract, ALU.min))
                nc.vector.tensor_scalar(wq_i, wq_f, -127.0, None, ALU.max).then_inc(sem("wq_whole"), 1)
                link(nc.vector.reciprocal(tinv[:, :], tinv[:, :]))
                nc.vector.tensor_scalar(tinv[:, :], tinv[:, :], 0.5, None, ALU.mult).then_inc(sem("tinv"), 1)

            def spread(v, n):
                return v.unsqueeze(2).to_broadcast((P, B, n))

            def softmax(L):
                n = EXPERTS[L]
                lg = f_lg[:, :, 0:n]
                mx, sm, rc = f_s8[:, 0, :], f_s8[:, 1, :], f_s8[:, 2, :]
                dve.wait_ge(sem("router"), L + 1)
                scores = ps[:, 4, 0:B * n].rearrange("p (t e) -> p t e", e=n)
                link(nc.vector.tensor_reduce(mx, scores, AX.X, ALU.max))
                nc.vector.tensor_tensor(lg, scores, spread(mx, n), ALU.subtract).then_inc(sem("router_arg"), 1)
                dve.wait_ge(sem("router_exp"), min(L, 2) + 1)
                link(nc.vector.tensor_reduce(sm, lg, AX.X, ALU.add))
                link(nc.vector.reciprocal(rc, sm))
                link(nc.vector.tensor_tensor(f_w[:, :, 0:n], lg, spread(rc, n), ALU.mult))

            def before(v):
                ve = v.unsqueeze(3).to_broadcast((P, B, E0, E0))
                vj = v.unsqueeze(2).to_broadcast((P, B, E0, E0))
                nc.vector.tensor_tensor(f_cmp, vj, ve, ALU.is_gt)
                link(nc.vector.tensor_tensor(f_eq, vj, ve, ALU.is_equal))
                link(nc.vector.tensor_tensor(f_eq, f_eq, f_tri.unsqueeze(1).to_broadcast((P, B, E0, E0)), ALU.mult))
                link(nc.vector.tensor_tensor(f_cmp, f_cmp, f_eq, ALU.add))

            def make_tri():
                link(nc.vector.memset(f_tri, 0.0))
                for e in range(1, E0):
                    ins = nc.vector.memset(f_tri[:, e, 0:e], 1.0)
                link(ins)

            def hidden(L, k, half, j=None):
                n = halves(L) + 2 * k + half + 1
                dve.wait_ge(sem("sw_done"), at(n, j, 4))
                dve.wait_ge(sem("gu_done"), at(n, j, 4))
                nc.vector.scalar_tensor_tensor(f_h[:, half, :], bank(2 + half), 1.0 / WSCALE, f_sw[:, half, :],
                                               ALU.mult, ALU.mult).then_inc(sem("h_full"), 1)

            def h_lo(L, k, half, j=None):
                hi, lo = (f_h16[:, k % 2, i, half * HALF:(half + 1) * HALF] for i in range(2))
                dve.wait_ge(sem("h_hi"), at(halves(L) + 2 * k + half + 1, j, 4))
                nc.vector.tensor_tensor(lo, f_h[:, half, :], hi, ALU.subtract).then_inc(sem("h_lo"), 1)

            def gu_lo(L, k, j=None):
                dve.wait_ge(sem("wgu_hi"), at(tiles(L) + k + 1, j))
                nc.vector.scalar_tensor_tensor(W16[:, k % 2, 1, 0:2 * D], W[:, k % 2, 0:2 * D], WSCALE,
                                               W16[:, k % 2, 0, 0:2 * D], ALU.mult, ALU.subtract).then_inc(sem("wgu_lo"), 1)

            def down_lo(L, k, j=None):
                dve.wait_ge(sem("wd_hi"), at(tiles(L) + k + 1, j))
                nc.vector.scalar_tensor_tensor(W16[:, k % 2, 1, 2 * D:3 * D], W[:, k % 2, 2 * D:3 * D], WSCALE,
                                               W16[:, k % 2, 0, 2 * D:3 * D], ALU.mult, ALU.subtract).then_inc(sem("wd_lo"), 1)

            def x_lo(s, L):
                for half in range(2):
                    for c in range(KD):
                        n = KD * half + c + 1
                        dve.wait_ge(sem("turned"), 2 * KD * turns_before(s) + n)
                        hi, lo = (x16[:, i, c, half * HALF:(half + 1) * HALF] for i in range(2))
                        nc.vector.scalar_tensor_tensor(lo, bank(2 * c + half), normw[:, c:c + 1] if L == 1 else 1.0, hi,
                                                       ALU.mult, ALU.subtract).then_inc(sem("x_lo"), 1)

            def star(k, j=None, own=True, before=True):
                n = k + 1
                dve.wait_ge(sem("star_mm"), at(n, j))
                if before:
                    e = k - 1 if j is None else 2 * j + (k - 1)
                    ins = nc.vector.tensor_copy(m_rT[:, :, bass.ds(e, 1)], ps[:, 2, 2:4].unsqueeze(2))
                if own:
                    dve.wait_ge(sem("star_silu"), at(n, j))
                    nc.vector.scalar_tensor_tensor(m_hs, ps[:, 2, 0:1], 1.0 / WSCALE, m_ss, ALU.mult, ALU.mult)\
                        .then_inc(sem("star_full"), 1)
                    dve.wait_ge(sem("star_full"), at(n, j))
                    nc.vector.tensor_copy(m_hs16[:, k % 2, 0:1], m_hs).then_inc(sem("star_hi"), 1)
                    dve.wait_ge(sem("star_hi"), at(n, j))
                    ins = nc.vector.tensor_tensor(m_hs16[:, k % 2, 1:2], m_hs, m_hs16[:, k % 2, 0:1], ALU.subtract)
                ins.then_inc(sem("star_done"), 1)

            def tile(L, k, j=None, last=False):
                down_lo(L, k, j)
                hidden(L, k, 0, j)
                if not last:
                    gu_lo(L, k + 1, j)
                h_lo(L, k, 0, j)
                if L == 1:
                    star(k, j, own=(k < E1), before=(k > 0))
                hidden(L, k, 1, j)
                h_lo(L, k, 1, j)

            def ffn(L):
                tile(L, 0)
                tile(L, 1)
                with dve.Fori(0, MID_TURNS[L]) as j:
                    tile(L, 2, j)
                    tile(L, 3, j)
                for k in range(2 + 2 * MID_TURNS[L], NT[L]):
                    tile(L, k, last=(k == NT[L] - 1))
                dve.wait_ge(sem("down_done"), tiles(L + 1))
                add_banks(4, 4 + L, tg_ffn)

            dve.wait_ge(sem("x_in"), 16)
            layer_norm(0)
            wkv()
            dve.wait_ge(sem("wr_hi"), 1)
            nc.vector.tensor_tensor(wr16[:, 1, :, :], wr[:, :, :], wr16[:, 0, :, :], ALU.subtract).then_inc(sem("wr_lo"), 1)
            gu_lo(0, 0)
            layer_norm(1)
            x_lo(1, 0)
            make_tri()
            softmax(0)
            before(f_w[:, :, 0:E0])
            link(nc.vector.tensor_reduce(f_rk, f_cmp, AX.X, ALU.add))
            nc.vector.scalar_tensor_tensor(f_w[:, :, 0:E0], f_rk, TOP0 - 0.5, f_w[:, :, 0:E0], ALU.is_lt, ALU.mult)\
                .then_inc(sem("w_ready"), 1)
            ffn(0)
            layer_norm(2)
            dve.wait_ge(sem("mask"), 1)
            link(nc.vector.tensor_reduce(a1_s[:, 0, :], a1_mask, AX.X, ALU.max))
            dve.wait_ge(sem("a1_mm"), 1)
            flat = a1_p.rearrange("p b s -> p (b s)")
            link(nc.vector.scalar_tensor_tensor(flat, ps[:, 4:6, :].rearrange("p h s -> p (h s)"), float(D) ** -0.5,
                                                a1_mask.rearrange("p b s -> p (b s)"), ALU.mult, ALU.mult))
            link(nc.vector.tensor_tensor(a1_p, a1_p, a1_neg, ALU.add))
            link(nc.vector.tensor_reduce(a1_s[:, 1, :], a1_p, AX.X, ALU.max))
            nc.vector.tensor_tensor(a1_p, a1_p, spread(a1_s[:, 1, :], S), ALU.subtract).then_inc(sem("a1_arg"), 1)
            dve.wait_ge(sem("a1_p"), 1)
            link(nc.vector.tensor_reduce(a1_s[:, 2, :], a1_p, AX.X, ALU.add))
            link(nc.vector.reciprocal(a1_s[:, 3, :], a1_s[:, 2, :]))
            link(nc.vector.scalar_tensor_tensor(a1_s[:, 4, :], a1_s[:, 3, :], tg[:, 1:2], a1_s[:, 0, :], ALU.mult, ALU.mult))
            dve.wait_ge(sem("a1_pv"), 1)
            for b in range(B):
                ins = nc.vector.scalar_tensor_tensor(x[:, b, :], ps[:, b // 2, (b % 2) * D:(b % 2 + 1) * D],
                                                     a1_s[:, 4, b:b + 1], x[:, b, :], ALU.mult, ALU.add)
            link(ins)
            layer_norm(3, signal=False)
            link(nc.vector.tensor_tensor(rms[:, :], mv[:, :, 1], rstd[:, :], ALU.mult))
            link(nc.vector.tensor_tensor(rms[:, :], rms[:, :], rstd[:, :], ALU.mult))
            nc.vector.tensor_scalar(veps[:, :], rms[:, :], RMS_EPS, None, ALU.add).then_inc(sem("rms_var"), 1)
            flat = x[:, :, :].rearrange("p t d -> p (t d)")
            link(nc.vector.scalar_tensor_tensor(flat, xn[:, :, :].rearrange("p t d -> p (t d)"), tg[:, 5:6], flat, ALU.mult, ALU.add))
            dve.wait_ge(sem("rms"), 1)
            for t in range(B):
                nc.vector.tensor_scalar(x_rms[:, t, :], xn[:, t, :], rms[:, t:t + 1], None, ALU.mult)\
                    .then_inc(sem("xn_ready"), 1)
            x_lo(3, 1)
            nc.vector.memset(m_zero, 0.0)
            nc.vector.memset(m_x[:, :, E1:E1 + 8], -1.0)
            softmax(1)
            nc.vector.tensor_copy(m_x[:, :, 0:E1], f_w)
            for t in range(B):
                ins = nc.vector.max(m_top[:, t, :], f_w[:, t, :])
            link(ins)
            link(nc.vector.memset(m_top[:, :, TOP1:8], -1.0))
            for t in range(B):
                ins = nc.vector.match_replace(m_rep[:, t, :], m_top[:, t, :], m_x[:, t, :], -2.0)
            link(ins)
            link(nc.vector.tensor_scalar(m_sel, m_rep[:, :, 0:E1], -2.0, None, ALU.is_equal))
            link(nc.vector.tensor_tensor(f_w, f_w, m_sel, ALU.mult))
            link(nc.vector.tensor_reduce(f_s8[:, 3, :], f_w, AX.X, ALU.add))
            link(nc.vector.reciprocal(f_s8[:, 4, :], f_s8[:, 3, :]))
            nc.vector.tensor_tensor(f_w, f_w, spread(f_s8[:, 4, :], E1), ALU.mult).then_inc(sem("w_ready"), 1)
            dve.wait_ge(sem("wT_out"), 4)
            link(nc.vector.tensor_tensor_scan(m_cum, m_selT, m_zero, 0.0, ALU.add, ALU.add))
            nc.vector.scalar_tensor_tensor(f_wT, m_cum, float(CAPACITY), m_raw, ALU.is_le, ALU.mult)\
                .then_inc(sem("wT_ready", 1), 1)
            nc.vector.scalar_tensor_tensor(m_dropT, m_cum, float(CAPACITY), m_raw, ALU.is_gt, ALU.mult)\
                .then_inc(sem("drop_ready"), 1)
            nc.vector.scalar_tensor_tensor(m_lastT, m_cum, float(CAPACITY), m_selT, ALU.is_equal, ALU.mult)\
                .then_inc(sem("last_ready"), 1)
            dve.wait_ge(sem("xs_hi"), KD)
            for c in range(KD):
                nc.vector.scalar_tensor_tensor(m_xs[:, 1, c, :], ps[:, 6, c * E1:(c + 1) * E1], normw[:, c:c + 1],
                                               m_xs[:, 0, c, :], ALU.mult, ALU.subtract).then_inc(sem("xs_lo"), 1)
            ffn(1)
            layer_norm(4)
            groups = a2_q.rearrange("p b h d -> p (b h) d")
            dve.wait_ge(sem("q2_sq"), 4)
            link(nc.vector.tensor_reduce(a2_n[:, 0, :], groups, AX.X, ALU.add))
            nc.vector.tensor_scalar(a2_n[:, 0, :], a2_n[:, 0, :], 1.0 / DH2, RMS_EPS, ALU.mult, ALU.add).then_inc(sem("q2_ss"), 1)
            dve.wait_ge(sem("q2_rms"), 1)
            guess, t = a2_n[:, 1, :], a2_n[:, 2, :]
            link(nc.vector.tensor_tensor(t, guess, guess, ALU.mult))
            link(nc.vector.tensor_tensor(t, t, a2_n[:, 0, :], ALU.mult))
            link(nc.vector.tensor_scalar(t, t, -0.5, 1.5, ALU.mult, ALU.add))
            link(nc.vector.tensor_tensor(guess, t, guess, ALU.mult))
            for b in range(B):
                nc.vector.tensor_tensor(a2_q[:, b, :, :], ps[:, 4 + b // 2, (b % 2) * D:(b % 2 + 1) * D].rearrange("p (h d) -> p h d", d=DH2),
                                        a2_n[:, 1, b * H2:(b + 1) * H2].unsqueeze(2).to_broadcast((P, H2, DH2)), ALU.mult)\
                    .then_inc(sem("q2_norm"), 1)
                dve.wait_ge(sem("q2_norm"), b + 1)
                nc.vector.tensor_copy(a2_st[:, b, :, 0, :], a2_q[:, b, :, :]).then_inc(sem("q2_hi"), 1)
                dve.wait_ge(sem("q2_hi"), b + 1)
                nc.vector.tensor_tensor(a2_st[:, b, :, 2, :], a2_q[:, b, :, :], a2_st[:, b, :, 0, :], ALU.subtract)\
                    .then_inc(sem("q2_lo"), 1)

            def q2T(b):
                dve.wait_ge(sem("q2_turn"), b + 1)
                if b >= 2:
                    dve.wait_ge(sem("s2_mm"), 4 * (b - 1))
                nc.vector.tensor_copy(a2_qT[:, b % 2, :, :].rearrange("p g s -> p (g s)"), seq_heads(4 + b % 2)).then_inc(sem("q2T"), 1)

            q2T(0)
            for b in range(B):
                if b + 1 < B:
                    q2T(b + 1)
                dve.wait_ge(sem("pv2_job"), 4 * (b + 1))
                pv = ps[:, 6 + b % 2, 0:H2 * (DH2 + 1)].rearrange("p (h d) -> p h d", d=DH2 + 1)
                link(nc.vector.reciprocal(a2_rc.unsqueeze(2), pv[:, :, DH2:DH2 + 1]))
                ins = nc.vector.tensor_tensor(a2_o, pv[:, :, 0:DH2], a2_rc.unsqueeze(2).to_broadcast((P, H2, DH2)), ALU.mult)
                ins.then_inc(sem("o2"), 1)
                dve.wait_ge(sem("o2"), b + 1)
                link(nc.vector.scalar_tensor_tensor(x[:, b, :], a2_o.rearrange("p h d -> p (h d)"), tg[:, 2:3], x[:, b, :],
                                                    ALU.mult, ALU.add))
            gu_lo(2, 0)
            layer_norm(5)
            x_lo(5, 2)
            make_tri()
            w, lg, dist, fb = f_w[:, :, 0:E2], f_lg[:, :, 0:E2], f_a, f_b
            zone = f_rk
            dve.wait_ge(sem("golden_tanh"), 1)
            link(nc.vector.tensor_scalar(lg, lg, 0.5, 0.5, ALU.mult, ALU.add))
            link(nc.vector.tensor_scalar(zone, lg, GOLDEN_LOWER, None, ALU.is_ge))
            link(nc.vector.scalar_tensor_tensor(zone, lg, GOLDEN_UPPER, zone, ALU.is_le, ALU.mult))
            link(nc.vector.tensor_scalar(dist, lg, GOLDEN_CENTER, None, ALU.subtract))
            link(nc.vector.tensor_scalar(lg, dist, -1.0, None, ALU.mult))
            nc.vector.tensor_tensor(dist, dist, lg, ALU.max).then_inc(sem("golden_dist"), 1)
            dve.wait_ge(sem("golden_exp"), 2)
            link(nc.vector.tensor_tensor(w, w, zone, ALU.mult))
            link(nc.vector.tensor_reduce(f_s8[:, 0, :], w, AX.X, ALU.add))
            link(nc.vector.tensor_scalar(f_s8[:, 1, :], f_s8[:, 0, :], 1e-8, None, ALU.is_lt))
            link(nc.vector.tensor_scalar(f_s8[:, 2, :], f_s8[:, 0, :], 1e-8, None, ALU.is_ge))
            before(fb)
            link(nc.vector.tensor_reduce(zone, f_cmp, AX.X, ALU.add))
            link(nc.vector.scalar_tensor_tensor(fb, zone, 1.5, fb, ALU.is_lt, ALU.mult))
            link(nc.vector.tensor_reduce(f_s8[:, 3, :], fb, AX.X, ALU.add))
            link(nc.vector.tensor_scalar(f_s8[:, 3, :], f_s8[:, 3, :], 1e-8, None, ALU.max))
            link(nc.vector.reciprocal(f_s8[:, 4, :], f_s8[:, 3, :]))
            link(nc.vector.tensor_tensor(f_s8[:, 4, :], f_s8[:, 4, :], f_s8[:, 1, :], ALU.mult))
            nc.vector.tensor_tensor(fb, fb, spread(f_s8[:, 4, :], E2), ALU.mult)
            link(nc.vector.tensor_tensor(w, w, spread(f_s8[:, 2, :], E2), ALU.mult))
            link(nc.vector.tensor_tensor(w, w, fb, ALU.add))
            link(nc.vector.tensor_reduce(f_s8[:, 0, :], w, AX.X, ALU.add))
            link(nc.vector.tensor_scalar(f_s8[:, 0, :], f_s8[:, 0, :], 1e-8, None, ALU.max))
            link(nc.vector.reciprocal(f_s8[:, 1, :], f_s8[:, 0, :]))
            nc.vector.tensor_tensor(w, w, spread(f_s8[:, 1, :], E2), ALU.mult).then_inc(sem("w_ready"), 1)
            ffn(2)
            def whole(src, k):
                amax, scale, inv = (a3_s[:, k, i, :] for i in range(3))
                link(nc.vector.tensor_reduce(amax, src, AX.X, ALU.max, apply_absolute_value=True))
                link(nc.vector.tensor_scalar(scale, amax, 1.0 / 127.0, 1e-8, ALU.mult, ALU.max))
                link(nc.vector.reciprocal(inv, scale))
                for t in range(B):
                    ins = nc.vector.tensor_scalar(a3_y[:, t, :], src[:, t, :], inv[:, t:t + 1], ROUND, ALU.mult, ALU.add)
                link(ins)
                link(nc.vector.tensor_scalar(a3_y, a3_y, ROUND, 127.0, ALU.subtract, ALU.min))
                nc.vector.tensor_scalar(a3_xi, a3_y, -127.0, None, ALU.max).then_inc(sem("xi", k), 1)
                dve.wait_ge(sem("xi", k), 1)

            def whole_out(k):
                dve.wait_ge(sem("whole_mm", k), 1)
                for t in range(B):
                    ins = nc.vector.scalar_tensor_tensor(a3_y[:, t, :], ps[:, t // 2, (t % 2) * D:(t % 2 + 1) * D],
                                                         a3_s[:, k, 1, t:t + 1], wscale[:, k, :], ALU.mult, ALU.mult)
                return ins

            layer_norm(6)
            whole(xn[:, :, :], 0)
            whole_out(0).then_inc(sem("q3"), 1)
            dve.wait_ge(sem("q3"), 1)
            dve.wait_ge(sem("qp_zero"), 1)

            def q3p(b):
                if b >= 2:
                    dve.wait_ge(sem("q3_turn"), b - 1)
                nc.vector.tensor_tensor(a3_qp[:, b % 2, :, 0:DH3], a3_y[:, b, :].rearrange("p (h d) -> p h d", d=DH3),
                                        bq3[:, :].rearrange("p (h d) -> p h d", d=DH3), ALU.add).then_inc(sem("q3p"), 1)

            q3p(0)
            for b in range(B):
                if b + 1 < B:
                    q3p(b + 1)
                dve.wait_ge(sem("s3_mm"), b + 1)
                scores = ps[:, 0:4, :].rearrange("p i (g s) -> p (i g) s", s=S)
                link(nc.vector.tensor_reduce(a3_mx, scores, AX.X, ALU.max))
                if b >= 2:
                    dve.wait_ge(sem("p3_turn"), 2 * (b - 1))
                nc.vector.tensor_tensor(a3_p[:, b % 2, :, :], scores, a3_mx.unsqueeze(2).to_broadcast((P, H3, S)), ALU.subtract)\
                    .then_inc(sem("p3_arg"), 1)

                def out_3(b):
                    dve.wait_ge(sem("pv3_half"), 2 * (b + 1))
                    pv = ps[:, 7, 0:H3 * (DH3 + 1)].rearrange("p (h d) -> p h d", d=DH3 + 1)
                    link(nc.vector.reciprocal(a3_rc.unsqueeze(2), pv[:, :, DH3:DH3 + 1]))
                    for i in range(4):
                        ins = nc.vector.tensor_tensor(a3_o[:, b, :].rearrange("p (g i d) -> p i g d", i=4, d=DH3)[:, i, :, :],
                                                      pv[:, 4 * i:4 * i + 4, 0:DH3],
                                                      a3_rc[:, 4 * i:4 * i + 4].unsqueeze(2).to_broadcast((P, 4, DH3)), ALU.mult)
                    ins.then_inc(sem("o3"), 1)

                if b >= 1:
                    out_3(b - 1)
            out_3(B - 1)
            dve.wait_ge(sem("o3"), B)
            whole(a3_o, 1)
            link(whole_out(1))
            link(nc.vector.tensor_tensor(a3_y, a3_y, bp3[:, :].unsqueeze(1).to_broadcast((P, B, D)), ALU.add))
            flat = x[:, :, :].rearrange("p t d -> p (t d)")
            link(nc.vector.scalar_tensor_tensor(flat, a3_y.rearrange("p t d -> p (t d)"), tg[:, 3:4], flat, ALU.mult, ALU.add))
            layer_norm(7)
            x_lo(7, 3)
            make_tri()
            softmax(3)
            before(f_w[:, :, 0:E3])
            link(nc.vector.tensor_tensor(f_eq, f_cmp, f_w[:, :, 0:E3].unsqueeze(2).to_broadcast((P, B, E3, E3)), ALU.mult))
            link(nc.vector.tensor_reduce(f_rk, f_eq, AX.X, ALU.add))
            nc.vector.scalar_tensor_tensor(f_w[:, :, 0:E3], f_rk, TOP_P, f_w[:, :, 0:E3], ALU.is_le, ALU.mult)\
                .then_inc(sem("w_ready"), 1)
            ffn(3)
            nc.vector.tensor_copy(x[:, 0, 0:1], x[:, 0, 0:1]).then_inc(sem("x_done"), 1)


PIECES = []
for _i in range(NT0):
    _cuts = [e * F0 for e in range(E0 + 1) if _i * P < e * F0 < (_i + 1) * P] or [_i * P + P // 2]
    PIECES.append([(lo - _i * P, hi - _i * P, min(lo // F0, E0))
                   for lo, hi in ((_i * P, _cuts[0]), (_cuts[0], (_i + 1) * P))])


def pack_tiles(gate, up, down):
    f, d = gate.shape
    n = -(-f // P)

    def pad(m):
        return np.concatenate([m, np.zeros((n * P - f, d), m.dtype)])

    first = [pad(m).reshape(n, P, KD, P).transpose(0, 3, 2, 1).reshape(n, P, D) for m in (gate, up)]
    return np.ascontiguousarray(np.concatenate(first + [pad(down).reshape(n, P, D)], axis=2))


def feature_rows(m):
    return np.ascontiguousarray(m.reshape(KD, P, -1).transpose(1, 0, 2))


def by_feature(m):
    return m.transpose(0, 2, 1).reshape(-1, D)


def lay_out(inputs):
    i = {k: np.asarray(v) for k, v in inputs.items()}
    g = {"x": i["x"], "ctx": i["ctx_2048"], "mask": i["mask_BxS2_bk0"]}
    g["time_decay"] = np.ascontiguousarray(i["L0_xattn_time_decay"].reshape(KD, P).T)
    g["time_first"] = np.ascontiguousarray(i["L0_xattn_time_first"].reshape(KD, P).T)
    g["norm_w"] = np.ascontiguousarray(i["L1_ffn_norm_w"].reshape(KD, P).T)
    g["gates"] = np.concatenate([i["g_xattn"], i["g_ffn"]])
    g["temperature"] = i["L2_ffn_temperature"]
    g["wr"] = feature_rows(np.concatenate([i["L0_ffn_Wr"].T, i["L1_ffn_gate_w"].T, i["L2_ffn_Wr"],
                                           i["L3_ffn_router_w"].T], axis=1))
    g["w0"] = pack_tiles(np.concatenate([i["L0_ffn_Wg"].reshape(-1, D), i["L0_ffn_Wsg"]]),
                         np.concatenate([i["L0_ffn_Wu"].reshape(-1, D), i["L0_ffn_Wsu"]]),
                         np.concatenate([by_feature(i["L0_ffn_Wd"]), i["L0_ffn_Wsd"].T]))
    w13 = i["L1_ffn_w13"]
    g["w1"] = pack_tiles(np.concatenate([by_feature(w13[:, :, :F1]), i["L1_ffn_shared_gate_w"].T]),
                         np.concatenate([by_feature(w13[:, :, F1:]), i["L1_ffn_shared_up_w"].T]),
                         np.concatenate([i["L1_ffn_w2"].reshape(-1, D), i["L1_ffn_shared_down_w"]]))
    g["w2"] = pack_tiles(by_feature(i["L2_ffn_Wg"]), by_feature(i["L2_ffn_Wu"]), i["L2_ffn_Wd"].reshape(-1, D))
    g["w3"] = pack_tiles(i["L3_ffn_gate_w"].reshape(-1, D), i["L3_ffn_up_w"].reshape(-1, D), by_feature(i["L3_ffn_down_w"]))
    g["lora"] = np.ascontiguousarray(np.stack(
        [i["L2_ffn_Ga"].transpose(0, 2, 1), i["L2_ffn_Gb"], i["L2_ffn_Ua"].transpose(0, 2, 1), i["L2_ffn_Ub"],
         i["L2_ffn_Da"].transpose(0, 2, 1), i["L2_ffn_Db"]]).transpose(2, 1, 0, 3))
    g["wq2"] = feature_rows(i["L2_xattn_Wq"].T)
    both = np.concatenate([i["L2_xattn_Wk"], i["L2_xattn_Wv"]])
    g["wkv2"] = feature_rows(np.concatenate([both[0::2], both[1::2]]).T)
    g["wkv3"] = feature_rows(i["L3_xattn_wkv"].T)
    g["bkv3"] = i["L3_xattn_bkv"].reshape(1, -1)
    g["bq3"] = i["L3_xattn_bq"]
    g["bp3"] = i["L3_xattn_bp"]
    g["wqp3"] = np.ascontiguousarray(np.stack([i["L3_xattn_wq"], i["L3_xattn_wp"]]).reshape(2, KD, P, D).transpose(2, 0, 1, 3))
    return g


def kernel(**inputs):
    import concourse.bacc as _bacc
    from concourse.bass_utils import run_bass_kernel_spmd as _run

    nc = _bacc.Bacc("TRN2", target_bir_lowering=False, num_devices=1)
    arrays, aps = {}, {}
    for name, v in lay_out(inputs).items():
        arrays[f"in_{name}"] = v
        dt = U8 if v.dtype == np.bool_ else mybir.dt.from_np(v.dtype)
        aps[name] = nc.dram_tensor(f"in_{name}", v.shape, dt, kind="ExternalInput").ap()
    result = nc.dram_tensor("out_x", (B, S, D), F32, kind="ExternalOutput").ap()
    build(nc, aps, result)
    r = _run(nc, [arrays], core_ids=[0])
    return r.results[0]["out_x"]
```

```python
from contextlib import ExitStack

import numpy as np

import concourse.bass as bass
from concourse import mybir
from concourse.alu_op_type import AluOpType as ALU


F32 = mybir.dt.float32
F16 = mybir.dt.float16
BF16 = mybir.dt.bfloat16
U8 = mybir.dt.uint8
ACT = mybir.ActivationFunctionType
AX = mybir.AxisListType

P = 128
B, S, D = 8, 128, 256
T = B * S
KD = D // P
HALF = T // 2
SEG = S + 1
LN_EPS = 1e-5
RMS_EPS = 1e-6
FAR = -1e38

E0, F0, FS0 = 8, 176, 352
E1, F1 = 32, 128
E2, F2 = 8, 256
E3, F3 = 8, 512
NT0 = -(-(E0 * F0 + FS0) // P)
NT1 = E1 * F1 // P + 1
NT2 = E2 * F2 // P
NT3 = E3 * F3 // P
NT = (NT0, NT1, NT2, NT3)
EXPERTS = (E0, E1, E2, E3)
ROUTER_AT = (0, E0, E0 + E1, E0 + E1 + E2)
ROUTERS = E0 + E1 + E2 + E3
TOP0, TOP1 = 2, 4
CAPACITY = 2 * T * TOP1 // E1
WSCALE = 64.0
WROW = 3 * D
LORA_E, LORA_R = 2, 64
GOLDEN_CENTER = float(1.0 / np.e)
GOLDEN_LOWER = float(0.5 - np.log(4.0 / 3.0))
GOLDEN_UPPER = 0.5
TOP_P = 0.9
H2, DH2 = 32, 8
H3, DH3 = 16, 16
ROUND = 1.5 * 2.0 ** 23


def build(nc, a, out):
    with ExitStack() as ctx:
        def sb(name, shape, dt=F32):
            return ctx.enter_context(nc.sbuf_tensor(name, shape, dt))

        sems = {}

        def sem(name, k=None):
            key = name if k is None else f"{name}_{k}"
            if key not in sems:
                sems[key] = ctx.enter_context(nc.semaphore(key))
            return sems[key]

        ps = ctx.enter_context(nc.psum_tensor("ps", [P, 8, 512], F32))
        x = sb("x", [P, B, D])
        xn = sb("xn", [P, B, D])
        turned_buf = sb("turned_buf", [P, KD * B * SEG])
        xT = turned_buf[:, 0:KD * T].rearrange("p (c t) -> p c t", c=KD)
        x16 = turned_buf[:, 0:KD * T].bitcast(F16).rearrange("p (i c t) -> p i c t", i=2, c=KD)
        wk_k = turned_buf[:, :].rearrange("p (c b s) -> p c b s", c=KD, b=B)
        ctx_sb = sb("ctx_sb", [P, B, D])
        ctxT = sb("ctxT", [P, KD, B, SEG])
        ident = sb("ident", [P, P])
        ident16 = sb("ident16", [P, P], F16)
        identb = sb("identb", [P, P], BF16)
        gates = sb("gates", [P, 8])
        tg = sb("tg", [P, 8])
        tg_ffn = sb("tg_ffn", [P, 8])
        wr = sb("wr", [P, KD, ROUTERS])
        wr16 = sb("wr16", [P, 2, KD, ROUTERS], F16)
        normw = sb("normw", [P, KD])
        stats = sb("stats", [P, B, 6])
        mv = sb("mv", [P, B, 2])
        veps = sb("veps", [P, B])
        rstd = sb("rstd", [P, B])
        rms = sb("rms", [P, B])
        resid = sb("resid", [P, 2, B])
        mhalf = sb("mhalf", [P, B])
        ones = sb("ones", [P, P])
        W = sb("W", [P, 2, WROW])
        W16 = sb("W16", [P, 2, 2, WROW], F16)
        wb = sb("wb", [P, 2, T])
        td = sb("td", [P, KD])
        tf = sb("tf", [P, KD])
        wdec = sb("wdec", [P, KD])
        tinv = sb("tinv", [P, 1])
        mask8 = sb("mask8", [P, B, S], U8)
        k2T = sb("k2T", [P, B, H2 // 4, S], F16)
        v2 = sb("v2", [P, B, H2, DH2 + 1])
        k3T = sb("k3T", [P, B, H3 // 2, S], F16)
        v3 = sb("v3", [P, B, H3, DH3 + 1])
        wq2 = sb("wq2", [P, KD, D])
        wkv2 = sb("wkv2", [P, KD, 2 * D])
        wkv3 = sb("wkv3", [P, KD, 2 * D])
        bkv3 = sb("bkv3", [1, 2 * D])
        bq3 = sb("bq3", [P, D])
        bp3 = sb("bp3", [P, D])
        wi = sb("wi", [P, 2, KD, D], BF16)
        wscale = sb("wscale", [P, 2, D])
        k_raw = xn
        k_norm = sb("k_norm", [P, 3, B, H2])
        k_st = sb("k_st", [P, 2, H2, 4, DH2], F16)
        k_sq = k_st[:, 0, :, :, :].rearrange("p h i d -> p (h i d)").bitcast(F32).rearrange("p (k d) -> p k d", k=2)
        k3_raw = sb("k3_raw", [P, D])
        k3_st = sb("k3_st", [P, H3, 4, DH3], F16)
        ARENA = 16520
        arena = sb("arena", [P, ARENA])

        class Arena:
            def __init__(self):
                self.at = 0

            def take(self, shape, dt=F32, rows=P):
                n = 1
                for k in shape:
                    n *= k
                words = n if dt == F32 else (n + 1) // 2
                v = arena[0:rows, self.at:self.at + words]
                self.at += words
                assert self.at <= ARENA, self.at
                if dt != F32:
                    v = v.bitcast(dt)
                if len(shape) > 1:
                    names = "abcdef"[:len(shape)]
                    v = v.rearrange(f"p ({' '.join(names)}) -> p {' '.join(names)}",
                                    **{c: k for c, k in zip(names[1:], shape[1:])})
                return v

        routed = [nc.dram_tensor(f"routed_{L}", (EXPERTS[L] + 1, T), F32, kind="Internal").ap() for L in range(4)]
        LORA_T = LORA_E * F2 // P
        folded = nc.dram_tensor("folded", (LORA_T, P, WROW), F32, kind="Internal").ap()

        ar = Arena()
        LW = B * SEG
        wk_dec = ar.take([LW])
        wk_pp = ar.take([LW + 1])
        wk_aa = ar.take([LW + 1])
        wk_bb = ar.take([LW + 1])
        wk_d = ar.take([2, LW])
        wk_e = ar.take([KD, 4, LW])
        wk_ev = ar.take([2, LW])
        lora = W16[0:LORA_R, :, :, :].rearrange("p a b c -> p (a b c)").bitcast(F32)\
            .rearrange("p (k d) -> p k d", d=D)
        fold = W[:, 0, :]
        fold_add = W[:, 1, :]
        wq_s = sb("wq_s", [P, 3, 4])
        wq_f = wb[:, 0, :].rearrange("p (w o d) -> p w o d", w=2, o=KD)
        wq_i = wb[:, 1, 0:HALF].bitcast(BF16).rearrange("p (w o d) -> p w o d", w=2, o=KD)
        wq_diag = wb[:, 1, HALF:T].rearrange("p (k o) -> p k o", k=4)

        ar = Arena()
        a1_mask = ar.take([B, S])
        a1_neg = ar.take([B, S])
        a1_p = ar.take([B, S])
        a1_pT = ar.take([B, S])
        a1_s = ar.take([6, B])

        ar = Arena()
        f_s = ar.take([2, HALF])
        f_g = ar.take([2, HALF])
        f_h = ar.take([2, HALF])
        f_h16 = ar.take([2, 2, T], F16)
        f_lg = ar.take([B, E1])
        f_w = ar.take([B, E1])
        f_s8 = ar.take([6, B])
        f_wT = ar.take([T], rows=E1)
        f_cmp = ar.take([B, E0, E0])
        f_eq = ar.take([B, E0, E0])
        f_tri = ar.take([E0, E0])
        f_rk = ar.take([B, E0])
        f_a = ar.take([B, E0])
        f_b = ar.take([B, E0])
        m_x = ar.take([B, E1 + 8])
        m_rep = ar.take([B, E1 + 8])
        m_top = ar.take([B, 8])
        m_sel = ar.take([B, E1])
        m_last = ar.take([B, E1])
        m_raw = ar.take([T], rows=E1)
        m_selT = ar.take([T], rows=E1)
        m_cum = ar.take([T], rows=E1)
        m_zero = ar.take([T], rows=E1)
        m_dropT = ar.take([T], rows=E1)
        m_lastT = ar.take([T], rows=E1)
        m_xs = ar.take([KD, E1, 2], F16)
        m_gu = ar.take([2])
        m_ss = ar.take([1])
        m_hs = ar.take([1])
        m_hs16 = ar.take([2, 2], F16)
        m_rT = ar.take([KD, E1])
        m_r = ar.take([D], rows=E1)
        x_rms = xn

        ar = Arena()
        a2_q = ar.take([B, H2, DH2])
        a2_st = ar.take([B, H2, 4, DH2], F16)
        a2_qT = ar.take([2, H2 // 4, S], F16)
        a2_p = ar.take([2, 2, 4, S])
        a2_n = ar.take([3, 256])
        a2_p16 = ar.take([2, 2, 2, 4, S], F16)
        v2_16 = ar.take([B, H2, 2, DH2 + 1], F16)
        a2_t = ar.take([2, H2 // 2, DH2 + 1])
        a2_o = ar.take([H2 // 2, DH2])
        a2_rc = ar.take([2, H2 // 2])

        ar = Arena()
        a3_y = ar.take([B, D])
        a3_o = ar.take([B, D])
        v3_16 = ar.take([B, H3, 2, DH3 + 1], F16)
        at_whole = ar.at
        a3_s = ar.take([2, 3, B])
        a3_st = ar.take([2, H3, 4, DH3], F16)
        a3_qT = ar.take([2, H3 // 2, S], F16)
        a3_p = ar.take([2, H3, S])
        a3_pT = ar.take([2, H3, S], F16)
        a3_mx = ar.take([H3])
        a3_t = ar.take([2, 8, DH3 + 1])
        a3_rc = ar.take([2, 8])
        ar.at = 2 * B * D
        a3_xi = ar.take([B, D], BF16)
        a3_xiT = ar.take([KD, T], BF16)
        assert ar.at <= at_whole

        block = ctx.enter_context(nc.Block())

        def bank(k):
            return ps[:, k, :]

        def seq_heads(k):
            return ps[:, k, :].bitcast(F16)

        KEYS_BEFORE = (2, 6)
        K2_ORDER = (0, 4, 1, 5, 2, 6, 3, 7)
        TURNS = [(NT[L] - 2) // 2 for L in range(4)]
        MID_TURNS = TURNS[:3] + [TURNS[3] - 1]

        def tiles(L):
            return sum(NT[:L])

        def halves(L):
            return 2 * tiles(L)

        def slot_tiles(L, slot):
            return sum((NT[m] + 1 - slot) // 2 for m in range(L))

        def wb_loads(L, slot):
            return slot_tiles(L, slot) + (slot_tiles(1, slot) if L else 0)

        def at(n, j, per=2):
            return n if j is None else per * j + n

        def wT_copied(L):
            return 2 * (L if L else 1)

        def turns_before(s):
            return s if s < 7 else 6

        @block.sync
        def _(sp):
            sp.dma_start(x[:, :, :], a["x"].rearrange("b s d -> s b d")).then_inc(sem("x_in"), 16)
            sp.dma_start(td[:, :], a["time_decay"]).then_inc(sem("small_in"), 16)
            sp.dma_start(tf[:, :], a["time_first"]).then_inc(sem("small_in"), 16)
            sp.dma_start(gates[:, :], a["gates"].partition_broadcast(P)).then_inc(sem("small_in"), 16)
            sp.dma_start(tinv[:, :], a["temperature"].partition_broadcast(P)).then_inc(sem("small_in"), 16)
            sp.dma_start(normw[:, :], a["norm_w"]).then_inc(sem("small_in"), 16)
            sp.dma_start(ctx_sb[:, :, :], a["ctx"].rearrange("b s d -> s b d")).then_inc(sem("ctx_in"), 16)
            sp.dma_start(wkv2[:, :, :], a["wkv2"]).then_inc(sem("kv_in"), 16)
            sp.dma_start(wkv3[:, :, :], a["wkv3"]).then_inc(sem("kv_in"), 16)
            sp.dma_start(bkv3[:, :], a["bkv3"]).then_inc(sem("kv_in"), 16)
            sp.dma_start(wq_f, a["wqp3"]).then_inc(sem("wqp_in"), 16)
            for k in range(LORA_T):
                if k:
                    sp.wait_ge(sem("folded_out"), 16 * k)
                if k % (F2 // P) == 0:
                    if k:
                        sp.wait_ge(sem("fold_mm"), k)
                    sp.dma_start(lora[:, :, :], a["lora"][:, k * P // F2]).then_inc(sem("lora_in"), 16)
                sp.dma_start(fold, a["w2"][k]).then_inc(sem("fold_in"), 16)
                sp.wait_ge(sem("fold_sum"), k + 1)
                sp.dma_start(folded[k], fold).then_inc(sem("folded_out"), 16)
            sp.wait_ge(sem("folded_out"), 16 * LORA_T)
            sp.dma_start(wr[:, :, :], a["wr"]).then_inc(sem("late_in"), 16)
            sp.dma_start(wq2[:, :, :], a["wq2"]).then_inc(sem("late_in"), 16)
            sp.dma_start(bq3[:, :], a["bq3"].partition_broadcast(P)).then_inc(sem("late_in"), 16)
            sp.dma_start(bp3[:, :], a["bp3"].partition_broadcast(P)).then_inc(sem("late_in"), 16)
            sp.dma_start(mask8[:, :, :].rearrange("p b s -> p (b s)"),
                         a["mask"].rearrange("b s -> (b s)").partition_broadcast(P)).then_inc(sem("late_in"), 16)

            sp.wait_ge(sem("ones"), 1)
            for L in range(2):
                sp.dma_start(routed[L][EXPERTS[L]].rearrange("(p k) -> p k", p=P), ones[:, 0:T // P]).then_inc(sem("ones_out"), 16)
            sp.wait_ge(sem("ones_out"), 16 * 2)

            def source(L, i):
                return folded[i] if L == 2 and i < LORA_T else a[f"w{L}"][i]

            def head_loads(L):
                for i in range(2):
                    if L > 0:
                        sp.wait_ge(sem("wd_lo"), tiles(L) - (NT[L - 1] + 1 - i) % 2)
                    sp.dma_start(W[:, i, :], source(L, i)).then_inc(sem("w_in", i), 16)

            def routed_out(L):
                if L == 1:
                    sp.wait_ge(sem("by_expert"), 2)
                else:
                    sp.wait_ge(sem("wT_half"), wT_copied(L))
                sp.dma_start(routed[L][0:EXPERTS[L], :], f_wT[0:EXPERTS[L], :]).then_inc(sem("routed_out"), 16)
                sp.wait_ge(sem("routed_out"), 16 * (L + 1))

            def w_load(src, slot, before):
                sp.wait_ge(sem("wd_lo"), before)
                sp.dma_start(W[:, slot, :], src).then_inc(sem("w_in", slot), 16)

            def wb_load(L, row, slot, before):
                sp.wait_ge(sem("h_full"), before)
                sp.dma_start(wb[:, slot, :], routed[L][row].partition_broadcast(P))\
                    .then_inc(sem("wb_in", slot), 16)

            def tile_loads(L, i, row, e=None, per=0):
                if e is None:
                    src, before = source(L, i), tiles(L) + i - 1
                    twice = 2 * before
                else:
                    src, before = a[f"w{L}"][e * per + i], e * per + (tiles(L) + i - 1)
                    twice = e * (2 * per) + 2 * (tiles(L) + i - 1)
                if e is not None or i >= 2:
                    w_load(src, i % 2, before)
                wb_load(L, row, i % 2, twice)

            def loads_0():
                sp.wait_ge(sem("wi"), 2)
                for i in range(NT0):
                    if i >= 2:
                        w_load(a["w0"][i], i % 2, i - 1)
                        sp.wait_ge(sem("h_full"), 2 * i - 2)
                    for lo, hi, row in PIECES[i]:
                        sp.dma_start(wb[lo:hi, i % 2, :], routed[0][row].partition_broadcast(hi - lo))\
                            .then_inc(sem("wb_in", i % 2), 16)

            def loads_1():
                for i in range(2):
                    tile_loads(1, i, i)
                with sp.Fori(1, E1 // 2) as e:
                    for k in range(2):
                        tile_loads(1, k, 2 * e + k, e, 2)
                tile_loads(1, E1, E1)

            def loads_2():
                for i in range(LORA_T):
                    tile_loads(2, i, i // 2)
                with sp.Fori(LORA_T // 2, E2) as e:
                    for k in range(2):
                        tile_loads(2, k, e, e, 2)

            def loads_3():
                per = F3 // P
                for i in range(per):
                    tile_loads(3, i, 0)
                with sp.Fori(1, E3) as e:
                    for k in range(per):
                        tile_loads(3, k, e, e, per)

            for L, loads in enumerate((loads_0, loads_1, loads_2, loads_3)):
                head_loads(L)
                routed_out(L)
                loads()

            for h in range(2):
                sp.wait_ge(sem("x_done"), h + 1)
                sp.dma_start(out.rearrange("b s d -> s b d")[:, 4 * h:4 * h + 4, :], x[:, 4 * h:4 * h + 4, :])\
                    .then_inc(sem("out_done"), 16)
            sp.wait_ge(sem("out_done"), 16 * 2)
            sp.wait_ge(sem("late_in"), 16 * 5)

        @block.gpsimd
        def _(pool):
            steps = [0]

            def link(ins):
                steps[0] += 1
                ins.then_inc(sem("pool_step"), 1)
                pool.wait_ge(sem("pool_step"), steps[0])

            link(nc.gpsimd.memset(ident[:, :], 0.0))
            nc.gpsimd.affine_select(out=ident[:, :], in_=ident[:, :], compare_op=ALU.not_equal, fill=1.0,
                                    base=0, pattern=[[-1, P]], channel_multiplier=1).then_inc(sem("ident"), 1)
            nc.gpsimd.memset(mhalf[:, :], -0.5).then_inc(sem("mhalf"), 1)
            nc.gpsimd.memset(ctxT[:, :, :, 0:1], 0.0).then_inc(sem("wkv_edges"), 1)
            nc.gpsimd.memset(wk_k[:, :, :, 0:1], FAR).then_inc(sem("wkv_edges"), 1)
            nc.gpsimd.memset(wk_pp[:, 0:1], 0.0).then_inc(sem("wkv_edges"), 1)
            nc.gpsimd.memset(wk_aa[:, 0:1], 0.0).then_inc(sem("wkv_edges"), 1)
            nc.gpsimd.memset(wk_bb[:, 0:1], 1.0).then_inc(sem("wkv_edges"), 1)
            pool.wait_ge(sem("ident"), 1)
            nc.gpsimd.tensor_copy(ident16[:, :], ident[:, :]).then_inc(sem("ident"), 1)
            nc.gpsimd.tensor_copy(identb[:, :], ident[:, :]).then_inc(sem("ident"), 1)
            nc.gpsimd.memset(ones[:, :], 1.0).then_inc(sem("ones"), 1)
            nc.gpsimd.memset(v2[:, :, :, DH2:DH2 + 1], 1.0).then_inc(sem("v_ones"), 1)
            nc.gpsimd.memset(v3[:, :, :, DH3:DH3 + 1], 1.0).then_inc(sem("v_ones"), 1)

            def inv_sqrt(s):
                for h in range(2):
                    sl = slice(4 * h, 4 * h + 4)
                    pool.wait_ge(sem("ln_var"), 2 * s + h + 1)
                    if s == 0 and h == 0:
                        pool.wait_ge(sem("mhalf"), 1)
                    ins = nc.gpsimd.tensor_tensor(rstd[:, sl], veps[:, sl], mhalf[:, sl], ALU.pow)
                    if s == 3:
                        link(ins)
                        link(nc.gpsimd.tensor_tensor(rms[:, sl], mv[:, sl, 1], rstd[:, sl], ALU.mult))
                        link(nc.gpsimd.tensor_tensor(rms[:, sl], rms[:, sl], rstd[:, sl], ALU.mult))
                        link(nc.gpsimd.tensor_scalar(rms[:, sl], rms[:, sl], 1.0, RMS_EPS, ALU.mult, ALU.add))
                        link(nc.gpsimd.tensor_tensor(rms[:, sl], rms[:, sl], mhalf[:, sl], ALU.pow))
                        ins = nc.gpsimd.tensor_tensor(rms[:, sl], rms[:, sl], rstd[:, sl], ALU.mult)
                    ins.then_inc(sem("ln_rstd"), 1)

            def wkv(c):
                pool.wait_ge(sem("wkv_exp"), 4 * c + 3)
                pool.wait_ge(sem("ctxT_ready"), 4)
                if c:
                    pool.wait_ge(sem("wkv_y"), c)
                v = ctxT[:, c, :, :].rearrange("p b s -> p (b s)")
                for k, e in ((0, 1), (1, 2)):
                    nc.gpsimd.tensor_tensor(wk_ev[:, k, :], wk_e[:, c, e, :], v, ALU.mult)\
                        .then_inc(sem("wkv_ev"), 1)

            def fold_lora(k):
                pool.wait_ge(sem("fold_in"), 16 * (k + 1))
                pool.wait_ge(sem("fold_add"), 2 * (k + 1))
                nc.gpsimd.tensor_tensor(fold, fold, fold_add, ALU.add).then_inc(sem("fold_sum"), 1)

            def scale_diagonals():
                pool.wait_ge(sem("wq_scale"), 1)
                for k in range(4):
                    ins = nc.gpsimd.tensor_scalar(wq_diag[:, k, :], ident[:, :], wq_s[:, 1, k:k + 1], None, ALU.mult)
                ins.then_inc(sem("wq_diag"), 1)

            def keys(b):
                sq = k_sq[:, b % 2, :].rearrange("p (h d) -> p h d", d=DH2)
                ms = k_norm[:, 0, b, :]
                pool.wait_ge(sem("k2_raw"), 2 * (b + 1))
                for n in (4, 2):
                    link(nc.gpsimd.tensor_tensor(sq[:, :, 0:n], sq[:, :, 0:n], sq[:, :, n:2 * n], ALU.add))
                link(nc.gpsimd.tensor_tensor(ms.unsqueeze(2), sq[:, :, 0:1], sq[:, :, 1:2], ALU.add))
                nc.gpsimd.tensor_scalar(ms, ms, 1.0 / DH2, RMS_EPS, ALU.mult, ALU.add).then_inc(sem("k2_ms"), 1)
                pool.wait_ge(sem("k3_raw"), 3 * (b + 1))
                for i in (1, 3):
                    nc.gpsimd.tensor_tensor(k3_st[:, :, i, :], k3_raw[:, :].rearrange("p (h d) -> p h d", d=DH3),
                                            k3_st[:, :, i - 1, :], ALU.subtract).then_inc(sem("k3_split"), 1)

            def refine_norms():
                ms, guess, t = (k_norm[:, i, :, :] for i in range(3))
                pool.wait_ge(sem("k2_guess"), 1)
                link(nc.gpsimd.tensor_tensor(t, guess, guess, ALU.mult))
                link(nc.gpsimd.tensor_tensor(t, t, ms, ALU.mult))
                link(nc.gpsimd.tensor_scalar(t, t, -0.5, 1.5, ALU.mult, ALU.add))
                nc.gpsimd.tensor_tensor(t, t, guess, ALU.mult).then_inc(sem("k2_scale"), 1)
                pool.wait_ge(sem("k2_scale"), 1)

            def norm_k2(b):
                raw = k_raw[:, b, :].rearrange("p (h d) -> p h d", d=DH2)
                nc.gpsimd.tensor_tensor(raw, raw, k_norm[:, 2, b, :].unsqueeze(2).to_broadcast((P, H2, DH2)), ALU.mult)\
                    .then_inc(sem("k2_norm"), 1)

            def lo_k2(b):
                raw = k_raw[:, b, :].rearrange("p (h d) -> p h d", d=DH2)
                pool.wait_ge(sem("k2_hi"), 2 * (K2_ORDER.index(b) + 1))
                for i in (1, 3):
                    nc.gpsimd.tensor_tensor(k_st[:, 0, :, i, :], raw, k_st[:, 0, :, i - 1, :], ALU.subtract)\
                        .then_inc(sem("k2_split"), 1)

            def weigh(L, k, half, j=None):
                loads = 32 if L == 0 else 16
                arrived = 16 * wb_loads(L, k % 2) + loads * (k // 2 + 1)
                n = halves(L) + 2 * k + half + 1
                pool.wait_ge(sem("gated"), at(n, j, 4))
                if half == 0:
                    pool.wait_ge(sem("wb_in", k % 2), at(arrived, j, loads))
                if tiles(L) + k:
                    pool.wait_ge(sem("h_lo"), at(n - 2, j, 4))
                nc.gpsimd.tensor_tensor(f_h[:, half, :], f_g[:, half, :], wb[:, k % 2, half * HALF:(half + 1) * HALF],
                                        ALU.mult).then_inc(sem("h_full"), 1)

            def ffn(L):
                for k in range(2):
                    for half in range(2):
                        weigh(L, k, half)
                with pool.Fori(0, TURNS[L]) as j:
                    for k in (2, 3):
                        for half in range(2):
                            weigh(L, k, half, j)
                if NT[L] % 2:
                    for half in range(2):
                        weigh(L, NT[L] - 1, half)

            inv_sqrt(0)
            for b in range(B):
                if b in KEYS_BEFORE:
                    wkv(KEYS_BEFORE.index(b))
                keys(b)
                if b % 2:
                    fold_lora(b // 2)
            scale_diagonals()
            refine_norms()
            norm_k2(0)
            for b in range(B // 2):
                if b + 1 < B // 2:
                    norm_k2(b + 1)
                lo_k2(b)
            inv_sqrt(1)
            ffn(0)
            pool.wait_ge(sem("late_in"), 16 * 5)
            inv_sqrt(2)
            link(nc.gpsimd.tensor_copy(a1_mask, mask8[:, :, :]))
            nc.gpsimd.tensor_scalar(a1_neg, a1_mask, -1.0, 1e30, ALU.add, ALU.mult).then_inc(sem("mask"), 1)
            inv_sqrt(3)
            ffn(1)
            inv_sqrt(4)
            for b in range(B):
                pool.wait_ge(sem("q2_hi"), b + 1)
                nc.gpsimd.tensor_tensor(a2_st[:, b, :, 3, :], a2_q[:, b, :, :], a2_st[:, b, :, 0, :], ALU.subtract)\
                    .then_inc(sem("q2_lo_pool"), 1)
                pool.wait_ge(sem("v2_hi"), 1)
                nc.gpsimd.tensor_tensor(v2_16[:, b, :, 1, :], v2[:, b, :, :], v2_16[:, b, :, 0, :], ALU.subtract)\
                    .then_inc(sem("v2_lo"), 1)
            for m in range(2 * B):
                b, hg = m // 2, m % 2
                xs = x[:, b, hg * P:(hg + 1) * P]
                pool.wait_ge(sem("o2_rc"), m + 1)
                link(nc.gpsimd.tensor_scalar(a2_rc[:, m % 2, :], a2_rc[:, m % 2, :], tg[:, 2:3], None, ALU.mult))
                link(nc.gpsimd.tensor_tensor(a2_o, a2_t[:, m % 2, :, 0:DH2],
                                             a2_rc[:, m % 2, :].unsqueeze(2).to_broadcast((P, H2 // 2, DH2)), ALU.mult))
                nc.gpsimd.tensor_tensor(xs, a2_o.rearrange("p h d -> p (h d)"), xs, ALU.add).then_inc(sem("x_2"), 1)
                pool.wait_ge(sem("x_2"), m + 1)
            inv_sqrt(5)
            ffn(2)
            inv_sqrt(6)
            link(nc.gpsimd.tensor_scalar(bp3[:, :], bp3[:, :], tg[:, 3:4], None, ALU.mult))
            pool.wait_ge(sem("xn_ready"), B * 7)
            nc.gpsimd.tensor_tensor(x[:, :, :], x[:, :, :], bp3[:, :].unsqueeze(1).to_broadcast((P, B, D)), ALU.add)\
                .then_inc(sem("x_bias"), 1)

            def q3_lo(b):
                pool.wait_ge(sem("q3_hi"), 2 * (b + 1))
                for i in (2, 3):
                    nc.gpsimd.tensor_tensor(a3_st[:, b % 2, :, i, :], a3_y[:, b, :].rearrange("p (h d) -> p h d", d=DH3),
                                            a3_st[:, b % 2, :, i - 2, :], ALU.subtract).then_inc(sem("q3_lo"), 1)

            q3_lo(0)
            q3_lo(1)
            pool.wait_ge(sem("v3_hi"), 1)
            nc.gpsimd.tensor_tensor(v3_16[:, :, :, 1, :], v3[:, :, :, :], v3_16[:, :, :, 0, :], ALU.subtract)\
                .then_inc(sem("v3_lo"), 1)
            q3_lo(2)

            def out_3(b, i):
                pool.wait_ge(sem("o3_rc"), 2 * b + i + 1)
                nc.gpsimd.tensor_tensor(a3_o[:, b, :].rearrange("p (j i d) -> p i j d", i=2, d=DH3)[:, i, :, :],
                                        a3_t[:, i, :, 0:DH3], a3_rc[:, i, :].unsqueeze(2).to_broadcast((P, 8, DH3)),
                                        ALU.mult).then_inc(sem("a3_o"), 1)

            for b in range(B):
                if b:
                    out_3(b - 1, 1)
                if b + 3 < B:
                    q3_lo(b + 3)
                out_3(b, 0)
            out_3(B - 1, 1)
            inv_sqrt(7)
            ffn(3)

        @block.scalar
        def _(act):
            act.wait_ge(sem("small_in"), 16 * 5)
            nc.scalar.activation(tg[:, :], gates[:, :], ACT.Tanh).then_inc(sem("tg"), 1)
            nc.scalar.activation(wdec[:, :], td[:, :], ACT.Exp).then_inc(sem("decay"), 1)

            def turned(s, dst, scale=None):
                for half in range(2):
                    act.wait_ge(sem("turn"), 2 * turns_before(s) + half + 1)
                    for c in range(KD):
                        src = bank(2 * c + half)
                        o = dst(c, half)
                        if len(o.shape) == 3:
                            src = src.rearrange("p (b s) -> p b s", b=B // 2)
                        nc.scalar.activation(o, src, ACT.Copy, scale=1.0 if scale is None else scale(c))\
                            .then_inc(sem("turned"), 1)

            def turned_16(s, scale=None):
                for half in range(2):
                    act.wait_ge(sem("turn"), 2 * turns_before(s) + half + 1)
                    for c in range(KD):
                        nc.scalar.activation(x16[:, 0, c, half * HALF:(half + 1) * HALF], bank(2 * c + half), ACT.Copy,
                                             scale=1.0 if scale is None else scale(c)).then_inc(sem("turned"), 1)

            def xT_of(c, half):
                return xT[:, c, half * HALF:(half + 1) * HALF]

            def seg_of(t):
                return lambda c, half: t[:, c, half * (B // 2):(half + 1) * (B // 2), 1:SEG]

            act.wait_ge(sem("wkv_edges"), 5)
            for half in range(2):
                act.wait_ge(sem("ctxT_turn"), half + 1)
                for c in range(KD):
                    nc.scalar.activation(seg_of(ctxT)(c, half), bank(4 + 2 * c + half).rearrange("p (b s) -> p b s", b=B // 2),
                                         ACT.Copy).then_inc(sem("ctxT_ready"), 1)
            turned(0, seg_of(wk_k))

            def wkv_exp(c):
                for k, scale in ((0, 1.0), (1, -1.0), (2, 1.0), (3, -1.0)):
                    act.wait_ge(sem("wkv_arg"), 4 * c + k + 1)
                    nc.scalar.activation(wk_e[:, c, k, :], wk_e[:, c, k, :], ACT.Exp, scale=scale)\
                        .then_inc(sem("wkv_exp"), 1)

            act.wait_ge(sem("v_ones"), 2)

            def k2_guess():
                ms, guess, log = (k_norm[:, i, :, :] for i in range(3))
                act.wait_ge(sem("k2_ms"), B)
                nc.scalar.activation(log, ms, ACT.Ln).then_inc(sem("k2_log"), 1)
                act.wait_ge(sem("k2_log"), 1)
                nc.scalar.activation(guess, log, ACT.Exp, scale=-0.5).then_inc(sem("k2_guess"), 1)

            def k2_hi(n):
                b = K2_ORDER[n]
                if n % 2 == 0:
                    act.wait_ge(sem("k2_norm"), b + 1)
                else:
                    act.wait_ge(sem("k2_norm_dve"), b - B // 2 + 1)
                if n >= 2:
                    act.wait_ge(sem("k2_turn"), n - 1)
                for i in (0, 2):
                    nc.scalar.activation(k_st[:, n % 2, :, i, :], k_raw[:, b, :].rearrange("p (h d) -> p h d", d=DH2),
                                         ACT.Copy).then_inc(sem("k2_hi"), 1)

            def fold_copy(k):
                act.wait_ge(sem("fold_mm"), k + 1)
                if k:
                    act.wait_ge(sem("fold_sum"), k)
                    act.wait_ge(sem("folded_out"), 16 * k)
                nc.scalar.activation(fold_add[:, 0:2 * D], bank(0), ACT.Copy).then_inc(sem("fold_add"), 1)
                nc.scalar.activation(fold_add[:, 2 * D:3 * D], ps[:, 1, 0:D], ACT.Copy).then_inc(sem("fold_add"), 1)

            def k3_out(b):
                act.wait_ge(sem("k3_turn"), b + 1)
                nc.scalar.activation(k3T[:, b, :, :].rearrange("p g s -> p (g s)"), seq_heads(4), ACT.Copy)\
                    .then_inc(sem("k3_ready"), 1)

            def k2_out(n):
                b = K2_ORDER[n]
                act.wait_ge(sem("k2_turn"), n + 1)
                nc.scalar.activation(k2T[:, b, :, :].rearrange("p g s -> p (g s)"), seq_heads(7 - n % 2), ACT.Copy)\
                    .then_inc(sem("k2_ready"), 1)

            for b in range(B):
                sl = b % 2
                if b in KEYS_BEFORE:
                    wkv_exp(KEYS_BEFORE.index(b))
                act.wait_ge(sem("kv2_mm"), b + 1)
                if b >= 2:
                    act.wait_ge(sem("k2_ms"), b - 1)
                nc.scalar.activation(k_sq[:, sl, :], ps[:, 6, 0:D], ACT.Square).then_inc(sem("k2_raw"), 1)
                nc.scalar.activation(k_raw[:, b, :], ps[:, 6, 0:D], ACT.Copy).then_inc(sem("k2_raw"), 1)
                nc.scalar.activation(v2[:, b, :, 0:DH2], ps[:, 6, D:2 * D].rearrange("p (h d) -> p h d", d=DH2), ACT.Copy)\
                    .then_inc(sem("v2_out"), 1)
                act.wait_ge(sem("kv3_mm"), b + 1)
                if b >= 1:
                    act.wait_ge(sem("k3_turn"), b)
                nc.scalar.activation(k3_raw[:, :], ps[:, 5, 0:D], ACT.Copy).then_inc(sem("k3_raw"), 1)
                for i in (0, 2):
                    nc.scalar.activation(k3_st[:, :, i, :], ps[:, 5, 0:D].rearrange("p (h d) -> p h d", d=DH3), ACT.Copy)\
                        .then_inc(sem("k3_raw"), 1)
                nc.scalar.activation(v3[:, b, :, 0:DH3], ps[:, 5, D:2 * D].rearrange("p (h d) -> p h d", d=DH3), ACT.Copy)\
                    .then_inc(sem("v3_out"), 1)
                if b >= 1:
                    k3_out(b - 1)
                if b % 2:
                    fold_copy(b // 2)
            k3_out(B - 1)
            k2_guess()
            act.wait_ge(sem("wi_turn"), 1)
            nc.scalar.activation(wi[:, :, :, :].rearrange("p a b c -> p (a b c)"), ps[:, 2, :].bitcast(BF16), ACT.Copy)\
                .then_inc(sem("wi"), 1)
            act.wait_ge(sem("wscale_mm"), 1)
            nc.scalar.activation(wscale[:, :, :].rearrange("p a b -> p (a b)"), bank(3), ACT.Copy).then_inc(sem("wi"), 1)
            for b in range(B):
                k2_hi(b)
                if b:
                    k2_out(b - 1)
            k2_out(B - 1)

            def router_exp(L):
                n = EXPERTS[L]
                act.wait_ge(sem("router_arg"), min(L, 2) + 1)
                nc.scalar.activation(f_lg[:, :, 0:n], f_lg[:, :, 0:n], ACT.Exp).then_inc(sem("router_exp"), 1)

            def wT_copy(L):
                n = EXPERTS[L]
                act.wait_ge(sem("w_turn"), L + 1)
                dst = m_raw if L == 1 else f_wT
                for h in range(2):
                    nc.scalar.activation(dst[0:n, h * HALF:(h + 1) * HALF], ps[0:n, 5 + h, :], ACT.Copy)\
                        .then_inc(sem("wT_out" if L == 1 else "wT_half"), 1)

            def silu(L, k, half, j=None):
                n = halves(L) + 2 * k + half + 1
                act.wait_ge(sem("gu_done"), at(n, j, 4))
                if tiles(L) + k:
                    act.wait_ge(sem("gated"), at(n - 2, j, 4))
                nc.scalar.activation(f_s[:, half, :], bank(half), ACT.Silu, scale=1.0 / WSCALE).then_inc(sem("silu_done"), 1)

            def gu_hi(L, k, j=None):
                act.wait_ge(sem("w_in", k % 2), at(16 * (slot_tiles(L, k % 2) + k // 2 + 1), j, 16))
                if tiles(L) + k >= 2:
                    act.wait_ge(sem("gu_done"), at(halves(L) + 2 * k - 2, j, 4))
                    if L == 1 and k >= 2:
                        act.wait_ge(sem("star_mm"), at(k - 1, j))
                nc.scalar.activation(W16[:, k % 2, 0, 0:2 * D], W[:, k % 2, 0:2 * D], ACT.Copy, scale=WSCALE)\
                    .then_inc(sem("wgu_hi"), 1)

            def down_hi(L, k, j=None):
                if tiles(L) + k >= 2:
                    act.wait_ge(sem("down_done"), at(tiles(L) + k - 1, j))
                nc.scalar.activation(W16[:, k % 2, 0, 2 * D:3 * D], W[:, k % 2, 2 * D:3 * D], ACT.Copy, scale=WSCALE)\
                    .then_inc(sem("wd_hi"), 1)

            def h_hi(L, k, half, j=None):
                act.wait_ge(sem("h_full"), at(halves(L) + 2 * k + half + 1, j, 4))
                if tiles(L) + k >= 2 and half == 0:
                    act.wait_ge(sem("down_done"), at(tiles(L) + k - 1, j))
                nc.scalar.activation(f_h16[:, k % 2, 0, half * HALF:(half + 1) * HALF], f_h[:, half, :], ACT.Copy)\
                    .then_inc(sem("h_hi"), 1)

            def tile(L, k, j=None, last=False, meanwhile=None):
                down_hi(L, k, j)
                silu(L, k, 0, j)
                if meanwhile:
                    silu(L, k, 1, j)
                    meanwhile()
                if not last:
                    gu_hi(L, k + 1, j)
                h_hi(L, k, 0, j)
                if L == 1 and meanwhile:
                    last_slots_hi()
                if not meanwhile:
                    silu(L, k, 1, j)
                if L == 1 and k < E1:
                    silu_star(k, j)
                h_hi(L, k, 1, j)

            def last_slots_hi():
                act.wait_ge(sem("xs_mm"), 1)
                for c in range(KD):
                    nc.scalar.activation(m_xs[:, c, :, 0], ps[:, 6, c * E1:(c + 1) * E1], ACT.Copy, scale=normw[:, c:c + 1])\
                        .then_inc(sem("xs_hi"), 1)

            def silu_star(k, j=None):
                n = k + 1
                act.wait_ge(sem("star_read"), at(n, j))
                if k >= 1:
                    act.wait_ge(sem("star_done"), at(n - 1, j))
                nc.scalar.activation(m_ss, m_gu[:, 0:1], ACT.Silu, scale=1.0 / WSCALE).then_inc(sem("star_silu"), 1)

            def ffn(L):
                def meanwhile():
                    wT_copy(L)
                    if L == 1:
                        for h, bk in ((0, 7), (1, 4)):
                            nc.scalar.activation(m_selT[:, h * HALF:(h + 1) * HALF], ps[0:E1, bk, :], ACT.Copy)\
                                .then_inc(sem("wT_out"), 1)
                        act.wait_ge(sem("last_turn"), 1)
                        nc.scalar.activation(m_last, ps[:, 5, 0:B * E1].rearrange("p (t e) -> p t e", e=E1), ACT.Copy)\
                            .then_inc(sem("last_out"), 1)

                tile(L, 0, meanwhile=meanwhile)
                tile(L, 1)
                with act.Fori(0, MID_TURNS[L]) as j:
                    tile(L, 2, j)
                    tile(L, 3, j)
                for k in range(2 + 2 * MID_TURNS[L], NT[L]):
                    tile(L, k, last=(k == NT[L] - 1))

            act.wait_ge(sem("late_in"), 16 * 5)
            nc.scalar.activation(wr16[:, 0, :, :], wr[:, :, :], ACT.Copy).then_inc(sem("wr_hi"), 1)
            gu_hi(0, 0)
            turned_16(1)
            router_exp(0)
            ffn(0)
            turned(2, xT_of)
            for h in range(2):
                sl = slice(4 * h, 4 * h + 4)
                act.wait_ge(sem("a1_arg"), h + 1)
                nc.scalar.activation(a1_p[:, sl, :], a1_p[:, sl, :], ACT.Exp).then_inc(sem("a1_p"), 1)
                act.wait_ge(sem("a1_turn"), h + 1)
                nc.scalar.activation(a1_pT[:, sl, :].rearrange("p b s -> p (b s)"), bank(6 + h), ACT.Copy)\
                    .then_inc(sem("a1_pT"), 1)
            turned_16(3, lambda c: normw[:, c:c + 1])
            router_exp(1)
            ffn(1)
            act.wait_ge(sem("r_turn"), 1)
            nc.scalar.activation(m_r, ps[0:E1, 0, 0:D], ACT.Copy).then_inc(sem("r_out"), 1)
            turned(4, xT_of)
            for b in range(4):
                act.wait_ge(sem("q2_mm"), b + 1)
                nc.scalar.activation(a2_q[:, 2 * b:2 * b + 2, :, :].rearrange("p b h d -> p (b h d)"), bank(4 + b), ACT.Square)\
                    .then_inc(sem("q2_sq"), 1)
            act.wait_ge(sem("q2_ss"), 1)
            nc.scalar.activation(a2_n[:, 2, :], a2_n[:, 0, :], ACT.Ln).then_inc(sem("q2_log"), 1)
            act.wait_ge(sem("q2_log"), 1)
            nc.scalar.activation(a2_n[:, 1, :], a2_n[:, 2, :], ACT.Exp, scale=-0.5).then_inc(sem("q2_rms"), 1)
            nc.scalar.activation(v2_16[:, :, :, 0, :], v2[:, :, :, :], ACT.Copy).then_inc(sem("v2_hi"), 1)
            for b in range(B):
                act.wait_ge(sem("q2_norm"), b + 1)
                nc.scalar.activation(a2_st[:, b, :, 1, :], a2_q[:, b, :, :], ACT.Copy).then_inc(sem("q2_hi_act"), 1)
            for n in range(4 * B):
                act.wait_ge(sem("s2_mm"), n + 1)
                pr = n % 2
                scores = ps[:, 2 * pr:2 * pr + 2, :].rearrange("p j s -> p (j s)")
                if n >= 2:
                    act.wait_ge(sem("p2_lo"), n - 1)
                nc.scalar.activation(a2_p[:, n % 2, :, :, :].rearrange("p j g s -> p (j g s)"), scores,
                                     ACT.Exp, scale=float(DH2) ** -0.5).then_inc(sem("p2"), 1)
                if n >= 2:
                    act.wait_ge(sem("pv2_job"), n - 1)
                nc.scalar.activation(a2_p16[:, n % 2, 0, :, :, :].rearrange("p j g s -> p (j g s)"), scores,
                                     ACT.Exp, scale=float(DH2) ** -0.5).then_inc(sem("p2"), 1)
            gu_hi(2, 0)
            turned_16(5)
            act.wait_ge(sem("router"), 3)
            act.wait_ge(sem("tinv"), 1)
            nc.scalar.activation(f_lg[:, :, 0:E2], ps[:, 4, 0:B * E2].rearrange("p (t e) -> p t e", e=E2), ACT.Tanh,
                                 scale=tinv[:, 0:1]).then_inc(sem("golden_tanh"), 1)
            act.wait_ge(sem("golden_dist"), 1)
            nc.scalar.activation(f_w[:, :, 0:E2], f_a, ACT.Exp, scale=-1.0 / 0.1).then_inc(sem("golden_exp"), 1)
            nc.scalar.activation(f_b, f_a, ACT.Exp, scale=-1.0 / 0.3).then_inc(sem("golden_exp"), 1)
            ffn(2)

            def whole_turned(k):
                def less_round(h):
                    act.wait_ge(sem("clipped"), 2 * k + h + 1)
                    nc.scalar.activation(a3_xi[:, 4 * h:4 * h + 4, :], a3_y[:, 4 * h:4 * h + 4, :], ACT.Copy, bias=-ROUND)\
                        .then_inc(sem("xi"), 1)

                def copy(h):
                    act.wait_ge(sem("xi_turn"), 2 * k + h + 1)
                    for c in range(KD):
                        nc.scalar.activation(a3_xiT[:, c, h * HALF:(h + 1) * HALF],
                                             ps[:, 4 + 2 * h + c, 0:HALF // 2].bitcast(BF16), ACT.Copy)\
                            .then_inc(sem("xi_turned"), 1)

                less_round(0)
                copy(0)
                less_round(1)
                copy(1)

            whole_turned(0)

            def q3_hi(b):
                if b >= 2:
                    act.wait_ge(sem("q3_turn"), b - 1)
                for i in (0, 1):
                    nc.scalar.activation(a3_st[:, b % 2, :, i, :], a3_y[:, b, :].rearrange("p (h d) -> p h d", d=DH3),
                                         ACT.Copy).then_inc(sem("q3_hi"), 1)

            def q3_copy(b):
                act.wait_ge(sem("q3_turn"), b + 1)
                nc.scalar.activation(a3_qT[:, b % 2, :, :].rearrange("p g s -> p (g s)"), seq_heads(4), ACT.Copy)\
                    .then_inc(sem("q3_ready"), 1)

            act.wait_ge(sem("q3"), 1)
            q3_hi(0)
            q3_hi(1)
            act.wait_ge(sem("q3"), 2)
            nc.scalar.activation(v3_16[:, :, :, 0, :], v3[:, :, :, :], ACT.Copy).then_inc(sem("v3_hi"), 1)
            q3_copy(0)
            q3_copy(1)
            q3_hi(2)

            def p3_exp(b, h):
                act.wait_ge(sem("p3_arg"), 2 * b + h + 1)
                p = a3_p[:, b % 2, 8 * h:8 * h + 8, :]
                nc.scalar.activation(p, p, ACT.Exp, scale=float(DH3) ** -0.5).then_inc(sem("p3"), 1)

            def p3_hi(n):
                g = n % 4
                act.wait_ge(sem("p3_turn"), n + 1)
                if n >= 4:
                    act.wait_ge(sem("pv3"), n - 3)
                nc.scalar.activation(a3_pT[:, 0, 4 * g:4 * g + 4, :].rearrange("p h s -> p (h s)"), bank(5 - g % 2),
                                     ACT.Copy).then_inc(sem("p3T_hi"), 1)

            for h in range(2):
                p3_exp(0, h)
            for b in range(B):
                p3_hi(4 * b)
                if b + 2 < B:
                    q3_copy(b + 2)
                p3_hi(4 * b + 1)
                if b + 3 < B:
                    q3_hi(b + 3)
                for h in range(2):
                    p3_hi(4 * b + 2 + h)
                    if b + 1 < B:
                        p3_exp(b + 1, h)
            whole_turned(1)
            turned_16(7)
            router_exp(3)
            ffn(3)

        @block.tensor
        def _(pe):
            def turn(s, src=xn):
                for t in range(B):
                    pe.wait_ge(sem("xn_ready"), B * s + t + 1)
                    for c in range(KD):
                        last = nc.tensor.transpose(ps[:, 2 * c + t // 4, (t % 4) * S:(t % 4 + 1) * S],
                                                   src[:, t, c * P:(c + 1) * P], ident[:, :])
                    if t % 4 == 3:
                        last.then_inc(sem("turn"), 1)

            THREE = ((0, 0), (1, 0), (0, 1))

            def router(L):
                n = EXPERTS[L]
                for half in range(2):
                    pe.wait_ge(sem("x_lo"), 2 * KD * L + KD * (half + 1))
                    for t in range(4 * half, 4 * half + 4):
                        for c in range(KD):
                            for i, w in THREE:
                                last = nc.tensor.matmul(ps[:, 4, t * n:(t + 1) * n], x16[:, i, c, t * S:(t + 1) * S],
                                                        wr16[:, w, c, ROUTER_AT[L]:ROUTER_AT[L] + n],
                                                        start=(c == 0 and i + w == 0), stop=(c == KD - 1 and w == 1))
                last.then_inc(sem("router"), 1)

            def turn_w(L):
                n = EXPERTS[L]
                pe.wait_ge(sem("w_ready"), L + 1)
                for t in range(B):
                    last = nc.tensor.transpose(ps[0:n, 5 + t // 4, (t % 4) * S:(t % 4 + 1) * S],
                                               f_w[:, t, 0:n], ident[:, :])
                if L == 1:
                    for t in range(B):
                        last = nc.tensor.transpose(ps[0:n, (7, 4)[t // 4], (t % 4) * S:(t % 4 + 1) * S],
                                                   m_sel[:, t, :], ident[:, :])
                last.then_inc(sem("w_turn"), 1)

            def gate_up(L, k, half, j=None):
                if half == 0:
                    pe.wait_ge(sem("wgu_lo"), at(tiles(L) + k + 1, j))
                if k >= 1:
                    pe.wait_ge(sem("gated"), at(halves(L) + 2 * k + half - 1, j, 4))
                    if L == 1 and half == 0:
                        pe.wait_ge(sem("star_read"), at(k, j))
                for g in range(2):
                    for c in range(KD):
                        for i, w in THREE:
                            last = nc.tensor.matmul(bank(2 * g + half), W16[:, k % 2, w, g * D + c * P:g * D + (c + 1) * P],
                                                    x16[:, i, c, half * HALF:(half + 1) * HALF],
                                                    start=(c == 0 and i + w == 0), stop=(c == KD - 1 and w == 1))
                last.then_inc(sem("gu_done"), 1)

            def down(L, k, half, j=None, first=False, final=False):
                if half == 0:
                    pe.wait_ge(sem("wd_lo"), at(tiles(L) + k + 1, j))
                pe.wait_ge(sem("h_lo"), at(halves(L) + 2 * k + half + 1, j, 4))
                for t in range(4 * half, 4 * half + 4):
                    for w, i in THREE:
                        last = nc.tensor.matmul(ps[:, 4 + t // 2, (t % 2) * D:(t % 2 + 1) * D],
                                                f_h16[:, k % 2, i, t * S:(t + 1) * S], W16[:, k % 2, w, 2 * D:3 * D],
                                                start=(first and t % 2 == 0 and i + w == 0), stop=final,
                                                skip_group_check=True)
                if half == 1:
                    last.then_inc(sem("down_done"), 1)
                elif final:
                    last.then_inc(sem("first_half_out"), 1)

            def star(k, j=None, own=True, before=True):
                pe.wait_ge(sem("gated"), at(halves(1) + 2 * k + 1, j, 4))
                if k == 0:
                    pe.wait_ge(sem("xs_lo"), KD)
                if before:
                    pe.wait_ge(sem("star_done"), at(k, j))
                e = at(k, j)
                if own:
                    for g in range(2):
                        for c in range(KD):
                            for w in range(2):
                                last = nc.tensor.matmul(ps[:, 2, 2 * g:2 * g + 2 - w], W16[:, k % 2, w, g * D + c * P:g * D + (c + 1) * P],
                                                        m_xs[:, c, bass.ds(e, 1), 0:2 - w].rearrange("p e i -> p (e i)"),
                                                        start=(c == 0 and w == 0), stop=(c == KD - 1 and w == 1),
                                                        skip_group_check=True)
                if before:
                    for c in range(KD):
                        for w in range(2):
                            last = nc.tensor.matmul(ps[:, 2, 4 + 2 * c:6 + 2 * c - w],
                                                    W16[:, (k + 1) % 2, w, 2 * D + c * P:2 * D + (c + 1) * P],
                                                    m_hs16[:, (k + 1) % 2, 0:2 - w], start=(w == 0), stop=(w == 1),
                                                    skip_group_check=True)
                last.then_inc(sem("star_mm"), 1)

            def ffn(L):
                gate_up(L, 0, 0)
                gate_up(L, 0, 1)
                turn_w(L)
                if L == 1:
                    pe.wait_ge(sem("by_expert"), 1)
                    for t in range(B):
                        last = nc.tensor.transpose(ps[:, 5, t * E1:(t + 1) * E1], m_lastT[:, t * S:(t + 1) * S], ident[0:E1, 0:E1])
                    last.then_inc(sem("last_turn"), 1)
                    pe.wait_ge(sem("last_out"), 1)
                    for c in range(KD):
                        for t in range(B):
                            last = nc.tensor.matmul(ps[:, 6, c * E1:(c + 1) * E1], x_rms[:, t, c * P:(c + 1) * P], m_last[:, t, :],
                                                    start=(t == 0), stop=(t == B - 1))
                    last.then_inc(sem("xs_mm"), 1)
                    star(0, before=False)
                else:
                    pe.wait_ge(sem("wT_half"), wT_copied(L))

                def pair(k, j=None, first=False):
                    for half in range(2):
                        gate_up(L, k, half, j)
                        if L == 1 and half == 1:
                            star(k, j, own=(k < E1))
                        down(L, k - 1, half, j, first=first)

                if L == 1:
                    pair(1, first=True)
                else:
                    for half in range(2):
                        gate_up(L, 1, half)
                    for half in range(2):
                        down(L, 0, half, first=True)
                with pe.Fori(0, TURNS[L]) as j:
                    pair(2, j)
                    pair(3, j)
                if NT[L] % 2:
                    pair(NT[L] - 1)
                if L == 1:
                    pe.wait_ge(sem("star_read"), E1 + 1)
                    pe.wait_ge(sem("gated"), halves(2))
                    for c in range(KD):
                        last = nc.tensor.transpose(ps[0:E1, 0, c * P:(c + 1) * P], m_rT[:, c, :], ident[:, :])
                    last.then_inc(sem("r_turn"), 1)
                    pe.wait_ge(sem("r_out"), 1)
                    pe.wait_ge(sem("by_expert"), 3)
                    for t in range(B):
                        nc.tensor.matmul(ps[:, 4 + t // 2, (t % 2) * D:(t % 2 + 1) * D], m_dropT[:, t * S:(t + 1) * S], m_r,
                                         start=False, stop=False, skip_group_check=True)
                for half in range(2):
                    down(L, NT[L] - 1, half, final=True)

            pe.wait_ge(sem("ident"), 3)
            pe.wait_ge(sem("ctx_in"), 16)
            for t in range(B):
                for c in range(KD):
                    last = nc.tensor.transpose(ps[:, 4 + 2 * c + t // 4, (t % 4) * S:(t % 4 + 1) * S],
                                               ctx_sb[:, t, c * P:(c + 1) * P], ident[:, :])
                if t % 4 == 3:
                    last.then_inc(sem("ctxT_turn"), 1)
            turn(0)

            pe.wait_ge(sem("ctxT_ready"), 4)
            pe.wait_ge(sem("kv_in"), 16 * 3)
            pe.wait_ge(sem("ones"), 1)

            def fold_products(k):
                e, f = k // (F2 // P), k % (F2 // P)
                if k:
                    pe.wait_ge(sem("fold_add"), 2 * k)
                else:
                    pe.wait_ge(sem("turned"), 2 * KD)
                pe.wait_ge(sem("lora_in"), 16 * (e + 1))
                for g in range(2):
                    for c in range(KD):
                        nc.tensor.matmul(ps[:, 0, (2 * g + c) * P:(2 * g + c + 1) * P], lora[:, 2 * g, c * P:(c + 1) * P],
                                         lora[:, 2 * g + 1, f * P:(f + 1) * P], start=True, stop=True)
                nc.tensor.matmul(ps[:, 1, 0:D], lora[:, 4, f * P:(f + 1) * P], lora[:, 5, :], start=True, stop=True)\
                    .then_inc(sem("fold_mm"), 1)

            def turn_k3(b):
                pe.wait_ge(sem("k3_split"), 2 * (b + 1))
                if b:
                    pe.wait_ge(sem("k3_ready"), b)
                for g in range(H3 // 2):
                    last = nc.tensor.transpose(seq_heads(4)[:, g * S:(g + 1) * S],
                                               k3_st[:, 2 * g:2 * g + 2, :, :].rearrange("p h i d -> p (h i d)"), ident16[:, :])
                last.then_inc(sem("k3_turn"), 1)

            def turn_k2(n):
                b = K2_ORDER[n]
                if n % 2 == 0:
                    pe.wait_ge(sem("k2_split"), 2 * (b + 1))
                else:
                    pe.wait_ge(sem("k2_split_dve"), 2 * (b - B // 2 + 1))
                if n == 1:
                    pe.wait_ge(sem("v2_out"), B)
                if n >= 2:
                    pe.wait_ge(sem("k2_ready"), n - 1)
                for g in range(H2 // 4):
                    last = nc.tensor.transpose(seq_heads(7 - n % 2)[:, g * S:(g + 1) * S],
                                               k_st[:, n % 2, 4 * g:4 * g + 4, :, :].rearrange("p h i d -> p (h i d)"), ident16[:, :])
                last.then_inc(sem("k2_turn"), 1)

            for b in range(B):
                if b:
                    pe.wait_ge(sem("v2_out"), b)
                    pe.wait_ge(sem("k2_raw"), 2 * b)
                for c in range(KD):
                    last = nc.tensor.matmul(bank(6), ctxT[:, c, b, 1:SEG], wkv2[:, c, :], start=(c == 0), stop=(c == KD - 1))
                last.then_inc(sem("kv2_mm"), 1)
                if b:
                    pe.wait_ge(sem("v3_out"), b)
                for c in range(KD):
                    nc.tensor.matmul(bank(5), ctxT[:, c, b, 1:SEG], wkv3[:, c, :], start=(c == 0), stop=False)
                nc.tensor.matmul(bank(5), ones[0:1, :], bkv3[:, :], start=False, stop=True).then_inc(sem("kv3_mm"), 1)
                if b >= 1:
                    turn_k3(b - 1)
                if b % 2:
                    fold_products(b // 2)
            turn_k3(B - 1)

            pe.wait_ge(sem("wq_whole"), 1)
            for w in range(2):
                for c in range(KD):
                    for o in range(KD):
                        k = (w * KD + c) * D + o * P
                        last = nc.tensor.transpose(ps[:, 2, :].bitcast(BF16)[:, k:k + P], wq_i[:, w, o, c * P:(c + 1) * P], identb[:, :])
            last.then_inc(sem("wi_turn"), 1)
            pe.wait_ge(sem("wq_diag"), 1)
            for k in range(4):
                last = nc.tensor.matmul(ps[:, 3, k * P:(k + 1) * P], ones[:, :], wq_diag[:, k, :], start=True, stop=True)
            last.then_inc(sem("wscale_mm"), 1)

            for c in range(KD):
                pe.wait_ge(sem("wkv_y"), c + 1)
                if c == 0:
                    pe.wait_ge(sem("fold_add"), 2 * LORA_T)
                    pe.wait_ge(sem("wi"), 2)
                for t in range(B):
                    last = nc.tensor.transpose(ps[:, t // 2, (t % 2) * D + c * P:(t % 2) * D + (c + 1) * P],
                                               wk_k[:, c, t, 1:SEG], ident[:, :])
            last.then_inc(sem("wkv_turn"), 1)
            for n in range(B):
                turn_k2(n)
            pe.wait_ge(sem("k2_ready"), B)
            pe.wait_ge(sem("k3_ready"), B)
            pe.wait_ge(sem("v3_out"), B)

            pe.wait_ge(sem("late_in"), 16 * 5)
            turn(1)
            pe.wait_ge(sem("wr_lo"), 1)
            router(0)
            ffn(0)
            turn(2)
            for h in range(2):
                pe.wait_ge(sem("turned"), 2 * KD * 2 + KD * (h + 1))
                for b in range(4):
                    t = 4 * h + b
                    for c in range(KD):
                        last = nc.tensor.matmul(ps[:, 4 + h, b * S:(b + 1) * S], xT[:, c, t * S:(t + 1) * S],
                                                ctxT[:, c, t, 1:SEG], start=(c == 0), stop=(c == KD - 1))
                last.then_inc(sem("a1_mm"), 1)
            for h in range(2):
                pe.wait_ge(sem("a1_p"), h + 1)
                for b in range(4):
                    last = nc.tensor.transpose(ps[:, 6 + h, b * S:(b + 1) * S], a1_p[:, 4 * h + b, :], ident[:, :])
                last.then_inc(sem("a1_turn"), 1)
                pe.wait_ge(sem("a1_pT"), h + 1)
                for b in range(4 * h, 4 * h + 4):
                    last = nc.tensor.matmul(ps[:, b // 2, (b % 2) * D:(b % 2 + 1) * D], a1_pT[:, b, :], ctx_sb[:, b, :],
                                            start=True, stop=True)
                last.then_inc(sem("a1_pv"), 1)
            turn(3, x_rms)
            router(1)
            ffn(1)
            turn(4)
            pe.wait_ge(sem("turned"), 2 * KD * 5)
            for t in range(B):
                for c in range(KD):
                    last = nc.tensor.matmul(ps[:, 4 + t // 2, (t % 2) * D:(t % 2 + 1) * D], xT[:, c, t * S:(t + 1) * S],
                                            wq2[:, c, :], start=(c == 0), stop=(c == KD - 1))
                if t % 2:
                    last.then_inc(sem("q2_mm"), 1)

            def turn_q2(b):
                pe.wait_ge(sem("q2_lo"), b + 1)
                pe.wait_ge(sem("q2_lo_pool"), b + 1)
                pe.wait_ge(sem("q2_hi_act"), b + 1)
                if b == 0:
                    pe.wait_ge(sem("q2_norm"), B)
                else:
                    pe.wait_ge(sem("q2T"), b)
                for g in range(H2 // 4):
                    last = nc.tensor.transpose(seq_heads(4)[:, g * S:(g + 1) * S],
                                               a2_st[:, b, 4 * g:4 * g + 4, :, :].rearrange("p h i d -> p (h i d)"), ident16[:, :])
                last.then_inc(sem("q2_turn"), 1)

            def pv2(n):
                b, hg, pr = n // 4, n % 4 // 2, n % 2
                m = 2 * b + hg
                pe.wait_ge(sem("p2_lo"), n + 1)
                if n % 4 == 0:
                    pe.wait_ge(sem("v2_lo"), b + 1)
                if n % 2 == 0 and m >= 3:
                    pe.wait_ge(sem("o2"), m - 2)
                for jj in range(2):
                    for g in range(4):
                        h = 4 * g + 2 * pr + jj
                        out = ps[:, 5 + m % 3, h * 2 * (DH2 + 1):(h + 1) * 2 * (DH2 + 1)]
                        v = v2_16[:, b, 16 * hg + h, :, :]
                        nc.tensor.matmul(out, a2_p16[:, n % 2, 0, jj, g, :], v.rearrange("p i d -> p (i d)"),
                                         start=True, stop=False)
                        last = nc.tensor.matmul(out[:, 0:DH2 + 1], a2_p16[:, n % 2, 1, jj, g, :], v[:, 0, :],
                                                start=False, stop=True)
                last.then_inc(sem("pv2_job"), 1)

            turn_q2(0)
            for n in range(4 * B):
                b, hg, pr = n // 4, n % 4 // 2, n % 2
                if n % 4 == 0:
                    pe.wait_ge(sem("q2T"), b + 1)
                if n >= 2:
                    pe.wait_ge(sem("p2"), 2 * (n - 1))
                for g in range(4 * hg, 4 * hg + 4):
                    for jj in range(2):
                        i = 2 * pr + jj
                        last = nc.tensor.matmul(ps[:, i, (g % 4) * S:(g % 4 + 1) * S], k2T[32 * i:32 * i + 32, b, g, :],
                                                a2_qT[32 * i:32 * i + 32, b % 2, g, :], start=True, stop=True)
                last.then_inc(sem("s2_mm"), 1)
                if n % 4 == 1 and b + 1 < B:
                    turn_q2(b + 1)
                if n >= 2:
                    pv2(n - 2)
            for n in (4 * B - 2, 4 * B - 1):
                pv2(n)
            turn(5)
            router(2)
            ffn(2)

            def whole_product(k):
                def turn_half(h):
                    pe.wait_ge(sem("xi"), 2 * k + h + 1)
                    for c in range(KD):
                        for t in range(4):
                            last = nc.tensor.transpose(ps[:, 4 + 2 * h + c, :].bitcast(BF16)[:, t * S:(t + 1) * S],
                                                       a3_xi[:, 4 * h + t, c * P:(c + 1) * P], identb[:, :])
                    last.then_inc(sem("xi_turn"), 1)

                def multiply(h):
                    pe.wait_ge(sem("xi_turned"), KD * (2 * k + h + 1))
                    for t in range(4 * h, 4 * h + 4):
                        for c in range(KD):
                            last = nc.tensor.matmul(ps[:, t // 2, (t % 2) * D:(t % 2 + 1) * D], a3_xiT[:, c, t * S:(t + 1) * S],
                                                    wi[:, k, c, :], start=(c == 0), stop=(c == KD - 1))
                    last.then_inc(sem("whole_mm"), 1)

                turn_half(0)
                multiply(0)
                turn_half(1)
                multiply(1)

            whole_product(0)

            def turn_q3(b):
                pe.wait_ge(sem("q3_lo"), 2 * (b + 1))
                if b >= 1:
                    pe.wait_ge(sem("q3_ready"), b)
                if b >= 3:
                    pe.wait_ge(sem("p3T_lo"), 4 * (b - 2))
                for g in range(H3 // 2):
                    last = nc.tensor.transpose(seq_heads(4)[:, g * S:(g + 1) * S],
                                               a3_st[:, b % 2, 2 * g:2 * g + 2, :, :].rearrange("p h i d -> p (h i d)"),
                                               ident16[:, :])
                last.then_inc(sem("q3_turn"), 1)

            def scores_3(b, i):
                pe.wait_ge(sem("q3_ready"), b + 1)
                if b:
                    pe.wait_ge(sem("p3_arg"), 2 * b - 1 + i)
                for j in range(H3 // 2):
                    last = nc.tensor.matmul(ps[:, 2 * i + j // 4, (j % 4) * S:(j % 4 + 1) * S],
                                            a3_qT[64 * i:64 * i + 64, b % 2, j, :],
                                            k3T[64 * i:64 * i + 64, b, j, :], start=True, stop=True)
                last.then_inc(sem("s3_mm"), 1)

            def turn_p3(n):
                b, g = n // 4, n % 4
                if g % 2 == 0:
                    pe.wait_ge(sem("p3"), 2 * b + 1 + g // 2)
                if n >= 2:
                    pe.wait_ge(sem("p3T_lo"), n - 1)
                for k in range(4):
                    last = nc.tensor.transpose(ps[:, 5 - g % 2, k * S:(k + 1) * S], a3_p[:, b % 2, 4 * g + k, :], ident[:, :])
                last.then_inc(sem("p3_turn"), 1)

            def weigh_v3(n):
                b, g = n // 4, n % 4
                pe.wait_ge(sem("p3T_lo"), n + 1)
                if n == 0:
                    pe.wait_ge(sem("v3_lo"), 1)
                if g % 2 == 0 and b:
                    pe.wait_ge(sem("o3"), 2 * b - 1 + g // 2)
                for k in range(4 * g, 4 * g + 4):
                    out = ps[:, 7 - g // 2, (k % 8) * 2 * (DH3 + 1):(k % 8 + 1) * 2 * (DH3 + 1)]
                    v = v3_16[:, b, 2 * (k % 8) + k // 8, :, :]
                    nc.tensor.matmul(out, a3_pT[:, 0, k, :], v.rearrange("p i d -> p (i d)"), start=True, stop=False)
                    last = nc.tensor.matmul(out[:, 0:DH3 + 1], a3_pT[:, 1, k, :], v[:, 0, :], start=False, stop=True)
                last.then_inc(sem("pv3"), 1)

            turn_q3(0)
            turn_q3(1)
            for b in range(2):
                for i in range(2):
                    scores_3(b, i)
            turn_p3(0)
            turn_q3(2)
            for b in range(B):
                pe.wait_ge(sem("q3_ready"), min(b + 3, B))
                for g in range(1, 4):
                    turn_p3(4 * b + g)
                    if g == 3 and b + 2 < B:
                        scores_3(b + 2, 0)
                    weigh_v3(4 * b + g - 1)
                if b + 2 < B:
                    scores_3(b + 2, 1)
                if b + 1 < B:
                    turn_p3(4 * b + 4)
                if b + 3 < B:
                    turn_q3(b + 3)
                weigh_v3(4 * b + 3)
            whole_product(1)
            turn(7)
            router(3)
            ffn(3)

        @block.vector
        def _(dve):
            steps = [0]

            def link(ins):
                steps[0] += 1
                ins.then_inc(sem("dve_step"), 1)
                dve.wait_ge(sem("dve_step"), steps[0])

            def statistics(s, h):
                sl = range(4 * h, 4 * h + 4)
                for t in sl:
                    ins = nc.vector.bn_stats(stats[:, t, :], x[:, t, :])
                link(ins)
                for t in sl:
                    ins = nc.vector.bn_aggr(mv[:, t, :], stats[:, t, :])
                link(ins)
                nc.vector.tensor_scalar(veps[:, 4 * h:4 * h + 4], mv[:, 4 * h:4 * h + 4, 1], LN_EPS, None, ALU.add)\
                    .then_inc(sem("ln_var"), 1)

            def layer_norm(s, add=None, halves=(0, 1), scale=rstd):
                for h in halves:
                    if add:
                        link(add(h))
                    statistics(s, h)
                for h in range(2):
                    dve.wait_ge(sem("ln_rstd"), 2 * s + h + 1)
                    for t in range(4 * h, 4 * h + 4):
                        nc.vector.tensor_scalar(xn[:, t, :], x[:, t, :], mv[:, t, 0:1], scale[:, t:t + 1],
                                                ALU.subtract, ALU.mult).then_inc(sem("xn_ready"), 1)
                dve.wait_ge(sem("xn_ready"), B * (s + 1))

            def wkv():
                dve.wait_ge(sem("decay"), 1)
                dve.wait_ge(sem("wkv_edges"), 5)
                link(nc.vector.tensor_scalar(wdec[:, :], wdec[:, :], -1.0, None, ALU.mult))
                for c in range(KD):
                    dve.wait_ge(sem("turned"), 2 * KD)
                    k = wk_k[:, c, :, :].rearrange("p b s -> p (b s)")
                    pp = wk_pp[:, 1:LW + 1]
                    before = wk_pp[:, 0:LW]
                    link(nc.vector.tensor_scalar(wk_dec, k, 0.0, wdec[:, c:c + 1], ALU.mult, ALU.add))
                    link(nc.vector.memset(wk_dec.rearrange("p (b s) -> p b s", b=B)[:, :, 0:1], FAR))
                    link(nc.vector.tensor_tensor_scan(pp, wk_dec, k, FAR, ALU.add, ALU.max))
                    nc.vector.scalar_tensor_tensor(wk_d[:, 0, :], before, wdec[:, c:c + 1], k, ALU.add, ALU.subtract)
                    link(nc.vector.scalar_tensor_tensor(wk_d[:, 1, :], k, tf[:, c:c + 1], before, ALU.add, ALU.subtract))
                    for e, (d, op) in enumerate(((0, ALU.min), (0, ALU.max), (1, ALU.min), (1, ALU.max))):
                        nc.vector.tensor_scalar(wk_e[:, c, e, :], wk_d[:, d, :], 0.0, None, op).then_inc(sem("wkv_arg"), 1)
                    dve.wait_ge(sem("wkv_arg"), 4 * c + 4)
                weight_scales()
                for c in range(KD):
                    dve.wait_ge(sem("wkv_exp"), 4 * c + 4)
                    e1b, e2b, e2, e1 = (wk_e[:, c, k, :] for k in range(4))
                    nc.vector.tensor_tensor_scan(wk_bb[:, 1:LW + 1], e1b, e2b, 0.0, ALU.mult, ALU.add)
                    dve.wait_ge(sem("wkv_ev"), 2 * c + 2)
                    link(nc.vector.tensor_tensor_scan(wk_aa[:, 1:LW + 1], e1b, wk_ev[:, 0, :], 0.0, ALU.mult, ALU.add))
                    nc.vector.tensor_tensor(wk_d[:, 0, :], e1, wk_bb[:, 0:LW], ALU.mult)
                    link(nc.vector.tensor_tensor(wk_d[:, 1, :], e1, wk_aa[:, 0:LW], ALU.mult))
                    nc.vector.tensor_tensor(wk_d[:, 0, :], wk_d[:, 0, :], e2, ALU.add)
                    link(nc.vector.tensor_tensor(wk_d[:, 1, :], wk_d[:, 1, :], wk_ev[:, 1, :], ALU.add))
                    link(nc.vector.reciprocal(wk_d[:, 0, :], wk_d[:, 0, :]))
                    ins = nc.vector.tensor_tensor(wk_k[:, c, :, :].rearrange("p b s -> p (b s)"), wk_d[:, 0, :], wk_d[:, 1, :], ALU.mult)
                    ins.then_inc(sem("wkv_y"), 1)
                    dve.wait_ge(sem("wkv_y"), c + 1)
                dve.wait_ge(sem("tg"), 1)
                link(nc.vector.tensor_scalar(tg_ffn[:, :], tg[:, :], 1.0 / WSCALE, None, ALU.mult))

            def add_banks(first, gate, tg, h):
                for b in (2 * h, 2 * h + 1):
                    xs = x[:, 2 * b:2 * b + 2, :].rearrange("p t d -> p (t d)")
                    ins = nc.vector.scalar_tensor_tensor(xs, ps[:, first + b, :], tg[:, gate:gate + 1], xs, ALU.mult, ALU.add)
                return ins

            def add_ffn(L):
                def add(h):
                    if h == 0:
                        dve.wait_ge(sem("first_half_out"), L + 1)
                    else:
                        dve.wait_ge(sem("down_done"), tiles(L + 1))
                    return add_banks(4, 4 + L, tg_ffn, h)
                return add

            def weight_scales():
                dve.wait_ge(sem("wqp_in"), 16)
                link(nc.vector.tensor_reduce(wq_s[:, 0, :], wq_f.rearrange("p w o d -> p (w o) d"), AX.X, ALU.max,
                                             apply_absolute_value=True))
                link(nc.vector.tensor_scalar(wq_s[:, 1, :], wq_s[:, 0, :], 1.0 / 127.0, 1e-8, ALU.mult, ALU.max))
                nc.vector.reciprocal(wq_s[:, 2, :], wq_s[:, 1, :]).then_inc(sem("wq_scale"), 1)
                dve.wait_ge(sem("wq_scale"), 1)
                for k in range(4):
                    w = wq_f[:, k // 2, k % 2, :]
                    ins = nc.vector.tensor_scalar(w, w, wq_s[:, 2, k:k + 1], ROUND, ALU.mult, ALU.add)
                link(ins)
                link(nc.vector.tensor_scalar(wq_f, wq_f, ROUND, 127.0, ALU.subtract, ALU.min))
                nc.vector.tensor_scalar(wq_i, wq_f, -127.0, None, ALU.max).then_inc(sem("wq_whole"), 1)
                link(nc.vector.reciprocal(tinv[:, :], tinv[:, :]))
                nc.vector.tensor_scalar(tinv[:, :], tinv[:, :], 0.5, None, ALU.mult).then_inc(sem("tinv"), 1)

            def spread(v, n):
                return v.unsqueeze(2).to_broadcast((P, B, n))

            def softmax(L):
                n = EXPERTS[L]
                lg = f_lg[:, :, 0:n]
                mx, sm, rc = f_s8[:, 0, :], f_s8[:, 1, :], f_s8[:, 2, :]
                dve.wait_ge(sem("router"), L + 1)
                scores = ps[:, 4, 0:B * n].rearrange("p (t e) -> p t e", e=n)
                link(nc.vector.tensor_reduce(mx, scores, AX.X, ALU.max))
                nc.vector.tensor_tensor(lg, scores, spread(mx, n), ALU.subtract).then_inc(sem("router_arg"), 1)
                dve.wait_ge(sem("router_exp"), min(L, 2) + 1)
                link(nc.vector.tensor_reduce(sm, lg, AX.X, ALU.add))
                link(nc.vector.reciprocal(rc, sm))
                link(nc.vector.tensor_tensor(f_w[:, :, 0:n], lg, spread(rc, n), ALU.mult))

            def before(v):
                ve = v.unsqueeze(3).to_broadcast((P, B, E0, E0))
                vj = v.unsqueeze(2).to_broadcast((P, B, E0, E0))
                nc.vector.tensor_tensor(f_cmp, vj, ve, ALU.is_gt)
                link(nc.vector.tensor_tensor(f_eq, vj, ve, ALU.is_equal))
                link(nc.vector.tensor_tensor(f_eq, f_eq, f_tri.unsqueeze(1).to_broadcast((P, B, E0, E0)), ALU.mult))
                link(nc.vector.tensor_tensor(f_cmp, f_cmp, f_eq, ALU.add))

            def make_tri():
                link(nc.vector.memset(f_tri, 0.0))
                for e in range(1, E0):
                    ins = nc.vector.memset(f_tri[:, e, 0:e], 1.0)
                link(ins)

            def gated(L, k, half, j=None):
                n = halves(L) + 2 * k + half + 1
                dve.wait_ge(sem("silu_done"), at(n, j, 4))
                if tiles(L) + k:
                    dve.wait_ge(sem("h_full"), at(n - 2, j, 4))
                nc.vector.scalar_tensor_tensor(f_g[:, half, :], bank(2 + half), 1.0 / WSCALE, f_s[:, half, :],
                                               ALU.mult, ALU.mult).then_inc(sem("gated"), 1)

            def h_lo(L, k, half, j=None):
                hi, lo = (f_h16[:, k % 2, i, half * HALF:(half + 1) * HALF] for i in range(2))
                dve.wait_ge(sem("h_hi"), at(halves(L) + 2 * k + half + 1, j, 4))
                nc.vector.tensor_tensor(lo, f_h[:, half, :], hi, ALU.subtract).then_inc(sem("h_lo"), 1)

            def gu_lo(L, k, j=None):
                dve.wait_ge(sem("wgu_hi"), at(tiles(L) + k + 1, j))
                nc.vector.scalar_tensor_tensor(W16[:, k % 2, 1, 0:2 * D], W[:, k % 2, 0:2 * D], WSCALE,
                                               W16[:, k % 2, 0, 0:2 * D], ALU.mult, ALU.subtract).then_inc(sem("wgu_lo"), 1)

            def down_lo(L, k, j=None):
                dve.wait_ge(sem("wd_hi"), at(tiles(L) + k + 1, j))
                nc.vector.scalar_tensor_tensor(W16[:, k % 2, 1, 2 * D:3 * D], W[:, k % 2, 2 * D:3 * D], WSCALE,
                                               W16[:, k % 2, 0, 2 * D:3 * D], ALU.mult, ALU.subtract).then_inc(sem("wd_lo"), 1)

            def x_lo(s, L):
                for half in range(2):
                    for c in range(KD):
                        n = KD * half + c + 1
                        dve.wait_ge(sem("turned"), 2 * KD * turns_before(s) + n)
                        hi, lo = (x16[:, i, c, half * HALF:(half + 1) * HALF] for i in range(2))
                        nc.vector.scalar_tensor_tensor(lo, bank(2 * c + half), normw[:, c:c + 1] if L == 1 else 1.0, hi,
                                                       ALU.mult, ALU.subtract).then_inc(sem("x_lo"), 1)

            def star_read(k, j=None, own=True, before=True):
                dve.wait_ge(sem("star_mm"), at(k + 1, j))
                if before:
                    ins = nc.vector.tensor_reduce(m_rT[:, :, bass.ds(at(k - 1, j), 1)].rearrange("p c e -> p (c e)"),
                                                  ps[:, 2, 4:8].rearrange("p (c i) -> p c i", c=KD), AX.X, ALU.add)
                if own:
                    ins = nc.vector.tensor_reduce(m_gu, ps[:, 2, 0:4].rearrange("p (g i) -> p g i", g=2), AX.X, ALU.add)
                ins.then_inc(sem("star_read"), 1)

            def star(k, j=None):
                n = k + 1
                dve.wait_ge(sem("star_silu"), at(n, j))
                nc.vector.scalar_tensor_tensor(m_hs, m_gu[:, 1:2], 1.0 / WSCALE, m_ss, ALU.mult, ALU.mult)\
                    .then_inc(sem("star_step"), 1)
                dve.wait_ge(sem("star_step"), at(2 * n - 1, j, 4))
                nc.vector.tensor_copy(m_hs16[:, k % 2, 0:1], m_hs).then_inc(sem("star_step"), 1)
                dve.wait_ge(sem("star_step"), at(2 * n, j, 4))
                nc.vector.tensor_tensor(m_hs16[:, k % 2, 1:2], m_hs, m_hs16[:, k % 2, 0:1], ALU.subtract)\
                    .then_inc(sem("star_done"), 1)

            def last_slots_lo():
                dve.wait_ge(sem("xs_hi"), KD)
                for c in range(KD):
                    nc.vector.scalar_tensor_tensor(m_xs[:, c, :, 1], ps[:, 6, c * E1:(c + 1) * E1], normw[:, c:c + 1],
                                                   m_xs[:, c, :, 0], ALU.mult, ALU.subtract).then_inc(sem("xs_lo"), 1)

            def tile(L, k, j=None, last=False):
                down_lo(L, k, j)
                gated(L, k, 0, j)
                if k == 0:
                    gated(L, k, 1, j)
                if not last:
                    gu_lo(L, k + 1, j)
                h_lo(L, k, 0, j)
                if L == 1 and k == 0:
                    last_slots_lo()
                if L == 1:
                    star_read(k, j, own=(k < E1), before=(k > 0))
                if k > 0:
                    gated(L, k, 1, j)
                h_lo(L, k, 1, j)
                if L == 1 and k < E1:
                    star(k, j)

            def ffn(L):
                tile(L, 0)
                tile(L, 1)
                with dve.Fori(0, MID_TURNS[L]) as j:
                    tile(L, 2, j)
                    tile(L, 3, j)
                for k in range(2 + 2 * MID_TURNS[L], NT[L]):
                    tile(L, k, last=(k == NT[L] - 1))

            dve.wait_ge(sem("x_in"), 16)
            layer_norm(0)
            wkv()
            dve.wait_ge(sem("k2_scale"), 1)
            for b in range(B // 2, B):
                raw = k_raw[:, b, :].rearrange("p (h d) -> p h d", d=DH2)
                nc.vector.tensor_tensor(raw, raw, k_norm[:, 2, b, :].unsqueeze(2).to_broadcast((P, H2, DH2)), ALU.mult)\
                    .then_inc(sem("k2_norm_dve"), 1)

            def lo_k2(b):
                raw = k_raw[:, b, :].rearrange("p (h d) -> p h d", d=DH2)
                dve.wait_ge(sem("k2_norm_dve"), b - B // 2 + 1)
                dve.wait_ge(sem("k2_hi"), 2 * (K2_ORDER.index(b) + 1))
                for i in (1, 3):
                    nc.vector.tensor_tensor(k_st[:, 1, :, i, :], raw, k_st[:, 1, :, i - 1, :], ALU.subtract)\
                        .then_inc(sem("k2_split_dve"), 1)

            lo_k2(4)
            dve.wait_ge(sem("wkv_turn"), 1)
            for h in range(2):
                link(add_banks(0, 0, tg, h))
                statistics(1, h)
                lo_k2(5 + h)
            lo_k2(7)
            dve.wait_ge(sem("wr_hi"), 1)
            nc.vector.tensor_tensor(wr16[:, 1, :, :], wr[:, :, :], wr16[:, 0, :, :], ALU.subtract).then_inc(sem("wr_lo"), 1)
            gu_lo(0, 0)
            dve.wait_ge(sem("k2_split"), B)
            dve.wait_ge(sem("k2_split_dve"), B)
            layer_norm(1, halves=())
            x_lo(1, 0)
            make_tri()
            softmax(0)
            before(f_w[:, :, 0:E0])
            link(nc.vector.tensor_reduce(f_rk, f_cmp, AX.X, ALU.add))
            nc.vector.scalar_tensor_tensor(f_w[:, :, 0:E0], f_rk, TOP0 - 0.5, f_w[:, :, 0:E0], ALU.is_lt, ALU.mult)\
                .then_inc(sem("w_ready"), 1)
            ffn(0)
            layer_norm(2, add_ffn(0))
            dve.wait_ge(sem("mask"), 1)
            link(nc.vector.tensor_reduce(a1_s[:, 0, :], a1_mask, AX.X, ALU.max))

            def mine(v, h):
                return v[:, 4 * h:4 * h + 4]

            for h in range(2):
                p = a1_p[:, 4 * h:4 * h + 4, :]
                dve.wait_ge(sem("a1_mm"), h + 1)
                link(nc.vector.scalar_tensor_tensor(p.rearrange("p b s -> p (b s)"), bank(4 + h), float(D) ** -0.5,
                                                    a1_mask[:, 4 * h:4 * h + 4, :].rearrange("p b s -> p (b s)"),
                                                    ALU.mult, ALU.mult))
                link(nc.vector.tensor_tensor(p, p, a1_neg[:, 4 * h:4 * h + 4, :], ALU.add))
                link(nc.vector.tensor_reduce(mine(a1_s[:, 1, :], h), p, AX.X, ALU.max))
                nc.vector.tensor_tensor(p, p, mine(a1_s[:, 1, :], h).unsqueeze(2).to_broadcast((P, 4, S)), ALU.subtract)\
                    .then_inc(sem("a1_arg"), 1)
            for h in range(2):
                rest, valid = mine(a1_s[:, 3, :], h), mine(a1_s[:, 0, :], h)
                dve.wait_ge(sem("a1_p"), h + 1)
                link(nc.vector.tensor_reduce(mine(a1_s[:, 2, :], h), a1_p[:, 4 * h:4 * h + 4, :], AX.X, ALU.add))
                link(nc.vector.reciprocal(rest, mine(a1_s[:, 2, :], h)))
                link(nc.vector.scalar_tensor_tensor(mine(a1_s[:, 4, :], h), rest, tg[:, 1:2], valid, ALU.mult, ALU.mult))

            def add_a1(h):
                dve.wait_ge(sem("a1_pv"), h + 1)
                for b in range(4 * h, 4 * h + 4):
                    ins = nc.vector.scalar_tensor_tensor(x[:, b, :], ps[:, b // 2, (b % 2) * D:(b % 2 + 1) * D],
                                                         a1_s[:, 4, b:b + 1], x[:, b, :], ALU.mult, ALU.add)
                return ins

            layer_norm(3, add_a1, scale=rms)
            x_lo(3, 1)
            factor, addend = resid[:, 0, :], resid[:, 1, :]
            link(nc.vector.tensor_scalar(factor, rstd[:, :], tg[:, 5:6], None, ALU.mult))
            link(nc.vector.scalar_tensor_tensor(addend, mv[:, :, 0], -1.0, factor, ALU.mult, ALU.mult))
            link(nc.vector.tensor_scalar(factor, factor, 1.0, None, ALU.add))
            for t in range(B):
                ins = nc.vector.tensor_scalar(x[:, t, :], x[:, t, :], factor[:, t:t + 1], addend[:, t:t + 1], ALU.mult, ALU.add)
            link(ins)
            nc.vector.memset(m_zero, 0.0)
            nc.vector.memset(m_x[:, :, E1:E1 + 8], -1.0)
            softmax(1)
            nc.vector.tensor_copy(m_x[:, :, 0:E1], f_w)
            for t in range(B):
                ins = nc.vector.max(m_top[:, t, :], f_w[:, t, :])
            link(ins)
            link(nc.vector.memset(m_top[:, :, TOP1:8], -1.0))
            for t in range(B):
                ins = nc.vector.match_replace(m_rep[:, t, :], m_top[:, t, :], m_x[:, t, :], -2.0)
            link(ins)
            link(nc.vector.tensor_scalar(m_sel, m_rep[:, :, 0:E1], -2.0, None, ALU.is_equal))
            link(nc.vector.tensor_tensor(f_w, f_w, m_sel, ALU.mult))
            link(nc.vector.tensor_reduce(f_s8[:, 3, :], f_w, AX.X, ALU.add))
            link(nc.vector.reciprocal(f_s8[:, 4, :], f_s8[:, 3, :]))
            nc.vector.tensor_tensor(f_w, f_w, spread(f_s8[:, 4, :], E1), ALU.mult).then_inc(sem("w_ready"), 1)
            dve.wait_ge(sem("wT_out"), 4)
            link(nc.vector.tensor_tensor_scan(m_cum, m_selT, m_zero, 0.0, ALU.add, ALU.add))
            nc.vector.scalar_tensor_tensor(m_lastT, m_cum, float(CAPACITY), m_selT, ALU.is_equal, ALU.mult)\
                .then_inc(sem("by_expert"), 1)
            nc.vector.scalar_tensor_tensor(f_wT, m_cum, float(CAPACITY), m_raw, ALU.is_le, ALU.mult)\
                .then_inc(sem("by_expert"), 1)
            nc.vector.scalar_tensor_tensor(m_dropT, m_cum, float(CAPACITY), m_raw, ALU.is_gt, ALU.mult)\
                .then_inc(sem("by_expert"), 1)
            ffn(1)
            layer_norm(4, add_ffn(1))
            groups = a2_q.rearrange("p b h d -> p (b h) d")
            per = 2 * H2
            for b in range(4):
                dve.wait_ge(sem("q2_sq"), b + 1)
                ins = nc.vector.tensor_reduce(a2_n[:, 0, b * per:(b + 1) * per], groups[:, b * per:(b + 1) * per, :],
                                              AX.X, ALU.add)
            link(ins)
            nc.vector.tensor_scalar(a2_n[:, 0, :], a2_n[:, 0, :], 1.0 / DH2, RMS_EPS, ALU.mult, ALU.add).then_inc(sem("q2_ss"), 1)
            dve.wait_ge(sem("q2_rms"), 1)
            guess, t = a2_n[:, 1, :], a2_n[:, 2, :]
            link(nc.vector.tensor_tensor(t, guess, guess, ALU.mult))
            link(nc.vector.tensor_tensor(t, t, a2_n[:, 0, :], ALU.mult))
            link(nc.vector.tensor_scalar(t, t, -0.5, 1.5, ALU.mult, ALU.add))
            link(nc.vector.tensor_tensor(guess, t, guess, ALU.mult))
            for b in range(B):
                nc.vector.tensor_tensor(a2_q[:, b, :, :], ps[:, 4 + b // 2, (b % 2) * D:(b % 2 + 1) * D].rearrange("p (h d) -> p h d", d=DH2),
                                        a2_n[:, 1, b * H2:(b + 1) * H2].unsqueeze(2).to_broadcast((P, H2, DH2)), ALU.mult)\
                    .then_inc(sem("q2_norm"), 1)
                dve.wait_ge(sem("q2_norm"), b + 1)
                nc.vector.tensor_copy(a2_st[:, b, :, 0, :], a2_q[:, b, :, :]).then_inc(sem("q2_hi"), 1)
                dve.wait_ge(sem("q2_hi"), b + 1)
                nc.vector.tensor_tensor(a2_st[:, b, :, 2, :], a2_q[:, b, :, :], a2_st[:, b, :, 0, :], ALU.subtract)\
                    .then_inc(sem("q2_lo"), 1)

            def q2T(b):
                dve.wait_ge(sem("q2_turn"), b + 1)
                if b >= 2:
                    dve.wait_ge(sem("s2_mm"), 4 * (b - 1))
                nc.vector.tensor_copy(a2_qT[:, b % 2, :, :].rearrange("p g s -> p (g s)"), seq_heads(4)).then_inc(sem("q2T"), 1)

            def p2_lo(n):
                p, hi, lo = (t.rearrange("p j g s -> p (j g s)") for t in
                             (a2_p[:, n % 2, :, :, :], a2_p16[:, n % 2, 0, :, :, :], a2_p16[:, n % 2, 1, :, :, :]))
                dve.wait_ge(sem("p2"), 2 * (n + 1))
                nc.vector.tensor_tensor(lo, p, hi, ALU.subtract).then_inc(sem("p2_lo"), 1)

            def out_2(m):
                dve.wait_ge(sem("pv2_job"), 2 * (m + 1))
                pv = ps[:, 5 + m % 3, 0:H2 // 2 * 2 * (DH2 + 1)].rearrange("p (h i d) -> p h i d", i=2, d=DH2 + 1)
                if m >= 2:
                    dve.wait_ge(sem("x_2"), m - 1)
                link(nc.vector.tensor_copy(a2_t[:, m % 2, :, :], pv[:, :, 1, :]))
                nc.vector.tensor_tensor(a2_t[:, m % 2, :, :], a2_t[:, m % 2, :, :], pv[:, :, 0, :], ALU.add)\
                    .then_inc(sem("o2"), 1)
                dve.wait_ge(sem("o2"), m + 1)
                nc.vector.reciprocal(a2_rc[:, m % 2, :].unsqueeze(2), a2_t[:, m % 2, :, DH2:DH2 + 1]).then_inc(sem("o2_rc"), 1)

            q2T(0)
            for n in range(4 * B):
                if n % 4 == 1 and n // 4 + 1 < B:
                    q2T(n // 4 + 1)
                p2_lo(n)
                if n >= 3 and n % 2:
                    out_2((n - 3) // 2)
                if n == 2 * B + 3:
                    dve.wait_ge(sem("x_2"), B)
                    statistics(5, 0)
            out_2(2 * B - 1)
            dve.wait_ge(sem("x_2"), 2 * B)
            gu_lo(2, 0)
            layer_norm(5, halves=(1,))
            x_lo(5, 2)
            make_tri()
            w, lg, dist, fb = f_w[:, :, 0:E2], f_lg[:, :, 0:E2], f_a, f_b
            zone = f_rk
            dve.wait_ge(sem("golden_tanh"), 1)
            link(nc.vector.tensor_scalar(lg, lg, 0.5, 0.5, ALU.mult, ALU.add))
            link(nc.vector.tensor_scalar(zone, lg, GOLDEN_LOWER, None, ALU.is_ge))
            link(nc.vector.scalar_tensor_tensor(zone, lg, GOLDEN_UPPER, zone, ALU.is_le, ALU.mult))
            link(nc.vector.tensor_scalar(dist, lg, GOLDEN_CENTER, None, ALU.subtract))
            link(nc.vector.tensor_scalar(lg, dist, -1.0, None, ALU.mult))
            nc.vector.tensor_tensor(dist, dist, lg, ALU.max).then_inc(sem("golden_dist"), 1)
            dve.wait_ge(sem("golden_exp"), 2)
            link(nc.vector.tensor_tensor(w, w, zone, ALU.mult))
            link(nc.vector.tensor_reduce(f_s8[:, 0, :], w, AX.X, ALU.add))
            link(nc.vector.tensor_scalar(f_s8[:, 1, :], f_s8[:, 0, :], 1e-8, None, ALU.is_lt))
            link(nc.vector.tensor_scalar(f_s8[:, 2, :], f_s8[:, 0, :], 1e-8, None, ALU.is_ge))
            before(fb)
            link(nc.vector.tensor_reduce(zone, f_cmp, AX.X, ALU.add))
            link(nc.vector.scalar_tensor_tensor(fb, zone, 1.5, fb, ALU.is_lt, ALU.mult))
            link(nc.vector.tensor_reduce(f_s8[:, 3, :], fb, AX.X, ALU.add))
            link(nc.vector.tensor_scalar(f_s8[:, 3, :], f_s8[:, 3, :], 1e-8, None, ALU.max))
            link(nc.vector.reciprocal(f_s8[:, 4, :], f_s8[:, 3, :]))
            link(nc.vector.tensor_tensor(f_s8[:, 4, :], f_s8[:, 4, :], f_s8[:, 1, :], ALU.mult))
            nc.vector.tensor_tensor(fb, fb, spread(f_s8[:, 4, :], E2), ALU.mult)
            link(nc.vector.tensor_tensor(w, w, spread(f_s8[:, 2, :], E2), ALU.mult))
            link(nc.vector.tensor_tensor(w, w, fb, ALU.add))
            link(nc.vector.tensor_reduce(f_s8[:, 0, :], w, AX.X, ALU.add))
            link(nc.vector.tensor_scalar(f_s8[:, 0, :], f_s8[:, 0, :], 1e-8, None, ALU.max))
            link(nc.vector.reciprocal(f_s8[:, 1, :], f_s8[:, 0, :]))
            nc.vector.tensor_tensor(w, w, spread(f_s8[:, 1, :], E2), ALU.mult).then_inc(sem("w_ready"), 1)
            ffn(2)

            def whole(src, k, h):
                sl = slice(4 * h, 4 * h + 4)
                amax, scale, inv = (a3_s[:, k, i, sl] for i in range(3))
                link(nc.vector.tensor_reduce(amax, src[:, sl, :], AX.X, ALU.max, apply_absolute_value=True))
                link(nc.vector.tensor_scalar(scale, amax, 1.0 / 127.0, 1e-8, ALU.mult, ALU.max))
                link(nc.vector.reciprocal(inv, scale))
                for t in range(4 * h, 4 * h + 4):
                    ins = nc.vector.tensor_scalar(a3_y[:, t, :], src[:, t, :], inv[:, t - 4 * h:t - 4 * h + 1], ROUND,
                                                  ALU.mult, ALU.add)
                link(ins)
                nc.vector.tensor_scalar(a3_y[:, sl, :], a3_y[:, sl, :], ROUND + 127.0, ROUND - 127.0, ALU.min, ALU.max)\
                    .then_inc(sem("clipped"), 1)

            def whole_out(k, h):
                dve.wait_ge(sem("whole_mm"), 2 * k + h + 1)
                for t in range(4 * h, 4 * h + 4):
                    ins = nc.vector.scalar_tensor_tensor(a3_y[:, t, :], ps[:, t // 2, (t % 2) * D:(t % 2 + 1) * D],
                                                         a3_s[:, k, 1, t:t + 1], wscale[:, k, :], ALU.mult, ALU.mult)
                link(ins)

            layer_norm(6, add_ffn(2))
            for h in range(2):
                whole(xn[:, :, :], 0, h)
            for h in range(2):
                sl = slice(4 * h, 4 * h + 4)
                whole_out(0, h)
                nc.vector.tensor_tensor(a3_y[:, sl, :], a3_y[:, sl, :],
                                        bq3[:, :].unsqueeze(1).to_broadcast((P, 4, D)), ALU.add).then_inc(sem("q3"), 1)

            def p3_lo(n):
                g = n % 4
                dve.wait_ge(sem("p3T_hi"), n + 1)
                hi, lo = (a3_pT[:, i, 4 * g:4 * g + 4, :].rearrange("p h s -> p (h s)") for i in range(2))
                nc.vector.tensor_tensor(lo, bank(5 - g % 2), hi, ALU.subtract).then_inc(sem("p3T_lo"), 1)

            def out_3(b, i):
                dve.wait_ge(sem("pv3"), 4 * b + 2 * (i + 1))
                if b:
                    dve.wait_ge(sem("a3_o"), 2 * b - 1 + i)
                pv = ps[:, 7 - i, 0:8 * 2 * (DH3 + 1)].rearrange("p (h i d) -> p h i d", i=2, d=DH3 + 1)
                link(nc.vector.tensor_copy(a3_t[:, i, :, :], pv[:, :, 1, :]))
                nc.vector.tensor_tensor(a3_t[:, i, :, :], a3_t[:, i, :, :], pv[:, :, 0, :], ALU.add).then_inc(sem("o3"), 1)
                dve.wait_ge(sem("o3"), 2 * b + i + 1)
                nc.vector.reciprocal(a3_rc[:, i, :].unsqueeze(2), a3_t[:, i, :, DH3:DH3 + 1]).then_inc(sem("o3_rc"), 1)

            def largest(b, h):
                sl = slice(8 * h, 8 * h + 8)
                scores = ps[:, 2 * h:2 * h + 2, :].rearrange("p i (g s) -> p (i g) s", s=S)
                dve.wait_ge(sem("s3_mm"), 2 * b + h + 1)
                link(nc.vector.tensor_reduce(a3_mx[:, sl], scores, AX.X, ALU.max))

            def less_largest(b, h):
                sl = slice(8 * h, 8 * h + 8)
                scores = ps[:, 2 * h:2 * h + 2, :].rearrange("p i (g s) -> p (i g) s", s=S)
                if b >= 2 and h == 0:
                    dve.wait_ge(sem("p3_turn"), 4 * (b - 1))
                nc.vector.tensor_tensor(a3_p[:, b % 2, sl, :], scores, a3_mx[:, sl].unsqueeze(2).to_broadcast((P, 8, S)),
                                        ALU.subtract).then_inc(sem("p3_arg"), 1)

            for h in range(2):
                largest(0, h)
            for h in range(2):
                less_largest(0, h)
            for b in range(B):
                more = b + 1 < B
                for g, step in enumerate((largest, largest, less_largest, less_largest)):
                    if more:
                        step(b + 1, g % 2)
                    if g == 1 and b:
                        out_3(b - 1, 1)
                    p3_lo(4 * b + g)
                out_3(b, 0)
                if b == B // 2 + 1:
                    dve.wait_ge(sem("a3_o"), B)
                    whole(a3_o, 1, 0)
            out_3(B - 1, 1)
            dve.wait_ge(sem("a3_o"), 2 * B)
            dve.wait_ge(sem("x_bias"), 1)
            whole(a3_o, 1, 1)

            def add_a3(h):
                sl = slice(4 * h, 4 * h + 4)
                whole_out(1, h)
                return nc.vector.scalar_tensor_tensor(x[:, sl, :], a3_y[:, sl, :], tg[:, 3:4], x[:, sl, :], ALU.mult, ALU.add)

            layer_norm(7, add_a3)
            x_lo(7, 3)
            make_tri()
            softmax(3)
            before(f_w[:, :, 0:E3])
            link(nc.vector.tensor_tensor(f_eq, f_cmp, f_w[:, :, 0:E3].unsqueeze(2).to_broadcast((P, B, E3, E3)), ALU.mult))
            link(nc.vector.tensor_reduce(f_rk, f_eq, AX.X, ALU.add))
            nc.vector.scalar_tensor_tensor(f_w[:, :, 0:E3], f_rk, TOP_P, f_w[:, :, 0:E3], ALU.is_le, ALU.mult)\
                .then_inc(sem("w_ready"), 1)
            ffn(3)
            for h in range(2):
                add_ffn(3)(h).then_inc(sem("x_done"), 1)


PIECES = []
for _i in range(NT0):
    _cuts = [e * F0 for e in range(E0 + 1) if _i * P < e * F0 < (_i + 1) * P] or [_i * P + P // 2]
    PIECES.append([(lo - _i * P, hi - _i * P, min(lo // F0, E0))
                   for lo, hi in ((_i * P, _cuts[0]), (_cuts[0], (_i + 1) * P))])


def pack_tiles(gate, up, down):
    f, d = gate.shape
    n = -(-f // P)

    def pad(m):
        return np.concatenate([m, np.zeros((n * P - f, d), m.dtype)])

    first = [pad(m).reshape(n, P, KD, P).transpose(0, 3, 2, 1).reshape(n, P, D) for m in (gate, up)]
    return np.ascontiguousarray(np.concatenate(first + [pad(down).reshape(n, P, D)], axis=2))


def feature_rows(m):
    return np.ascontiguousarray(m.reshape(KD, P, -1).transpose(1, 0, 2))


def by_feature(m):
    return m.transpose(0, 2, 1).reshape(-1, D)


def lay_out(inputs):
    i = {k: np.asarray(v) for k, v in inputs.items()}
    g = {"x": i["x"], "ctx": i["ctx_2048"], "mask": i["mask_BxS2_bk0"]}
    g["time_decay"] = np.ascontiguousarray(i["L0_xattn_time_decay"].reshape(KD, P).T)
    g["time_first"] = np.ascontiguousarray(i["L0_xattn_time_first"].reshape(KD, P).T)
    g["norm_w"] = np.ascontiguousarray(i["L1_ffn_norm_w"].reshape(KD, P).T)
    g["gates"] = np.concatenate([i["g_xattn"], i["g_ffn"]])
    g["temperature"] = i["L2_ffn_temperature"]
    g["wr"] = feature_rows(np.concatenate([i["L0_ffn_Wr"].T, i["L1_ffn_gate_w"].T, i["L2_ffn_Wr"],
                                           i["L3_ffn_router_w"].T], axis=1))
    g["w0"] = pack_tiles(np.concatenate([i["L0_ffn_Wg"].reshape(-1, D), i["L0_ffn_Wsg"]]),
                         np.concatenate([i["L0_ffn_Wu"].reshape(-1, D), i["L0_ffn_Wsu"]]),
                         np.concatenate([by_feature(i["L0_ffn_Wd"]), i["L0_ffn_Wsd"].T]))
    w13 = i["L1_ffn_w13"]
    g["w1"] = pack_tiles(np.concatenate([by_feature(w13[:, :, :F1]), i["L1_ffn_shared_gate_w"].T]),
                         np.concatenate([by_feature(w13[:, :, F1:]), i["L1_ffn_shared_up_w"].T]),
                         np.concatenate([i["L1_ffn_w2"].reshape(-1, D), i["L1_ffn_shared_down_w"]]))
    g["w2"] = pack_tiles(by_feature(i["L2_ffn_Wg"]), by_feature(i["L2_ffn_Wu"]), i["L2_ffn_Wd"].reshape(-1, D))
    g["w3"] = pack_tiles(i["L3_ffn_gate_w"].reshape(-1, D), i["L3_ffn_up_w"].reshape(-1, D), by_feature(i["L3_ffn_down_w"]))
    g["lora"] = np.ascontiguousarray(np.stack(
        [i["L2_ffn_Ga"].transpose(0, 2, 1), i["L2_ffn_Gb"], i["L2_ffn_Ua"].transpose(0, 2, 1), i["L2_ffn_Ub"],
         i["L2_ffn_Da"].transpose(0, 2, 1), i["L2_ffn_Db"]]).transpose(2, 1, 0, 3))
    g["wq2"] = feature_rows(i["L2_xattn_Wq"].T)
    both = np.concatenate([i["L2_xattn_Wk"], i["L2_xattn_Wv"]])
    g["wkv2"] = feature_rows(np.concatenate([both[0::2], both[1::2]]).T)
    g["wkv3"] = feature_rows(i["L3_xattn_wkv"].T)
    g["bkv3"] = i["L3_xattn_bkv"].reshape(1, -1)
    g["bq3"] = i["L3_xattn_bq"]
    g["bp3"] = i["L3_xattn_bp"]
    g["wqp3"] = np.ascontiguousarray(np.stack([i["L3_xattn_wq"], i["L3_xattn_wp"]]).reshape(2, KD, P, D).transpose(2, 0, 1, 3))
    return g


def kernel(**inputs):
    import concourse.bacc as _bacc
    from concourse.bass_utils import run_bass_kernel_spmd as _run

    nc = _bacc.Bacc("TRN2", target_bir_lowering=False, num_devices=1)
    arrays, aps = {}, {}
    for name, v in lay_out(inputs).items():
        arrays[f"in_{name}"] = v
        dt = U8 if v.dtype == np.bool_ else mybir.dt.from_np(v.dtype)
        aps[name] = nc.dram_tensor(f"in_{name}", v.shape, dt, kind="ExternalInput").ap()
    result = nc.dram_tensor("out_x", (B, S, D), F32, kind="ExternalOutput").ap()
    build(nc, aps, result)
    r = _run(nc, [arrays], core_ids=[0])
    return r.results[0]["out_x"]
```
